# Optimizing a Trainium2 kernel written in Bass

```python
import numpy as np
import jax
import jax.numpy as jnp

def _softmax(x, axis=-1):
    return jax.nn.softmax(x, axis=axis)

def _gelu(x):
    return jax.nn.gelu(x, approximate=True)

def _silu(x):
    return jax.nn.silu(x)

def _sigmoid(x):
    return jax.nn.sigmoid(x)

def _layernorm(x, axis=-1, eps=1e-05):
    m = jnp.mean(x, axis=axis, keepdims=True)
    v = jnp.var(x, axis=axis, keepdims=True)
    return (x - m) / jnp.sqrt(v + eps)

def _scatter_add(tgt, idx, src, axis=0):
    return tgt.at[idx].add(src)

def _segment_sum(src, seg, n):
    return jax.ops.segment_sum(src, seg, n)
kernel_name = 'mk_adaln_d2_jaxref_r4_ac9ce2'

def setup_inputs(seed: int=0):
    np.random.seed(seed)
    _w = jnp.asarray

    def _L0_attn_setup():
        import jax, jax.numpy as jnp
        import numpy as np
        HIDDEN, KEY_DIM, VALUE_DIM = (256, 256, 256)
        BATCH, SEQ = (8, 512)
        key = jax.random.key(seed)
        ks = jax.random.split(key, 9)
        s = lambda fan_in: 1.0 / np.sqrt(fan_in)
        return {'y_all': jax.random.normal(ks[0], (BATCH, SEQ, HIDDEN), dtype=jnp.float32), 'Wq': jax.random.uniform(ks[1], (HIDDEN, KEY_DIM), jnp.float32, -s(HIDDEN), s(HIDDEN)), 'bq': jax.random.uniform(ks[2], (KEY_DIM,), jnp.float32, -s(HIDDEN), s(HIDDEN)), 'Wk': jax.random.uniform(ks[3], (HIDDEN, KEY_DIM), jnp.float32, -s(HIDDEN), s(HIDDEN)), 'bk': jax.random.uniform(ks[4], (KEY_DIM,), jnp.float32, -s(HIDDEN), s(HIDDEN)), 'Wv': jax.random.uniform(ks[5], (HIDDEN, VALUE_DIM), jnp.float32, -s(HIDDEN), s(HIDDEN)), 'bv': jax.random.uniform(ks[6], (VALUE_DIM,), jnp.float32, -s(HIDDEN), s(HIDDEN)), 'Wo': jax.random.uniform(ks[7], (VALUE_DIM, HIDDEN), jnp.float32, -s(VALUE_DIM), s(VALUE_DIM)), 'bo': jax.random.uniform(ks[8], (HIDDEN,), jnp.float32, -s(VALUE_DIM), s(VALUE_DIM))}
    _L0_attn_in = _L0_attn_setup()

    def _L0_ffn_setup():
        import jax, jax.numpy as jnp
        import numpy as np
        TOP_K = 2
        ROUTE_SCALE = 1.0
        EPS = 1e-20
        B, S, D = (2, 128, 256)
        E = 8
        F = 192
        FS = 192 * 1
        key = jax.random.key(seed)
        ks = jax.random.split(key, 9)
        s = 0.02
        return {'hidden_states': jax.random.normal(ks[0], (B, S, D), dtype=jnp.float32), 'W_gate_router': jax.random.normal(ks[1], (D, E), dtype=jnp.float32) * s, 'expert_bias': jnp.zeros((E,), dtype=jnp.float32), 'Wg': jax.random.normal(ks[2], (E, D, F), dtype=jnp.float32) * s, 'Wu': jax.random.normal(ks[3], (E, D, F), dtype=jnp.float32) * s, 'Wd': jax.random.normal(ks[4], (E, F, D), dtype=jnp.float32) * s, 'Wg_s': jax.random.normal(ks[5], (D, FS), dtype=jnp.float32) * s, 'Wu_s': jax.random.normal(ks[6], (D, FS), dtype=jnp.float32) * s, 'Wd_s': jax.random.normal(ks[7], (FS, D), dtype=jnp.float32) * s}
    _L0_ffn_in = _L0_ffn_setup()
    _L0_c = _w((lambda *s: np.random.randn(*s).astype(np.float32) * 0.05)(2, 256))
    _L0_wmod = _w((lambda *s: np.random.randn(*s).astype(np.float32) * 0.05)(256, 6 * 256) * 256 ** (-0.5))

    def _L1_attn_setup():
        import jax, jax.numpy as jnp
        import numpy as np
        B, T, C, H = (8, 512, 256, 16)
        S = C // H
        LN_EPS = 1e-05
        key = jax.random.key(seed)
        ks = jax.random.split(key, 12)
        w = lambda k: jax.random.normal(k, (C, C), dtype=jnp.float32) * 0.02
        return {'x': jax.random.normal(ks[0], (B, T, C), dtype=jnp.float32), 'time_mix_k': jax.random.uniform(ks[1], (1, 1, C), dtype=jnp.float32), 'time_mix_v': jax.random.uniform(ks[2], (1, 1, C), dtype=jnp.float32), 'time_mix_r': jax.random.uniform(ks[3], (1, 1, C), dtype=jnp.float32), 'time_decay': -jax.random.uniform(ks[4], (H, S), minval=0.1, maxval=5.0, dtype=jnp.float32), 'time_first': jax.random.uniform(ks[5], (H, S), dtype=jnp.float32), 'Wk': w(ks[6]), 'Wv': w(ks[7]), 'Wr': w(ks[8]), 'Wo': w(ks[9]), 'ln_g': jnp.ones((C,), jnp.float32), 'ln_b': jnp.zeros((C,), jnp.float32)}
    _L1_attn_in = _L1_attn_setup()

    def _L1_ffn_setup():
        import jax, jax.numpy as jnp
        import numpy as np
        DIM = 256

        def _reference_tuple_inner(x, W_r, W_k, W_v, mu_r, mu_k):
            B, T, C = x.shape
            x_prev = jnp.concatenate([jnp.zeros((B, 1, C), x.dtype), x[:, :-1, :]], axis=1)
            xr = mu_r * x + (1.0 - mu_r) * x_prev
            xk = mu_k * x + (1.0 - mu_k) * x_prev
            r = jax.nn.sigmoid(jnp.einsum('btc,dc->btd', xr, W_r))
            k = jnp.einsum('btc,dc->btd', xk, W_k)
            k_act = jnp.square(jax.nn.relu(k))
            out = r * jnp.einsum('btc,dc->btd', k_act, W_v)
            new_state = x[:, -1, :]
            return (out, new_state)
        key = jax.random.key(seed)
        ks = jax.random.split(key, 6)
        B, T, C = (8, 512, DIM)
        x = jax.random.normal(ks[0], (B, T, C), dtype=jnp.float32)
        s = 1.0 / np.sqrt(C)
        W_r = jax.random.uniform(ks[1], (C, C), jnp.float32, -s, s)
        W_k = jax.random.uniform(ks[2], (C, C), jnp.float32, -s, s)
        W_v = jax.random.uniform(ks[3], (C, C), jnp.float32, -s, s)
        mu_r = jax.random.uniform(ks[4], (C,), jnp.float32)
        mu_k = jax.random.uniform(ks[5], (C,), jnp.float32)
        return {'x': x, 'W_r': W_r, 'W_k': W_k, 'W_v': W_v, 'mu_r': mu_r, 'mu_k': mu_k}
    _L1_ffn_in = _L1_ffn_setup()
    _L1_c = _w((lambda *s: np.random.randn(*s).astype(np.float32) * 0.05)(2, 256))
    _L1_wmod = _w((lambda *s: np.random.randn(*s).astype(np.float32) * 0.05)(256, 6 * 256) * 256 ** (-0.5))
    _d = {'L0_attn_y_all': _L0_attn_in['y_all'], 'L0_attn_Wq': _L0_attn_in['Wq'], 'L0_attn_bq': _L0_attn_in['bq'], 'L0_attn_Wk': _L0_attn_in['Wk'], 'L0_attn_bk': _L0_attn_in['bk'], 'L0_attn_Wv': _L0_attn_in['Wv'], 'L0_attn_bv': _L0_attn_in['bv'], 'L0_attn_Wo': _L0_attn_in['Wo'], 'L0_attn_bo': _L0_attn_in['bo'], 'L0_ffn_W_gate_router': _L0_ffn_in['W_gate_router'], 'L0_ffn_expert_bias': _L0_ffn_in['expert_bias'], 'L0_ffn_Wg': _L0_ffn_in['Wg'], 'L0_ffn_Wu': _L0_ffn_in['Wu'], 'L0_ffn_Wd': _L0_ffn_in['Wd'], 'L0_ffn_Wg_s': _L0_ffn_in['Wg_s'], 'L0_ffn_Wu_s': _L0_ffn_in['Wu_s'], 'L0_ffn_Wd_s': _L0_ffn_in['Wd_s'], 'L0_c': _L0_c, 'L0_wmod': _L0_wmod, 'L1_attn_time_mix_k': _L1_attn_in['time_mix_k'], 'L1_attn_time_mix_v': _L1_attn_in['time_mix_v'], 'L1_attn_time_mix_r': _L1_attn_in['time_mix_r'], 'L1_attn_time_decay': _L1_attn_in['time_decay'], 'L1_attn_time_first': _L1_attn_in['time_first'], 'L1_attn_Wk': _L1_attn_in['Wk'], 'L1_attn_Wv': _L1_attn_in['Wv'], 'L1_attn_Wr': _L1_attn_in['Wr'], 'L1_attn_Wo': _L1_attn_in['Wo'], 'L1_attn_ln_g': _L1_attn_in['ln_g'], 'L1_attn_ln_b': _L1_attn_in['ln_b'], 'L1_ffn_W_r': _L1_ffn_in['W_r'], 'L1_ffn_W_k': _L1_ffn_in['W_k'], 'L1_ffn_W_v': _L1_ffn_in['W_v'], 'L1_ffn_mu_r': _L1_ffn_in['mu_r'], 'L1_ffn_mu_k': _L1_ffn_in['mu_k'], 'L1_c': _L1_c, 'L1_wmod': _L1_wmod}
    _x0 = _d['L0_attn_y_all']
    _d['L0_attn_y_all'] = jax.random.normal(jax.random.fold_in(jax.random.key(seed), 1), (2, 2048, 256), dtype=_x0.dtype)
    del _x0
    return _d

def reference(L0_attn_y_all, L0_attn_Wq, L0_attn_bq, L0_attn_Wk, L0_attn_bk, L0_attn_Wv, L0_attn_bv, L0_attn_Wo, L0_attn_bo, L0_ffn_W_gate_router, L0_ffn_expert_bias, L0_ffn_Wg, L0_ffn_Wu, L0_ffn_Wd, L0_ffn_Wg_s, L0_ffn_Wu_s, L0_ffn_Wd_s, L0_c, L0_wmod, L1_attn_time_mix_k, L1_attn_time_mix_v, L1_attn_time_mix_r, L1_attn_time_decay, L1_attn_time_first, L1_attn_Wk, L1_attn_Wv, L1_attn_Wr, L1_attn_Wo, L1_attn_ln_g, L1_attn_ln_b, L1_ffn_W_r, L1_ffn_W_k, L1_ffn_W_v, L1_ffn_mu_r, L1_ffn_mu_k, L1_c, L1_wmod):

    def _L0_attn_ref(y_all, Wq, bq, Wk, bk, Wv, bv, Wo, bo):
        import jax, jax.numpy as jnp
        import numpy as np
        HIDDEN, KEY_DIM, VALUE_DIM = (256, 256, 256)
        BATCH, SEQ = (8, 512)
        B, T, H = y_all.shape
        dk = Wq.shape[1]
        q = (y_all @ Wq + bq) / jnp.sqrt(jnp.asarray(dk, y_all.dtype))
        k = y_all @ Wk + bk
        v = y_all @ Wv + bv
        scores = jnp.einsum('bid,bjd->bij', q, k)
        causal = jnp.tril(jnp.ones((T, T), dtype=bool))
        scores = jnp.where(causal, scores, -jnp.inf)
        weights = jax.nn.softmax(scores, axis=-1)
        ctx = jnp.einsum('bij,bjd->bid', weights, v)
        return ctx @ Wo + bo

    def _L0_ffn_ref(hidden_states, W_gate_router, expert_bias, Wg, Wu, Wd, Wg_s, Wu_s, Wd_s):
        import jax, jax.numpy as jnp
        import numpy as np
        TOP_K = 2
        ROUTE_SCALE = 1.0
        EPS = 1e-20
        B, S, D = (2, 128, 256)
        E = 8
        F = 192
        FS = 192 * 1
        b, s, d = hidden_states.shape
        x = hidden_states.reshape(-1, d)
        T = x.shape[0]
        logits = x @ W_gate_router
        scores = jax.nn.sigmoid(logits.astype(jnp.float32))
        _, sel = jax.lax.top_k(scores + expert_bias, TOP_K)
        top_scores = jnp.take_along_axis(scores, sel, axis=1)
        top_scores = top_scores / (top_scores.sum(-1, keepdims=True) + EPS)
        top_scores = top_scores * ROUTE_SCALE
        shared = jax.nn.silu(x @ Wg_s) * (x @ Wu_s) @ Wd_s
        tok = jnp.repeat(jnp.arange(T), TOP_K)
        exp = sel.reshape(-1)
        w = top_scores.reshape(-1)
        xr = x[tok]
        h = jax.nn.silu(jnp.einsum('nd,edf->enf', xr, Wg)) * jnp.einsum('nd,edf->enf', xr, Wu)
        out_all = jnp.einsum('enf,efd->end', h, Wd)
        routed = out_all[exp, jnp.arange(exp.shape[0])]
        routed = (routed.astype(jnp.float32) * w[:, None]).astype(hidden_states.dtype)
        out = shared.at[tok].add(routed)
        return out.reshape(b, s, d)

    def _L1_attn_ref(x, time_mix_k, time_mix_v, time_mix_r, time_decay, time_first, Wk, Wv, Wr, Wo, ln_g, ln_b):
        import jax, jax.numpy as jnp
        import numpy as np
        B, T, C, H = (8, 512, 256, 16)
        S = C // H
        LN_EPS = 1e-05
        Bx, Tx, Cx = x.shape
        xx = jnp.pad(x, ((0, 0), (1, 0), (0, 0)))[:, :-1]
        xk = x * time_mix_k + xx * (1 - time_mix_k)
        xv = x * time_mix_v + xx * (1 - time_mix_v)
        xr = x * time_mix_r + xx * (1 - time_mix_r)
        proj = lambda z, W: jnp.einsum('btc,dc->btd', z, W).reshape(Bx, Tx, H, S)
        k = proj(xk, Wk)
        v = proj(xv, Wv)
        r = proj(xr, Wr)
        kv = k * v
        decay = jnp.exp(time_decay)

        def step(state, inp):
            kv_t, r_t = inp
            state = kv_t + decay * state
            o = r_t * (time_first * kv_t + state)
            return (state, o)
        kvT = jnp.swapaxes(kv, 0, 1)
        rT = jnp.swapaxes(r, 0, 1)
        _, outT = jax.lax.scan(step, jnp.zeros((Bx, H, S), x.dtype), (kvT, rT))
        out = jnp.swapaxes(outT, 0, 1).reshape(Bx, Tx, Cx)
        mu = out.mean(-1, keepdims=True)
        var = out.var(-1, keepdims=True)
        out = (out - mu) / jnp.sqrt(var + LN_EPS) * ln_g + ln_b
        return jnp.einsum('btc,dc->btd', out, Wo)

    def _L1_ffn_ref(x, W_r, W_k, W_v, mu_r, mu_k):
        import jax, jax.numpy as jnp
        import numpy as np
        DIM = 256

        def _reference_tuple_inner(x, W_r, W_k, W_v, mu_r, mu_k):
            B, T, C = x.shape
            x_prev = jnp.concatenate([jnp.zeros((B, 1, C), x.dtype), x[:, :-1, :]], axis=1)
            xr = mu_r * x + (1.0 - mu_r) * x_prev
            xk = mu_k * x + (1.0 - mu_k) * x_prev
            r = jax.nn.sigmoid(jnp.einsum('btc,dc->btd', xr, W_r))
            k = jnp.einsum('btc,dc->btd', xk, W_k)
            k_act = jnp.square(jax.nn.relu(k))
            out = r * jnp.einsum('btc,dc->btd', k_act, W_v)
            new_state = x[:, -1, :]
            return (out, new_state)
        return _reference_tuple_inner(x, W_r, W_k, W_v, mu_r, mu_k)[0]
    x = L0_attn_y_all
    mod = (_silu(L0_c) @ L0_wmod).reshape(L0_c.shape[0], 6, 1, -1)
    sa, ca, ga, sb, cb, gb = (mod[:, 0], mod[:, 1], mod[:, 2], mod[:, 3], mod[:, 4], mod[:, 5])
    ga = (2 * (ga >= 0) - 1) * jnp.maximum(jnp.abs(ga), 0.25)
    gb = (2 * (gb >= 0) - 1) * jnp.maximum(jnp.abs(gb), 0.25)
    h = _layernorm(x, axis=-1) * (1 + ca) + sa
    x = x + ga * _L0_attn_ref(h, L0_attn_Wq, L0_attn_bq, L0_attn_Wk, L0_attn_bk, L0_attn_Wv, L0_attn_bv, L0_attn_Wo, L0_attn_bo)
    h = _layernorm(x, axis=-1) * (1 + cb) + sb
    x = x + gb * _L0_ffn_ref(h, L0_ffn_W_gate_router, L0_ffn_expert_bias, L0_ffn_Wg, L0_ffn_Wu, L0_ffn_Wd, L0_ffn_Wg_s, L0_ffn_Wu_s, L0_ffn_Wd_s)
    mod = (_silu(L1_c) @ L1_wmod).reshape(L1_c.shape[0], 6, 1, -1)
    sa, ca, ga, sb, cb, gb = (mod[:, 0], mod[:, 1], mod[:, 2], mod[:, 3], mod[:, 4], mod[:, 5])
    ga = (2 * (ga >= 0) - 1) * jnp.maximum(jnp.abs(ga), 0.25)
    gb = (2 * (gb >= 0) - 1) * jnp.maximum(jnp.abs(gb), 0.25)
    h = _layernorm(x, axis=-1) * (1 + ca) + sa
    x = x + ga * _L1_attn_ref(h, L1_attn_time_mix_k, L1_attn_time_mix_v, L1_attn_time_mix_r, L1_attn_time_decay, L1_attn_time_first, L1_attn_Wk, L1_attn_Wv, L1_attn_Wr, L1_attn_Wo, L1_attn_ln_g, L1_attn_ln_b)
    h = _layernorm(x, axis=-1) * (1 + cb) + sb
    x = x + gb * _L1_ffn_ref(h, L1_ffn_W_r, L1_ffn_W_k, L1_ffn_W_v, L1_ffn_mu_r, L1_ffn_mu_k)
    return x

_drawn_inputs = setup_inputs


def setup_inputs(seed=0):
    import zlib

    import numpy as np

    out = dict(_drawn_inputs(seed))
    spreads = {'L0_ffn_expert_bias': (0.0, 0.8), 'L1_attn_ln_g': (1.0, 0.6), 'L1_attn_ln_b': (0.0, 2.0)}
    factors = {'L0_attn_Wq': 8.0,
     'L0_attn_bq': 8.0,
     'L0_attn_Wk': 8.0,
     'L0_attn_bk': 200.0,
     'L0_attn_Wv': 8.0,
     'L0_attn_bv': 8.0,
     'L0_attn_Wo': 6.869,
     'L0_attn_bo': 6.345,
     'L0_ffn_W_gate_router': 8.0,
     'L0_ffn_Wg': 8.0,
     'L0_ffn_Wu': 8.0,
     'L0_ffn_Wd': 8.0,
     'L0_ffn_Wg_s': 8.0,
     'L0_ffn_Wu_s': 8.0,
     'L0_ffn_Wd_s': 8.0,
     'L0_c': 4.201,
     'L0_wmod': 4.528,
     'L1_attn_time_decay': 180.992,
     'L1_attn_time_first': 12.949,
     'L1_ffn_W_r': 8.0,
     'L1_ffn_W_k': 3.02,
     'L1_ffn_W_v': 2.773,
     'L1_ffn_mu_r': 8.0,
     'L1_ffn_mu_k': 5.015}
    for name, (base, spread) in spreads.items():
        noise = np.random.default_rng([zlib.crc32(name.encode()), seed]).standard_normal(out[name].shape)
        drawn = base * np.exp(spread * noise) if base else spread * noise
        out[name] = jnp.asarray(drawn.astype(out[name].dtype))
    for name, factor in factors.items():
        out[name] = (out[name] * factor).astype(out[name].dtype)
    return out
```

```python
from contextlib import ExitStack

import numpy as np

import concourse.bass as bass
from concourse import mybir



class Kept:
    pass


ALU = mybir.AluOpType
ACT = mybir.ActivationFunctionType
AX = mybir.AxisListType
F32 = mybir.dt.float32
F32R = mybir.dt.float32r
U32 = mybir.dt.uint32

P = 128
B, T, D = 2, 2048, 256
KC = D // P
TILES = B * T // P
TPB = T // P
GT = 4
GROUPS = TILES // GT
GPB = GROUPS // B
GW = GT * P
EPS = 1e-5
E = 8
F = 192
NEG = -1e30

COLS = ["bq", "bk", "mix_k", "mix_v", "mix_r", "decay", "first", "ln_g", "ln_b", "mu_r", "mu_k",
        "c00", "c01", "c10", "c11"]
COL = {n: i for i, n in enumerate(COLS)}
C0 = COL["c00"]
SHIFT_A, SCALE_A, GATE_A, SHIFT_B, SCALE_B, GATE_B = range(6)
COLKINDS = [SHIFT_A, SCALE_A, SHIFT_B, SCALE_B]


START = 1


def begin(eng, *sems):
    for sem in sems:
        eng.sem_inc(sem, START)


class Counted:

    def __init__(self, eng, sem, base=0):
        self.eng, self.sem, self.base, self.n = eng, sem, base, 0

    def link(self, ins, k=None):
        ins.then_inc(self.sem, 1)
        self.n += 1
        self.eng.wait_ge(self.sem, START + self.base + self.n)
        if k:
            apart(k, self.eng)


def three(eng, out, lh, ll, rh, rl, first, last):
    eng.matmul(out, lh, rh, start=first, stop=False)
    eng.matmul(out, lh, rl, start=False, stop=False)
    return eng.matmul(out, ll, rh, start=False, stop=last)


def apart(k, eng):
    eng.sem_inc(k.passed[eng.engine], 1)


def col(k, name, c):
    return k.cols[:, c, COL[name]:COL[name] + 1]


def setup(nc, k, d):
    with ExitStack() as ctx:
        sb = lambda n, s, t=F32: ctx.enter_context(nc.sbuf_tensor(n, s, t))
        sem = lambda n: ctx.enter_context(nc.semaphore(n))
        wmod = sb("wmod", [P, 2, KC, 6 * D])
        silu_c = sb("silu_c", [P, KC, 4])
        silu_t = sb("silu_t", [P, KC, 4])
        silu_bc = sb("silu_bc", [P, KC, 4, P])
        graw = sb("graw", [P, 8, D])
        gabs = sb("gabs", [P, 8, D])
        colp = ctx.enter_context(nc.psum_tensor("colp", [P, 2, 4, KC, 2], F32))
        rowp = ctx.enter_context(nc.psum_tensor("rowp", [P, 8, D], F32))
        small_in, wmod_in, silu_e, dve, bc_ready, cols_done, rows_done, id0 = (
            sem(n) for n in ("small_in", "wmod_in", "silu_e", "s0_dve", "bc_ready",
                             "cols_done", "rows_done", "id0"))
        k.x_in = [k.sem(f"x_in{b}") for b in range(B)]
        block = ctx.enter_context(nc.Block())

        @block.sync
        def _(sp):
            sp.dma_start(k.cols[:], d["cols"]).then_inc(small_in, 16)
            for l in range(2):
                sp.dma_start(wmod[:, l], d["wmod"][l].rearrange("(c p) n -> p c n", p=P)).then_inc(wmod_in, 16)
            sp.dma_start(k.rows[:], d["rows"].to_broadcast([P, 2 * D + E])).then_inc(small_in, 16)
            for g in range(GROUPS):
                sp.dma_start(k.x[:, g * GT:(g + 1) * GT, :],
                             d["x"][g * GW:(g + 1) * GW, :].rearrange("(t p) d -> p t d", p=P)).then_inc(k.x_in[g // GPB], 16)

        @block.gpsimd
        def _(pool):
            nc.gpsimd.memset(k.ident[:], 0.0).then_inc(id0, 1)
            nc.gpsimd.memset(k.causal[:], 0.0).then_inc(id0, 1)
            nc.gpsimd.memset(k.mhalf[:], -0.5)
            pool.wait_ge(id0, 2)
            nc.gpsimd.affine_select(out=k.ident[:], in_=k.ident[:], compare_op=ALU.not_equal, fill=1.0,
                                    base=0, pattern=[[-1, P]], channel_multiplier=1)
            nc.gpsimd.affine_select(out=k.causal[:], in_=k.causal[:], compare_op=ALU.is_ge, fill=NEG,
                                    base=0, pattern=[[-1, P]], channel_multiplier=1).then_inc(k.consts, 1)

        @block.scalar
        def _(act):
            act.wait_ge(small_in, 32)
            nc.scalar.activation(silu_t[:], k.cols[:, :, C0:C0 + 4], ACT.Exp, scale=-1.0).then_inc(silu_e, 1)

        @block.vector
        def _(v):
            c = Counted(v, dve, -START)
            v.wait_ge(silu_e, 1)
            c.link(nc.vector.tensor_scalar_add(silu_t[:], silu_t[:], 1.0))
            c.link(nc.vector.reciprocal(silu_t[:], silu_t[:]))
            c.link(nc.vector.tensor_tensor(silu_c[:], silu_t[:], k.cols[:, :, C0:C0 + 4], ALU.mult))
            for kc in range(KC):
                for j in range(4):
                    last = nc.vector.tensor_copy(silu_bc[:, kc, j, :],
                                                 silu_c[:, kc, j:j + 1].to_broadcast([P, P]))
            last.then_inc(bc_ready, 1)
            v.wait_ge(cols_done, 1)
            for l in range(2):
                for i, kind in enumerate(COLKINDS):
                    add = 1.0 if kind in (SCALE_A, SCALE_B) else 0.0
                    nc.vector.tensor_scalar_add(k.colmod[:, l, i], colp[:, l, i], add)
            v.wait_ge(rows_done, 1)
            c.link(nc.vector.tensor_copy(graw[:], rowp[:]))
            c.link(nc.vector.tensor_scalar(gabs[:], graw[:], -1.0, None, ALU.mult))
            c.link(nc.vector.tensor_tensor(gabs[:], gabs[:], graw[:], ALU.max))
            c.link(nc.vector.tensor_scalar(graw[:], graw[:], 0.0, 2.0, ALU.is_ge, ALU.mult))
            c.link(nc.vector.tensor_scalar(graw[:], graw[:], -1.0, None, ALU.add))
            c.link(nc.vector.tensor_scalar(gabs[:], gabs[:], 0.25, None, ALU.max))
            c.link(nc.vector.tensor_tensor(k.gate[:], gabs[:], graw[:], ALU.mult))
            for b in range(B):
                nc.vector.tensor_tensor(k.bo_gate[:, b], k.gate[:, b], k.rows[:, D:2 * D], ALU.mult)

        @block.tensor
        def _(pe):
            pe.wait_ge(wmod_in, 32)
            pe.wait_ge(bc_ready, 1)
            for l in range(2):
                for i, kind in enumerate(COLKINDS):
                    for c in range(KC):
                        for kc in range(KC):
                            o = kind * D + c * P
                            last = nc.tensor.matmul(colp[:, l, i, c], wmod[:, l, kc, o:o + P],
                                                    silu_c[:, kc, 2 * l:2 * l + 2], start=(kc == 0), stop=(kc == KC - 1))
            last.then_inc(cols_done, 1)
            for l in range(2):
                for gi, kind in enumerate((GATE_A, GATE_B)):
                    for b in range(B):
                        for kc in range(KC):
                            last = nc.tensor.matmul(rowp[:, l * 4 + gi * 2 + b, :], silu_bc[:, kc, 2 * l + b, :],
                                                    wmod[:, l, kc, kind * D:(kind + 1) * D],
                                                    start=(kc == 0), stop=(kc == KC - 1))
            last.then_inc(rows_done, 1)


class Norm:

    def __init__(self, nc, k, ctx, name, layer, shift):
        self.nc, self.k, self.layer, self.shift = nc, k, layer, shift
        sb = lambda n, s, t=F32: ctx.enter_context(nc.sbuf_tensor(name + n, s, t))
        sem = lambda n: ctx.enter_context(nc.semaphore(name + n))
        self.bn = sb("bn", [P, GT, 6])
        self.mv = sb("mv", [P, GT, 2])
        self.ve = sb("ve", [P, GT])
        self.rstd = sb("rstd", [P, GT])
        self.z = sb("z", [P, GT, D])
        self.bn_done, self.stats, self.ve_done, self.rstd_done, self.z_done, self.zt_done, self.h_done = (
            sem(n) for n in ("bn_done", "stats", "ve_done", "rstd_done", "z_done", "zt_done", "h_done"))

    def tile(self, t):
        return self.k.x[:, bass.ds(t, 1), :].rearrange("p o d -> p (o d)")

    def vector_stats(self, v, step, first):
        nc = self.nc
        for j in range(GT):
            last = nc.vector.bn_stats(self.bn[:, j], self.tile(first + j))
        last.then_inc(self.bn_done, 1)
        v.wait_ge(self.bn_done, START + step + 1)
        apart(self.k, v)
        for j in range(GT):
            last = nc.vector.bn_aggr(self.mv[:, j], self.bn[:, j])
        last.then_inc(self.stats, 1)

    def vector_z(self, v, step, first):
        nc = self.nc
        v.wait_ge(self.stats, START + step + 1)
        v.wait_ge(self.rstd_done, START + step + 1)
        v.wait_ge(self.zt_done, START + step * KC)
        for j in range(GT):
            last = nc.vector.tensor_scalar(self.z[:, j], self.tile(first + j), self.mv[:, j, 0:1],
                                           self.rstd[:, j:j + 1], ALU.subtract, ALU.mult)
        last.then_inc(self.z_done, 1)

    def gpsimd(self, pool, step):
        nc = self.nc
        pool.wait_ge(self.stats, START + step + 1)
        apart(self.k, pool)
        nc.gpsimd.tensor_scalar_add(self.ve[:], self.mv[:, :, 1], EPS).then_inc(self.ve_done, 1)
        pool.wait_ge(self.ve_done, START + step + 1)
        pool.wait_ge(self.z_done, START + step)
        nc.gpsimd.tensor_tensor(self.rstd[:], self.ve[:], self.k.mhalf[:], ALU.pow).then_inc(self.rstd_done, 1)

    def tensor(self, pe, step, c, zt):
        if c == 0:
            pe.wait_ge(self.z_done, START + step + 1)
        for j in range(GT):
            last = self.nc.tensor.transpose(zt[:, j * P:(j + 1) * P], self.z[:, j, c * P:(c + 1) * P], self.k.ident[:])
        last.then_inc(self.zt_done, 1)

    def scalar(self, act, step, c, zt, h, b):
        act.wait_ge(self.zt_done, START + step * KC + c + 1)
        m = self.k.colmod
        scale = m[:, self.layer, self.shift + 1, c, bass.ds(b, 1)]
        shift = m[:, self.layer, self.shift, c, bass.ds(b, 1)]
        apart(self.k, act)
        self.nc.scalar.activation(h, zt, ACT.Identity, bias=shift, scale=scale).then_inc(self.h_done, 1)


def attention(nc, k, d):
    with ExitStack() as ctx:
        sb = lambda n, s, t=F32: ctx.enter_context(nc.sbuf_tensor(n, s, t))
        sem = lambda n: ctx.enter_context(nc.semaphore(n))
        ps = lambda n, s: ctx.enter_context(nc.psum_tensor(n, s, F32))
        WQ, WK, WV, WO = range(4)
        wh = sb("wh", [P, 4, KC, D], F32R)
        wl = sb("wl", [P, 4, KC, D], F32R)
        kh, kl = sb("kh", [P, KC, T], F32R), sb("kl", [P, KC, T], F32R)
        vh, vl = sb("vh", [P, TPB, D], F32R), sb("vl", [P, TPB, D], F32R)
        hf = sb("hf", [P, KC, GW])
        hh, hl = sb("hh", [P, KC, GW], F32R), sb("hl", [P, KC, GW], F32R)
        qh, ql = sb("qh", [P, KC, GW], F32R), sb("ql", [P, KC, GW], F32R)
        qf = sb("qf", [P, 4, GW])
        vf = sb("vf", [P, GT, D])
        bq16 = sb("bq16", [P, KC])
        prob = sb("prob", [P, 2, T])
        pth, ptl = sb("pth", [P, 2, GW], F32R), sb("ptl", [P, 2, GW], F32R)
        mx, nmx = sb("mx", [P, 2]), sb("nmx", [P, 2])
        rsum, rinv = sb("rsum", [P, 2]), sb("rinv", [P, 2])
        cn = sb("cn", [P, D])
        cth, ctl = sb("cth", [P, KC, P], F32R), sb("ctl", [P, KC, P], F32R)
        y = sb("y1", [P, 2, D])
        norm = Norm(nc, k, ctx, "n1", 0, 0)
        sc = ps("sc", [P, 4, 512])
        tp = ps("tp", [P, 2, 512])
        cx = ps("cx", [P, 512])
        pj = ps("pj", [P, 512])
        w_in = [sem(f"a_w_in{i}") for i in range(4)]
        names = ("w_hi w_lo bq_done hi_h lo_h qk_ready v_ready qkf vf_done qk_hi qk_lo v_hi v_lo "
                 "s_ready dve1 nmax_done exp_done pt_ready pt_hi pt_lo pv_done cn_done ct_ready ct_hi "
                 "ct_lo pj_ready y_done bo_done")
        s = {n: sem("a_" + n) for n in names.split()}
        NCH = [(t + GT) // GT for t in range(TPB)]
        OFF = [sum(NCH[:t]) for t in range(TPB + 1)]
        CHB = OFF[-1]
        block = ctx.enter_context(nc.Block())

        def width(t, ch):
            return min(GW, (t + 1) * P - ch * GW)

        @block.sync
        def _(sp):
            raw = prob[:].rearrange("p a (w n) -> p (a w) n", n=KC * D)
            for i, w in enumerate((d["wq"], d["wk"], d["wv"], d["wo"])):
                sp.dma_start(raw[:, i].rearrange("p (c n) -> p c n", c=KC),
                             w.rearrange("(c p) n -> p c n", p=P)).then_inc(w_in[i], 16)

        @block.gpsimd
        def _(pool):
            begin(pool, s["hi_h"], s["bo_done"], s["qk_hi"], s["v_hi"], norm.ve_done, norm.rstd_done, k.x1_done)
            def split_hi(dst, src, sem_):
                apart(k, pool)
                nc.gpsimd.tensor_copy(dst, src).then_inc(sem_, 1)

            with pool.Fori(0, B) as b:
                for g in range(GPB):
                    G = b * GPB + g
                    norm.gpsimd(pool, G)
                    for c in range(KC):
                        pool.wait_ge(norm.h_done, START + G * KC + c + 1)
                        pool.wait_ge(s["v_ready"], START + G * 2)
                        split_hi(hh[:, c], hf[:, c], s["hi_h"])
                    for j in range(GT):
                        xt = k.x[:, bass.ds(b * TPB + g * GT + j, 1), :].rearrange("p o d -> p (o d)")
                        last = nc.gpsimd.tensor_tensor(xt, xt, k.bo_gate[:, bass.ds(b, 1), :].rearrange("p o d -> p (o d)"), ALU.add)
                    last.then_inc(s["bo_done"], 1)
                    for i in range(4):
                        pool.wait_ge(s["qkf"], START + G * 4 + i + 1)
                        if i < 2:
                            pool.wait_ge(s["s_ready"], START + b * TPB + g * GT)
                            split_hi(qh[:, i], qf[:, i], s["qk_hi"])
                        else:
                            split_hi(kh[:, i - 2, g * GW:(g + 1) * GW], qf[:, i], s["qk_hi"])
                    for i in range(2):
                        pool.wait_ge(s["vf_done"], START + G * 2 + i + 1)
                        pool.wait_ge(s["pv_done"], START + b * CHB)
                        split_hi(vh[:, g * GT + 2 * i:g * GT + 2 * i + 2], vf[:, 2 * i:2 * i + 2], s["v_hi"])
                    for j in range(GT):
                        t = g * GT + j
                        pool.wait_ge(s["y_done"], START + b * TPB + t + 1)
                        xt = k.x[:, bass.ds(b * TPB + t, 1), :].rearrange("p o d -> p (o d)")
                        apart(k, pool)
                        nc.gpsimd.tensor_tensor(xt, xt, y[:, t % 2], ALU.add).then_inc(k.x1_done, 1)

        @block.scalar
        def _(act):
            begin(act, s["bq_done"], s["w_hi"], s["ct_hi"], s["exp_done"], s["qkf"], s["pt_hi"], norm.h_done)
            raw = prob[:].rearrange("p a (w n) -> p (a w) n", n=KC * D)
            nc.scalar.activation(bq16[:], k.cols[:, :, COL["bq"]], ACT.Copy, scale=1.0 / 16).then_inc(s["bq_done"], 1)
            for i in range(4):
                act.wait_ge(w_in[i], 16)
                nc.scalar.copy(wh[:, i].rearrange("p c n -> p (c n)"), raw[:, i]).then_inc(s["w_hi"], 1)
            act.wait_ge(s["bq_done"], START + 1)

            def ct_hi(Tn):
                act.wait_ge(s["ct_ready"], START + Tn)
                nc.scalar.copy(cth[:].rearrange("p c n -> p (c n)"), pj[:, 0:D]).then_inc(s["ct_hi"], 1)

            def exp_of(b, t):
                act.wait_ge(s["nmax_done"], START + b * TPB + t + 1)
                if t >= 2:
                    act.wait_ge(s["pt_ready"], START + b * CHB + OFF[t - 1])
                    act.wait_ge(s["cn_done"], START + b * TPB + t - 1)
                else:
                    act.wait_ge(s["pt_ready"], START + b * CHB)
                    act.wait_ge(s["cn_done"], START + b * TPB)
                    act.wait_ge(s["w_lo"], START + 4)
                w = (t + 1) * P
                nc.scalar.activation(prob[:, t % 2, 0:w], sc[:].rearrange("p a n -> p (a n)")[:, 0:w], ACT.Exp,
                                     bias=nmx[:, t % 2:t % 2 + 1], accum_out=rsum[:, t % 2:t % 2 + 1]).then_inc(s["exp_done"], 1)

            with act.Fori(0, B) as b:
                for g in range(GPB):
                    G = b * GPB + g
                    for c in range(KC):
                        if c == 0:
                            act.wait_ge(s["lo_h"], START + G * KC)
                        norm.scalar(act, G, c, tp[:, c], hf[:, c], b)
                    for i in range(4):
                        act.wait_ge(s["qk_ready"], START + G * 4 + i + 1)
                        act.wait_ge(s["qk_lo"], START + G * 4)
                        bias, scale = (bq16[:, i:i + 1], 1.0 / 16) if i < 2 else (col(k, "bk", i - 2), 1.0)
                        nc.scalar.activation(qf[:, i], sc[:, i], ACT.Identity, bias=bias, scale=scale).then_inc(s["qkf"], 1)
                    exp_of(b, g * GT)
                    for j in range(GT):
                        t = g * GT + j
                        Tt = b * TPB + t
                        for ch in range(NCH[t]):
                            C = b * CHB + OFF[t] + ch
                            w = width(t, ch)
                            act.wait_ge(s["pt_ready"], START + C + 1)
                            act.wait_ge(s["pv_done"], START + (C - 1 if OFF[t] + ch >= 2 else b * CHB))
                            nc.scalar.copy(pth[:, (OFF[t] + ch) % 2, 0:w], tp[:, (OFF[t] + ch) % 2, 0:w]).then_inc(s["pt_hi"], 1)
                            if ch == 0 and j > 0:
                                ct_hi(Tt)
                        if j < GT - 1:
                            exp_of(b, t + 1)
                        else:
                            ct_hi(Tt + 1)

        @block.vector
        def _(v):
            begin(v, s["w_lo"], s["dve1"], s["nmax_done"], s["ct_lo"], s["y_done"], s["lo_h"], s["qk_lo"], s["vf_done"], s["v_lo"],
                  s["pt_lo"], s["cn_done"], norm.bn_done, norm.stats, norm.z_done)
            raw = prob[:].rearrange("p a (w n) -> p (a w) n", n=KC * D)
            for i in range(4):
                v.wait_ge(s["w_hi"], START + i + 1)
                nc.vector.tensor_tensor(wl[:, i].rearrange("p c n -> p (c n)"), raw[:, i],
                                        wh[:, i].rearrange("p c n -> p (c n)"), ALU.subtract).then_inc(s["w_lo"], 1)
            DV = 3 * TPB
            for b in range(B):
                v.wait_ge(k.x_in[b], 16 * GPB)

            with v.Fori(0, B) as b:
                chain = Counted(v, s["dve1"], b * DV)

                def softmax_max(t):
                    Tt = b * TPB + t
                    v.wait_ge(s["s_ready"], START + Tt + 1)
                    diag = sc[:, t // GT, (t % GT) * P:(t % GT + 1) * P]
                    chain.link(nc.vector.tensor_tensor(diag, diag, k.causal[:], ALU.add))
                    chain.link(nc.vector.tensor_reduce(mx[:, t % 2:t % 2 + 1],
                                                       sc[:].rearrange("p a n -> p (a n)")[:, 0:(t + 1) * P], AX.X, ALU.max))
                    if t >= 2:
                        v.wait_ge(s["exp_done"], START + Tt - 1)
                    nc.vector.tensor_scalar(nmx[:, t % 2:t % 2 + 1], mx[:, t % 2:t % 2 + 1], -1.0, None,
                                            ALU.mult).then_inc(s["nmax_done"], 1)

                def ct_lo(Tn):
                    v.wait_ge(s["ct_hi"], START + Tn)
                    nc.vector.tensor_tensor(ctl[:].rearrange("p c n -> p (c n)"), pj[:, 0:D],
                                            cth[:].rearrange("p c n -> p (c n)"), ALU.subtract).then_inc(s["ct_lo"], 1)

                def gated(t):
                    Tt = b * TPB + t
                    v.wait_ge(s["pj_ready"], START + Tt + 1)
                    if t >= 2:
                        v.wait_ge(k.x1_done, START + Tt - 1)
                    else:
                        v.wait_ge(k.x1_done, START + b * TPB)
                    nc.vector.tensor_tensor(y[:, t % 2], pj[:, 0:D], k.gate[:, bass.ds(b, 1), :].rearrange("p o d -> p (o d)"),
                                            ALU.mult).then_inc(s["y_done"], 1)

                for g in range(GPB):
                    G = b * GPB + g
                    norm.vector_stats(v, G, b * TPB + g * GT)
                    norm.vector_z(v, G, b * TPB + g * GT)
                    for c in range(KC):
                        v.wait_ge(s["hi_h"], START + G * KC + c + 1)
                        nc.vector.tensor_tensor(hl[:, c], hf[:, c], hh[:, c], ALU.subtract).then_inc(s["lo_h"], 1)
                    for i in range(4):
                        v.wait_ge(s["qk_hi"], START + G * 4 + i + 1)
                        hi, lo = ((qh[:, i], ql[:, i]) if i < 2 else
                                  (kh[:, i - 2, g * GW:(g + 1) * GW], kl[:, i - 2, g * GW:(g + 1) * GW]))
                        nc.vector.tensor_tensor(lo, qf[:, i], hi, ALU.subtract).then_inc(s["qk_lo"], 1)
                    for i in range(2):
                        v.wait_ge(s["v_ready"], START + G * 2 + i + 1)
                        v.wait_ge(s["v_lo"], START + G * 2)
                        for j in range(2):
                            last = nc.vector.tensor_tensor(vf[:, 2 * i + j], (cx, pj)[i][:, j * D:(j + 1) * D],
                                                           k.rows[:, 0:D], ALU.add)
                        last.then_inc(s["vf_done"], 1)
                    for i in range(2):
                        v.wait_ge(s["v_hi"], START + G * 2 + i + 1)
                        a = g * GT + 2 * i
                        nc.vector.tensor_tensor(vl[:, a:a + 2], vf[:, 2 * i:2 * i + 2], vh[:, a:a + 2],
                                                ALU.subtract).then_inc(s["v_lo"], 1)
                    softmax_max(g * GT)
                    for j in range(GT):
                        t = g * GT + j
                        Tt = b * TPB + t
                        for ch in range(NCH[t]):
                            C = b * CHB + OFF[t] + ch
                            w = width(t, ch)
                            v.wait_ge(s["pt_hi"], START + C + 1)
                            slot = (OFF[t] + ch) % 2
                            nc.vector.tensor_tensor(ptl[:, slot, 0:w], tp[:, slot, 0:w], pth[:, slot, 0:w],
                                                    ALU.subtract).then_inc(s["pt_lo"], 1)
                            if ch == 0 and j > 0:
                                ct_lo(Tt)
                        if j < GT - 1:
                            softmax_max(t + 1)
                        if j > 0:
                            gated(t - 1)
                        v.wait_ge(s["exp_done"], START + Tt + 1)
                        chain.link(nc.vector.reciprocal(rinv[:, t % 2:t % 2 + 1], rsum[:, t % 2:t % 2 + 1]))
                        v.wait_ge(s["pv_done"], START + b * CHB + OFF[t + 1])
                        v.wait_ge(s["ct_ready"], START + Tt)
                        nc.vector.tensor_scalar(cn[:], cx[:, 0:D], rinv[:, t % 2:t % 2 + 1], None,
                                                ALU.mult).then_inc(s["cn_done"], 1)
                    ct_lo(b * TPB + g * GT + GT)
                    gated(g * GT + GT - 1)
                assert chain.n == DV

        @block.tensor
        def _(pe):
            begin(pe, s["s_ready"], s["ct_ready"], s["pj_ready"], s["pt_ready"], s["pv_done"], s["qk_ready"], s["v_ready"],
                  norm.zt_done)
            with pe.Fori(0, B) as b:
                def scores(t):
                    j = t % GT
                    for ch in range(NCH[t]):
                        w = width(t, ch)
                        for kc in range(KC):
                            q = slice(j * P, (j + 1) * P)
                            kk = slice(ch * GW, ch * GW + w)
                            last = three(nc.tensor, sc[:, ch, 0:w], qh[:, kc, q], ql[:, kc, q], kh[:, kc, kk], kl[:, kc, kk],
                                         kc == 0, kc == KC - 1)
                    last.then_inc(s["s_ready"], 1)

                def ct(t):
                    Tt = b * TPB + t
                    pe.wait_ge(s["cn_done"], START + Tt + 1)
                    pe.wait_ge(s["y_done"], START + Tt)
                    if t % GT == 0:
                        pe.wait_ge(s["vf_done"], START + (b * GPB + t // GT) * 2 + 2)
                    for c in range(KC):
                        last = nc.tensor.transpose(pj[:, c * P:(c + 1) * P], cn[:, c * P:(c + 1) * P], k.ident[:])
                    last.then_inc(s["ct_ready"], 1)

                def project(t):
                    Tt = b * TPB + t
                    pe.wait_ge(s["ct_lo"], START + Tt + 1)
                    for kc in range(KC):
                        last = three(nc.tensor, pj[:, 0:D], cth[:, kc], ctl[:, kc], wh[:, WO, kc], wl[:, WO, kc],
                                     kc == 0, kc == KC - 1)
                    last.then_inc(s["pj_ready"], 1)

                def turn(t, ch):
                    n = OFF[t] + ch
                    if n >= 2:
                        pe.wait_ge(s["pt_lo"], START + b * CHB + n - 1)
                    for j in range(width(t, ch) // P):
                        a = ch * GW + j * P
                        last = nc.tensor.transpose(tp[:, n % 2, j * P:(j + 1) * P], prob[:, t % 2, a:a + P], k.ident[:])
                    last.then_inc(s["pt_ready"], 1)

                def values(t, ch):
                    n = OFF[t] + ch
                    pe.wait_ge(s["pt_lo"], START + b * CHB + n + 1)
                    if ch == 0:
                        pe.wait_ge(s["cn_done"], START + b * TPB + t)
                        if t % GT == 0:
                            pe.wait_ge(s["vf_done"], START + (b * GPB + t // GT) * 2 + 2)
                            pe.wait_ge(s["v_lo"], START + (b * GPB + t // GT) * 2 + 2)
                    nj = width(t, ch) // P
                    for j in range(nj):
                        a = ch * GT + j
                        q = slice(j * P, (j + 1) * P)
                        last = three(nc.tensor, cx[:, 0:D], pth[:, n % 2, q], ptl[:, n % 2, q], vh[:, a], vl[:, a],
                                     ch == 0 and j == 0, ch == NCH[t] - 1 and j == nj - 1)
                    last.then_inc(s["pv_done"], 1)

                for g in range(GPB):
                    G = b * GPB + g
                    if g == 0:
                        pe.wait_ge(s["pt_lo"], START + b * CHB)
                    else:
                        pe.wait_ge(s["pt_lo"], START + b * CHB + OFF[g * GT])
                    for c in range(KC):
                        norm.tensor(pe, G, c, tp[:, c])
                    pe.wait_ge(s["lo_h"], START + (G + 1) * KC)
                    pe.wait_ge(s["w_lo"], START + 4)
                    pe.wait_ge(s["exp_done"], START + b * TPB + g * GT)
                    for i in range(4):
                        w = WQ if i < 2 else WK
                        c = i % 2
                        for kc in range(KC):
                            m = slice(c * P, (c + 1) * P)
                            last = three(nc.tensor, sc[:, i], wh[:, w, kc, m], wl[:, w, kc, m], hh[:, kc], hl[:, kc],
                                         kc == 0, kc == KC - 1)
                        last.then_inc(s["qk_ready"], 1)
                    pe.wait_ge(s["y_done"], START + b * TPB + g * GT)
                    for i in range(2):
                        bank = (cx, pj)[i]
                        for j in range(2):
                            q = slice((2 * i + j) * P, (2 * i + j + 1) * P)
                            for kc in range(KC):
                                last = three(nc.tensor, bank[:, j * D:(j + 1) * D], hh[:, kc, q], hl[:, kc, q],
                                             wh[:, WV, kc], wl[:, WV, kc], kc == 0, kc == KC - 1)
                        last.then_inc(s["v_ready"], 1)
                    pe.wait_ge(s["qk_lo"], START + (G + 1) * 4)
                    pe.wait_ge(s["qkf"], START + (G + 1) * 4)
                    scores(g * GT)
                    for j in range(GT):
                        t = g * GT + j
                        pe.wait_ge(s["exp_done"], START + b * TPB + t + 1)
                        if j < GT - 1:
                            scores(t + 1)
                        turn(t, 0)
                        if j > 0:
                            ct(t - 1)
                        for ch in range(1, NCH[t]):
                            turn(t, ch)
                            values(t, ch - 1)
                        values(t, NCH[t] - 1)
                        if j > 0:
                            project(t - 1)
                    ct(g * GT + GT - 1)
                    project(g * GT + GT - 1)


def experts(nc, k, d):
    PAIR = 2 * F
    STEPS = E // 2 + 1
    GS = GT * STEPS
    HID = (E + 1) * F
    HC = PAIR // P
    DCH = -(-HID // P)
    TAIL = HID - (DCH - 1) * P
    LAST = GROUPS - 1
    with ExitStack() as ctx:
        sb = lambda n, s, t=F32: ctx.enter_context(nc.sbuf_tensor(n, s, t))
        sem = lambda n: ctx.enter_context(nc.semaphore(n))
        ps = lambda n, s: ctx.enter_context(nc.psum_tensor(n, s, F32))
        raw = [sb("raw_gate", [P, KC, HID]), sb("raw_up", [P, KC, HID]), sb("raw_down", [P, DCH, D])]
        high = [sb("gate_h", [P, KC, HID], F32R), sb("up_h", [P, KC, HID], F32R), sb("down_h", [P, DCH, D], F32R)]
        low = [sb("gate_l", [P, KC, HID], F32R), sb("up_l", [P, KC, HID], F32R), sb("down_l", [P, DCH, D], F32R)]
        router = sb("router", [P, KC, E])
        hf = sb("hf2", [P, KC, GW])
        hh, hl = sb("hh2", [P, GT, KC, P], F32R), sb("hl2", [P, GT, KC, P], F32R)
        act_g = sb("act_g", [P, 2, PAIR])
        hid = sb("hid", [P, 2, PAIR])
        hth, htl = sb("hth", [P, 2, PAIR], F32R), sb("htl", [P, 2, PAIR], F32R)
        y = sb("y2", [P, 2, D])
        iota = sb("iota", [P, GT, E])
        sig, sel, pick, second = (sb(n, [P, GT, E]) for n in ("sig", "sel", "pick", "second"))
        best = sb("best", [P, GT, 8])
        place = sb("place", [P, GT, 8], U32)
        placef = sb("placef", [P, GT, 2])
        total = sb("total", [P, GT])
        w = sb("w", [P, GT, E])
        norm = Norm(nc, k, ctx, "n2", 0, 2)
        gp = ps("gp", [P, 2, 512])
        up = ps("up", [P, 2, 512])
        tp = ps("tp2", [P, 2, 512])
        dp = ps("dp", [P, 512])
        mp = ps("mp", [P, 512])
        w_in = [sem(f"m_w_in{i}") for i in range(3)]
        names = ("w_hi w_lo r_in iota_done hi_h lo_h g_ready u_ready silu_done hid_done ht_ready ht_hi ht_lo "
                 "d_done y_done logits sig_done route dve2")
        s = {n: sem("m_" + n) for n in names.split()}
        block = ctx.enter_context(nc.Block())
        ROUTE = 10
        pieces = [(slice(0, P), 0, slice(0, KC)), (slice(0, P), 1, slice(0, KC)), (slice(0, P), 2, slice(0, DCH - 1)),
                  (slice(0, TAIL), 2, slice(DCH - 1, DCH))]

        def hidden(n):
            return PAIR if n % STEPS < STEPS - 1 else F

        @block.sync
        def _(sp):
            sp.dma_start(router[:], d["router"].rearrange("(c p) e -> p c e", p=P)).then_inc(s["r_in"], 16)
            for i, (we, ws) in enumerate(((d["wg"], d["wg_s"]), (d["wu"], d["wu_s"]))):
                for c in range(KC):
                    sp.dma_start(raw[i][:, c, 0:E * F].rearrange("p (e f) -> p e f", e=E),
                                 we[:, c * P:(c + 1) * P, :].rearrange("e p f -> p e f")).then_inc(w_in[i], 16)
                    sp.dma_start(raw[i][:, c, E * F:HID], ws[c * P:(c + 1) * P, :]).then_inc(w_in[i], 16)
            n = E * F // P
            sp.dma_start(raw[2][:, 0:n, :], d["wd"].rearrange("e f d -> (e f) d").rearrange("(c p) d -> p c d", p=P)).then_inc(w_in[2], 16)
            sp.dma_start(raw[2][:, n, :], d["wd_s"][0:P, :]).then_inc(w_in[2], 16)
            sp.dma_start(raw[2][0:TAIL, n + 1, :], d["wd_s"][P:F, :]).then_inc(w_in[2], 16)

        def loaded(eng, i):
            eng.wait_ge(w_in[pieces[i][1]], (64, 64, 48)[pieces[i][1]])

        def groups(eng, body):
            body(0, True)
            with eng.Fori(1, LAST) as G:
                body(G, False)
            body(LAST, False)

        @block.gpsimd
        def _(pool):
            begin(pool, s["iota_done"], s["hi_h"], norm.ve_done, norm.rstd_done, k.x2_done)
            nc.gpsimd.iota(place[:], pattern=[[0, GT], [1, E]], base=0, channel_multiplier=0).then_inc(s["iota_done"], 1)
            pool.wait_ge(s["iota_done"], START + 1)
            nc.gpsimd.tensor_copy(iota[:], place[:]).then_inc(s["iota_done"], 1)

            def split_hi(G, j):
                pool.wait_ge(norm.h_done, START + (G + 1) * KC)
                if not (isinstance(G, int) and G == 0):
                    pool.wait_ge(s["u_ready"], START + (G - 1) * GS + (j + 1) * STEPS)
                apart(k, pool)
                nc.gpsimd.tensor_copy(hh[:, j], hf[:, :, j * P:(j + 1) * P]).then_inc(s["hi_h"], 1)

            def add(G, j):
                pool.wait_ge(s["y_done"], START + G * GT + j + 1)
                xt = norm.tile(G * GT + j)
                apart(k, pool)
                nc.gpsimd.tensor_tensor(xt, xt, y[:, j % 2], ALU.add).then_inc(k.x2_done, 1)

            norm.gpsimd(pool, 0)
            for j in range(GT):
                split_hi(0, j)

            def body(G, first):
                last = isinstance(G, int) and G == LAST
                if not first:
                    split_hi(G, GT - 1)
                    add(G - 1, GT - 1)
                if not last:
                    norm.gpsimd(pool, G + 1)
                add(G, 0)
                if not last:
                    split_hi(G + 1, 0)
                    split_hi(G + 1, 1)
                add(G, 1)
                if not last:
                    split_hi(G + 1, 2)
                add(G, 2)

            groups(pool, body)
            add(LAST, GT - 1)

        @block.scalar
        def _(act):
            begin(act, s["w_hi"], s["sig_done"], s["silu_done"], s["ht_hi"], norm.h_done)
            for i, (p, t, c) in enumerate(pieces):
                loaded(act, i)
                nc.scalar.copy(high[t][p, c], raw[t][p, c]).then_inc(s["w_hi"], 1)

            def h_of(G, c):
                if isinstance(G, int) and G == 0:
                    norm.scalar(act, G, c, mp[:], hf[:, c], 0)
                else:
                    act.wait_ge(s["lo_h"], START + G * GT)
                    act.wait_ge(s["logits"], START + G)
                    norm.scalar(act, G, c, mp[:], hf[:, c], G // GPB)

            def sigmoid(G):
                act.wait_ge(s["logits"], START + G + 1)
                if not (isinstance(G, int) and G == 0):
                    act.wait_ge(s["route"], START + G * ROUTE)
                nc.scalar.activation(sig[:].rearrange("p t e -> p (t e)"), mp[:, 0:GT * E], ACT.Sigmoid).then_inc(s["sig_done"], 1)

            def silu(G, n):
                S = G * GS + n
                act.wait_ge(s["g_ready"], START + S + 1)
                if not (isinstance(G, int) and G == 0 and n < 2):
                    act.wait_ge(s["hid_done"], START + S - 1)
                nc.scalar.activation(act_g[:, n % 2, 0:hidden(n)], gp[:, n % 2, 0:hidden(n)], ACT.Silu).then_inc(s["silu_done"], 1)

            def ht_hi(G, n):
                S = G * GS + n
                act.wait_ge(s["ht_ready"], START + S + 1)
                if not (isinstance(G, int) and G == 0 and n < 2):
                    act.wait_ge(s["d_done"], START + S - 1)
                wd = PAIR if n % STEPS < STEPS - 1 else 2 * P
                nc.scalar.copy(hth[:, n % 2, 0:wd], tp[:, n % 2, 0:wd]).then_inc(s["ht_hi"], 1)

            h_of(0, 0)
            h_of(0, 1)
            sigmoid(0)

            def body(G, first):
                last = isinstance(G, int) and G == LAST
                for n in range(GS):
                    silu(G, n)
                    if n > 0:
                        ht_hi(G, n - 1)
                    elif not first:
                        ht_hi(G - 1, GS - 1)
                    if not last:
                        if n == 7:
                            h_of(G + 1, 0)
                        if n == 9:
                            h_of(G + 1, 1)
                        if n == 13:
                            sigmoid(G + 1)

            groups(act, body)
            ht_hi(LAST, GS - 1)

        @block.vector
        def _(v):
            begin(v, s["lo_h"], s["route"], s["dve2"], s["hid_done"], s["ht_lo"], s["y_done"], s["w_lo"], norm.bn_done,
                  norm.stats, norm.z_done)
            def split_lo(G, j):
                v.wait_ge(s["hi_h"], START + G * GT + j + 1)
                nc.vector.tensor_tensor(hl[:, j], hf[:, :, j * P:(j + 1) * P], hh[:, j], ALU.subtract).then_inc(s["lo_h"], 1)

            def route(G):
                c = Counted(v, s["route"], G * ROUTE)
                v.wait_ge(s["sig_done"], START + G + 1)
                c.link(nc.vector.tensor_tensor(sel[:], sig[:], k.rows[:, 2 * D:2 * D + E].unsqueeze(1).to_broadcast([P, GT, E]), ALU.add), k)
                for j in range(GT):
                    last = nc.vector.max(best[:, j], sel[:, j])
                c.link(last, k)
                for j in range(GT):
                    last = nc.vector.max_index(place[:, j], best[:, j], sel[:, j])
                c.link(last)
                c.link(nc.vector.tensor_copy(placef[:], place[:, :, 0:2]))
                for i, o in enumerate((pick, second)):
                    last = nc.vector.tensor_tensor(o[:], iota[:], placef[:, :, i:i + 1].to_broadcast([P, GT, E]), ALU.is_equal)
                c.link(last)
                c.link(nc.vector.tensor_tensor(pick[:], pick[:], second[:], ALU.add))
                c.link(nc.vector.tensor_tensor(pick[:], pick[:], sig[:], ALU.mult))
                c.link(nc.vector.tensor_reduce(total[:], pick[:], AX.X, ALU.add))
                c.link(nc.vector.tensor_scalar_add(total[:], total[:], 1e-20))
                nc.vector.reciprocal(total[:], total[:]).then_inc(s["dve2"], 1)
                v.wait_ge(s["dve2"], START + G + 1)
                c.link(nc.vector.tensor_tensor(w[:], pick[:], total[:].unsqueeze(2).to_broadcast([P, GT, E]), ALU.mult))
                assert c.n == ROUTE

            def weigh(G, n):
                S = G * GS + n
                j, p = divmod(n, STEPS)
                v.wait_ge(s["silu_done"], START + S + 1)
                v.wait_ge(s["u_ready"], START + S + 1)
                if not (isinstance(G, int) and G == 0 and n < 2):
                    v.wait_ge(s["ht_ready"], START + S - 1)
                if p < STEPS - 1:
                    for i in range(2):
                        f = slice(i * F, (i + 1) * F)
                        last = nc.vector.scalar_tensor_tensor(out=hid[:, n % 2, f], in0=act_g[:, n % 2, f],
                                                              scalar=w[:, j, 2 * p + i:2 * p + i + 1],
                                                              in1=up[:, n % 2, f], op0=ALU.mult, op1=ALU.mult)
                else:
                    last = nc.vector.tensor_tensor(hid[:, n % 2, 0:F], act_g[:, n % 2, 0:F], up[:, n % 2, 0:F], ALU.mult)
                last.then_inc(s["hid_done"], 1)

            def ht_lo(G, n):
                v.wait_ge(s["ht_hi"], START + G * GS + n + 1)
                wd = PAIR if n % STEPS < STEPS - 1 else 2 * P
                nc.vector.tensor_tensor(htl[:, n % 2, 0:wd], tp[:, n % 2, 0:wd], hth[:, n % 2, 0:wd], ALU.subtract).then_inc(s["ht_lo"], 1)

            def gated(G, j):
                v.wait_ge(s["d_done"], START + G * GS + (j + 1) * STEPS)
                if not (isinstance(G, int) and G == 0 and j < 2):
                    v.wait_ge(k.x2_done, START + G * GT + j - 1)
                b = G // GPB
                nc.vector.tensor_tensor(y[:, j % 2], dp[:, 0:D], k.gate[:, bass.ds(b + 2, 1), :].rearrange("p o d -> p (o d)"),
                                        ALU.mult).then_inc(s["y_done"], 1)

            norm.vector_stats(v, 0, 0)
            norm.vector_z(v, 0, 0)
            for i, (p, t, c) in enumerate(pieces):
                v.wait_ge(s["w_hi"], START + i + 1)
                nc.vector.tensor_tensor(low[t][p, c], raw[t][p, c], high[t][p, c], ALU.subtract).then_inc(s["w_lo"], 1)
            for j in range(GT):
                split_lo(0, j)
            v.wait_ge(s["iota_done"], START + 2)
            route(0)

            def body(G, first):
                last = isinstance(G, int) and G == LAST
                for n in range(GS):
                    weigh(G, n)
                    if n > 0:
                        ht_lo(G, n - 1)
                    elif not first:
                        ht_lo(G - 1, GS - 1)
                    if n == 1 and not first:
                        gated(G - 1, GT - 1)
                        split_lo(G, GT - 1)
                    if n > STEPS and n % STEPS == 1:
                        gated(G, n // STEPS - 1)
                    if not last:
                        if n == 2:
                            norm.vector_stats(v, G + 1, (G + 1) * GT)
                        if n == 5:
                            norm.vector_z(v, G + 1, (G + 1) * GT)
                        if n in (11, 12, 16):
                            split_lo(G + 1, (11, 12, 16).index(n))
                        if n == GS - 1:
                            route(G + 1)

            groups(v, body)
            ht_lo(LAST, GS - 1)
            gated(LAST, GT - 1)

        @block.tensor
        def _(pe):
            begin(pe, s["logits"], s["ht_ready"], s["d_done"], s["g_ready"], s["u_ready"], norm.zt_done)
            def zt(G, c):
                if not (isinstance(G, int) and G == 0):
                    pe.wait_ge(s["sig_done"], START + G)
                if c == 1:
                    pe.wait_ge(norm.h_done, START + G * KC + 1)
                norm.tensor(pe, G, c, mp)

            def logits(G):
                pe.wait_ge(norm.h_done, START + (G + 1) * KC)
                for j in range(GT):
                    for kc in range(KC):
                        last = nc.tensor.matmul(mp[:, j * E:(j + 1) * E], hf[:, kc, j * P:(j + 1) * P], router[:, kc],
                                                start=(kc == 0), stop=(kc == KC - 1))
                last.then_inc(s["logits"], 1)

            def gate_up(G, n):
                S = G * GS + n
                j, p = divmod(n, STEPS)
                if p == 0:
                    pe.wait_ge(s["lo_h"], START + G * GT + j + 1)
                if not (isinstance(G, int) and G == 0 and n < 2):
                    pe.wait_ge(s["hid_done"], START + S - 1)
                f = slice(p * PAIR, p * PAIR + hidden(n))
                for i, (bank, done) in enumerate(((gp, s["g_ready"]), (up, s["u_ready"]))):
                    for kc in range(KC):
                        last = three(nc.tensor, bank[:, n % 2, 0:hidden(n)], hh[:, j, kc], hl[:, j, kc],
                                     high[i][:, kc, f], low[i][:, kc, f], kc == 0, kc == KC - 1)
                    last.then_inc(done, 1)

            def turn(G, n):
                S = G * GS + n
                pe.wait_ge(s["hid_done"], START + S + 1)
                if not (isinstance(G, int) and G == 0 and n < 2):
                    pe.wait_ge(s["ht_lo"], START + S - 1)
                for c in range(-(-hidden(n) // P)):
                    m = min(P, hidden(n) - c * P)
                    last = nc.tensor.transpose(tp[0:m, n % 2, c * P:(c + 1) * P], hid[:, n % 2, c * P:c * P + m], k.ident[:])
                last.then_inc(s["ht_ready"], 1)

            def down(G, n):
                S = G * GS + n
                j, p = divmod(n, STEPS)
                pe.wait_ge(s["ht_lo"], START + S + 1)
                if p == 0:
                    pe.wait_ge(s["y_done"], START + G * GT + j)
                nch = -(-hidden(n) // P)
                for c in range(nch):
                    m = min(P, hidden(n) - c * P)
                    q = slice(c * P, (c + 1) * P)
                    last = three(nc.tensor, dp[:, 0:D], hth[0:m, n % 2, q], htl[0:m, n % 2, q],
                                 high[2][0:m, p * HC + c], low[2][0:m, p * HC + c],
                                 p == 0 and c == 0, p == STEPS - 1 and c == nch - 1)
                last.then_inc(s["d_done"], 1)

            zt(0, 0)
            zt(0, 1)
            pe.wait_ge(s["r_in"], 16)
            logits(0)
            pe.wait_ge(s["w_lo"], START + len(pieces))

            def body(G, first):
                last = isinstance(G, int) and G == LAST
                for n in range(GS):
                    gate_up(G, n)
                    if n >= 1:
                        turn(G, n - 1)
                    elif not first:
                        turn(G - 1, GS - 1)
                    if n >= 2:
                        down(G, n - 2)
                    elif not first:
                        down(G - 1, GS - 2 + n)
                    if not last:
                        if n == 7:
                            zt(G + 1, 0)
                        if n == 9:
                            zt(G + 1, 1)
                        if n == 12:
                            logits(G + 1)

            groups(pe, body)
            turn(LAST, GS - 1)
            down(LAST, GS - 2)
            down(LAST, GS - 1)


def mixing_weights(nc, ws, wh, wl, raw, w_in, w_hi, w_lo):

    def sync(sp):
        for i, w in enumerate(ws):
            sp.dma_start(raw[:, i], w.rearrange("(c p) n -> p c n", p=P)).then_inc(w_in[i], 16)

    def scalar(act, i, src=None):
        act.wait_ge(w_in[i], 16)
        nc.scalar.copy(wh[:, i], raw[:, i]).then_inc(w_hi, 1)

    def vector(v, i):
        v.wait_ge(w_hi, START + i + 1)
        nc.vector.tensor_tensor(wl[:, i], raw[:, i], wh[:, i], ALU.subtract).then_inc(w_lo, 1)

    return sync, scalar, vector


def time_mixing(nc, k, d):
    with ExitStack() as ctx:
        sb = lambda n, s, t=F32: ctx.enter_context(nc.sbuf_tensor(n, s, t))
        sem = lambda n: ctx.enter_context(nc.semaphore(n))
        ps = lambda n, s: ctx.enter_context(nc.psum_tensor(n, s, F32))
        raw = sb("raw3", [P, 4, KC, D])
        wh, wl = sb("wh3", [P, 3, KC, D], F32R), sb("wl3", [P, 3, KC, D], F32R)
        wo = sb("wo3", [P, KC, D])
        wog = sb("wog3", [P, B, KC, D])
        woh, wol = sb("woh3", [P, B, KC, D], F32R), sb("wol3", [P, B, KC, D], F32R)
        ones = sb("ones3", [P, P])
        lnb = sb("lnb3", [P, KC, P])
        csum = sb("csum3", [P, B, D])
        bias = sb("bias3", [P, B, D])
        h = sb("h3", [P, KC, GW + 1])
        delta = sb("delta3", [P, KC, GW])
        xf = sb("xf3", [P, 3, KC, GW])
        xh, xl = sb("xh3", [P, 3, KC, GW], F32R), sb("xl3", [P, 3, KC, GW], F32R)
        ks = sb("ks3", [P, KC, GW])
        kv = sb("kv3", [P, KC, GW])
        st = sb("st3", [P, KC, GW + 1])
        dec = sb("dec3", [P, KC])
        o = sb("o3", [P, KC, GW])
        oh, ol = sb("oh3", [P, KC, GW], F32R), sb("ol3", [P, KC, GW], F32R)
        obn, omv, ove, orstd, nmu = sb("obn3", [P, GT, 6]), sb("omv3", [P, GT, 2]), sb("ove3", [P, GT]), sb("orstd3", [P, GT]), sb("nmu3", [P, GT])
        t1 = sb("t13", [P, GT, D])
        norm = Norm(nc, k, ctx, "n3", 1, 0)
        kvr = ps("kvr", [P, 6, 512])
        zt = ps("zt3", [P, KC, 512])
        w_in = [sem(f"t_w_in{i}") for i in range(4)]
        names = ("w_hi w_lo wo_done wog_done ones_done sums_ready sums_done dec_done carry delta_done xf_done "
                 "hi_x lo_x kvr_ready ks_done kv_done o_done hi_o lo_o ot_ready ostats ove_done orstd_done out_ready "
                 "bias_added dve3 init3")
        s = {n: sem("t_" + n) for n in names.split()}
        block = ctx.enter_context(nc.Block())
        w_sync, w_scalar, w_vector = mixing_weights(nc, (d["w3k"], d["w3v"], d["w3r"], d["w3o"]), wh, wl, raw, w_in, s["w_hi"], s["w_lo"])

        @block.sync
        def _(sp):
            w_sync(sp)

        @block.gpsimd
        def _(pool):
            begin(pool, s["ones_done"], s["init3"], s["carry"], s["delta_done"], s["bias_added"], s["hi_o"], s["ove_done"],
                  s["orstd_done"], norm.ve_done, norm.rstd_done)
            nc.gpsimd.memset(ones[:], 1.0).then_inc(s["ones_done"], 1)
            pool.wait_ge(s["ones_done"], START + 1)
            for c in range(KC):
                last = nc.gpsimd.tensor_scalar_mul(lnb[:, c], ones[:], col(k, "ln_b", c))
            last.then_inc(s["ones_done"], 1)
            pool.wait_ge(s["sums_done"], START + 1)
            with pool.Fori(0, B) as b:
                pool.wait_ge(s["xf_done"], START + b * GPB * 3)
                pool.wait_ge(s["o_done"], START + b * GPB)
                apart(k, pool)
                nc.gpsimd.memset(h[:, :, 0:1], 0.0)
                nc.gpsimd.memset(st[:, :, 0:1], 0.0).then_inc(s["init3"], 1)
                for g in range(GPB):
                    G = b * GPB + g
                    norm.gpsimd(pool, G)
                    if g > 0:
                        pool.wait_ge(s["xf_done"], START + G * 3)
                        apart(k, pool)
                        nc.gpsimd.tensor_copy(h[:, :, 0:1], h[:, :, GW:GW + 1]).then_inc(s["carry"], 1)
                    pool.wait_ge(norm.h_done, START + (G + 1) * KC)
                    if g > 0:
                        pool.wait_ge(s["carry"], START + b * (GPB - 1) + g)
                    else:
                        pool.wait_ge(s["init3"], START + b + 1)
                    nc.gpsimd.tensor_tensor(delta[:], h[:, :, 1:GW + 1], h[:, :, 0:GW], ALU.subtract).then_inc(s["delta_done"], 1)
                    apart(k, pool)
                    for j in range(GT):
                        xt = norm.tile(G * GT + j)
                        last = nc.gpsimd.tensor_tensor(xt, xt, bias[:, bass.ds(b, 1), :].rearrange("p o d -> p (o d)"), ALU.add)
                    last.then_inc(s["bias_added"], 1)
                    pool.wait_ge(s["o_done"], START + G + 1)
                    pool.wait_ge(s["out_ready"], START + G * 2)
                    apart(k, pool)
                    nc.gpsimd.tensor_copy(oh[:], o[:]).then_inc(s["hi_o"], 1)
                    pool.wait_ge(s["ostats"], START + G + 1)
                    apart(k, pool)
                    nc.gpsimd.tensor_scalar_add(ove[:], omv[:, :, 1], EPS).then_inc(s["ove_done"], 1)
                    pool.wait_ge(s["ove_done"], START + G + 1)
                    pool.wait_ge(k.x3_done, START + G * GT)
                    nc.gpsimd.tensor_tensor(orstd[:], ove[:], k.mhalf[:], ALU.pow).then_inc(s["orstd_done"], 1)

        @block.scalar
        def _(act):
            begin(act, s["dec_done"], s["w_hi"], s["hi_x"], s["ks_done"], norm.h_done)
            nc.scalar.activation(dec[:], k.cols[:, :, COL["decay"]], ACT.Exp).then_inc(s["dec_done"], 1)
            for i in range(3):
                w_scalar(act, i)
            act.wait_ge(s["wog_done"], START + 1)
            nc.scalar.copy(woh[:], wog[:]).then_inc(s["w_hi"], 1)
            with act.Fori(0, B) as b:
                for g in range(GPB):
                    G = b * GPB + g
                    for c in range(KC):
                        act.wait_ge(s["delta_done"], START + G)
                        act.wait_ge(s["xf_done"], START + G * 3)
                        if g > 0:
                            act.wait_ge(s["carry"], START + b * (GPB - 1) + g)
                        else:
                            act.wait_ge(s["carry"], START + b * (GPB - 1))
                        norm.scalar(act, G, c, zt[:, c], h[:, c, 1:GW + 1], b)
                    for i in range(3):
                        act.wait_ge(s["xf_done"], START + G * 3 + i + 1)
                        act.wait_ge(s["kvr_ready"], START + G * 6)
                        nc.scalar.copy(xh[:, i], xf[:, i]).then_inc(s["hi_x"], 1)
                    for c in range(KC):
                        act.wait_ge(s["kvr_ready"], START + G * 6 + 3 * c + 1)
                        act.wait_ge(s["kv_done"], START + G * KC)
                        nc.scalar.copy(ks[:, c], kvr[:, 3 * c]).then_inc(s["ks_done"], 1)

        @block.vector
        def _(v):
            begin(v, s["wo_done"], s["wog_done"], s["w_lo"], s["sums_done"], s["dve3"], s["xf_done"], s["lo_x"], s["kv_done"],
                  s["o_done"], s["lo_o"], s["ostats"], norm.bn_done, norm.stats, norm.z_done, k.x3_done)
            for i in range(3):
                w_vector(v, i)
            v.wait_ge(w_in[3], 16)
            for c in range(KC):
                last = nc.vector.tensor_scalar(wo[:, c], raw[:, 3, c], col(k, "ln_g", c), None, ALU.mult)
            last.then_inc(s["wo_done"], 1)
            v.wait_ge(s["wo_done"], START + 1)
            for b in range(B):
                for c in range(KC):
                    last = nc.vector.tensor_tensor(wog[:, b, c], wo[:, c], k.gate[:, 4 + b], ALU.mult)
            last.then_inc(s["wog_done"], 1)
            v.wait_ge(s["w_hi"], START + 4)
            nc.vector.tensor_tensor(wol[:], wog[:], woh[:], ALU.subtract).then_inc(s["w_lo"], 1)
            v.wait_ge(s["sums_ready"], START + 1)
            nc.vector.tensor_copy(csum[:].rearrange("p b d -> p (b d)"), kvr[:, 0])
            for b in range(B):
                last = nc.vector.tensor_tensor(bias[:, b], kvr[:, 1, 0:D], k.gate[:, 4 + b], ALU.mult)
            last.then_inc(s["sums_done"], 1)
            v.wait_ge(s["sums_done"], START + 1)
            v.wait_ge(s["dec_done"], START + 1)
            PER = 12
            with v.Fori(0, B) as b:
                c3 = Counted(v, s["dve3"], b * GPB * PER)
                for g in range(GPB):
                    G = b * GPB + g
                    norm.vector_stats(v, G, G * GT)
                    norm.vector_z(v, G, G * GT)
                    v.wait_ge(s["delta_done"], START + G + 1)
                    v.wait_ge(s["lo_x"], START + G * 3)
                    for i, mix in enumerate(("mix_k", "mix_v", "mix_r")):
                        for c in range(KC):
                            last = nc.vector.scalar_tensor_tensor(out=xf[:, i, c], in0=delta[:, c], scalar=col(k, mix, c),
                                                                  in1=h[:, c, 0:GW], op0=ALU.mult, op1=ALU.add)
                        last.then_inc(s["xf_done"], 1)
                    for i in range(3):
                        v.wait_ge(s["hi_x"], START + G * 3 + i + 1)
                        nc.vector.tensor_tensor(xl[:, i], xf[:, i], xh[:, i], ALU.subtract).then_inc(s["lo_x"], 1)
                    if g == 0:
                        v.wait_ge(s["init3"], START + b + 1)
                    for c in range(KC):
                        v.wait_ge(s["ks_done"], START + G * KC + c + 1)
                        v.wait_ge(s["kvr_ready"], START + G * 6 + 3 * c + 2)
                        nc.vector.tensor_tensor(kv[:, c], ks[:, c], kvr[:, 3 * c + 1], ALU.mult).then_inc(s["kv_done"], 1)
                        v.wait_ge(s["kv_done"], START + G * KC + c + 1)
                        c3.link(nc.vector.tensor_tensor_scan(st[:, c, 1:GW + 1], dec[:, c:c + 1].to_broadcast([P, GW]), kv[:, c],
                                                             st[:, c, 0:1], ALU.mult, ALU.add))
                        c3.link(nc.vector.scalar_tensor_tensor(out=o[:, c], in0=kv[:, c], scalar=col(k, "first", c),
                                                               in1=st[:, c, 1:GW + 1], op0=ALU.mult, op1=ALU.add))
                        c3.link(nc.vector.tensor_copy(st[:, c, 0:1], st[:, c, GW:GW + 1]))
                        v.wait_ge(s["kvr_ready"], START + G * 6 + 3 * c + 3)
                        c3.link(nc.vector.tensor_tensor(o[:, c], o[:, c], kvr[:, 3 * c + 2], ALU.mult))
                    nc.vector.tensor_copy(nmu[:], ove[:] if False else k.mhalf[:]).then_inc(s["o_done"], 1)
                    v.wait_ge(s["hi_o"], START + G + 1)
                    nc.vector.tensor_tensor(ol[:], o[:], oh[:], ALU.subtract).then_inc(s["lo_o"], 1)
                    v.wait_ge(s["ot_ready"], START + G + 1)
                    for j in range(GT):
                        last = nc.vector.bn_stats(obn[:, j], kvr[:, j // 2, (j % 2) * D:(j % 2 + 1) * D])
                    c3.link(last, k)
                    for j in range(GT):
                        last = nc.vector.bn_aggr(omv[:, j], obn[:, j])
                    last.then_inc(s["ostats"], 1)
                    v.wait_ge(s["ostats"], START + G + 1)
                    c3.link(nc.vector.tensor_scalar(nmu[:], omv[:, :, 0], -1.0, None, ALU.mult))
                    v.wait_ge(s["orstd_done"], START + G + 1)
                    v.wait_ge(s["bias_added"], START + G + 1)
                    for i in range(2):
                        v.wait_ge(s["out_ready"], START + G * 2 + i + 1)
                        for j in (2 * i, 2 * i + 1):
                            last = nc.vector.scalar_tensor_tensor(out=t1[:, j], in0=csum[:, bass.ds(b, 1), :].rearrange("p o d -> p (o d)"),
                                                                  scalar=nmu[:, j:j + 1], in1=kvr[:, 2 + i, (j % 2) * D:(j % 2 + 1) * D],
                                                                  op0=ALU.mult, op1=ALU.add)
                        c3.link(last)
                        for j in (2 * i, 2 * i + 1):
                            xt = norm.tile(G * GT + j)
                            nc.vector.scalar_tensor_tensor(out=xt, in0=t1[:, j], scalar=orstd[:, j:j + 1], in1=xt,
                                                           op0=ALU.mult, op1=ALU.add).then_inc(k.x3_done, 1)
                assert c3.n == GPB * PER, c3.n

        @block.tensor
        def _(pe):
            begin(pe, s["sums_ready"], s["kvr_ready"], s["ot_ready"], s["out_ready"], norm.zt_done)
            pe.wait_ge(s["ones_done"], START + 2)
            pe.wait_ge(s["wog_done"], START + 1)
            for b in range(B):
                for c in range(KC):
                    nc.tensor.matmul(kvr[:, 0, b * D:(b + 1) * D], ones[:], wog[:, b, c], start=(c == 0), stop=(c == KC - 1))
            for c in range(KC):
                last = nc.tensor.matmul(kvr[:, 1, 0:D], lnb[:, c], raw[:, 3, c], start=(c == 0), stop=(c == KC - 1))
            last.then_inc(s["sums_ready"], 1)
            pe.wait_ge(s["sums_done"], START + 1)
            pe.wait_ge(s["w_lo"], START + 4)
            with pe.Fori(0, B) as b:
                for g in range(GPB):
                    G = b * GPB + g
                    pe.wait_ge(norm.h_done, START + G * KC)
                    for c in range(KC):
                        norm.tensor(pe, G, c, zt[:, c])
                    pe.wait_ge(k.x3_done, START + G * GT)
                    for c in range(KC):
                        m = slice(c * P, (c + 1) * P)
                        for i in range(3):
                            if c == 0:
                                pe.wait_ge(s["lo_x"], START + G * 3 + i + 1)
                            for kc in range(KC):
                                last = three(nc.tensor, kvr[:, 3 * c + i], wh[:, i, kc, m], wl[:, i, kc, m], xh[:, i, kc], xl[:, i, kc],
                                             kc == 0, kc == KC - 1)
                            last.then_inc(s["kvr_ready"], 1)
                    pe.wait_ge(s["o_done"], START + G + 1)
                    for j in range(GT):
                        for c in range(KC):
                            a = (j % 2) * D + c * P
                            last = nc.tensor.transpose(kvr[:, j // 2, a:a + P], o[:, c, j * P:(j + 1) * P], k.ident[:])
                    last.then_inc(s["ot_ready"], 1)
                    pe.wait_ge(s["lo_o"], START + G + 1)
                    for j in range(GT):
                        q = slice(j * P, (j + 1) * P)
                        for c in range(KC):
                            last = three_b(nc.tensor, kvr[:, 2 + j // 2, (j % 2) * D:(j % 2 + 1) * D], oh[:, c, q], ol[:, c, q],
                                           woh, wol, b, c)
                        if j % 2:
                            last.then_inc(s["out_ready"], 1)


def three_b(eng, out, lh, ll, rh, rl, b, c):
    pick = lambda r: r[:, bass.ds(b, 1), c, :].rearrange("p o d -> p (o d)")
    return three(eng, out, lh, ll, pick(rh), pick(rl), c == 0, c == KC - 1)


def channel_mixing(nc, k, d):
    with ExitStack() as ctx:
        sb = lambda n, s, t=F32: ctx.enter_context(nc.sbuf_tensor(n, s, t))
        sem = lambda n: ctx.enter_context(nc.semaphore(n))
        ps = lambda n, s: ctx.enter_context(nc.psum_tensor(n, s, F32))
        raw = sb("raw4", [P, 3, KC, D])
        wh, wl = sb("wh4", [P, 3, KC, D], F32R), sb("wl4", [P, 3, KC, D], F32R)
        h = sb("h4", [P, KC, GW + 1])
        delta = sb("delta4", [P, KC, GW])
        xf = sb("xf4", [P, 2, KC, GW])
        xh, xl = sb("xh4", [P, 2, KC, GW], F32R), sb("xl4", [P, 2, KC, GW], F32R)
        kr = sb("kr4", [P, KC, GW])
        ka = sb("ka4", [P, KC, GW])
        kah, kal = sb("kah4", [P, KC, GW], F32R), sb("kal4", [P, KC, GW], F32R)
        sr = sb("sr4", [P, GT, D])
        t1 = sb("t14", [P, GT, D])
        t2 = sb("t24", [P, GT, D])
        norm = Norm(nc, k, ctx, "n4", 1, 2)
        kp = ps("kp4", [P, KC, 512])
        rp = ps("rp4", [P, 2, 512])
        vp = ps("vp4", [P, 2, 512])
        zt = ps("zt4", [P, KC, 512])
        w_in = [sem(f"c_w_in{i}") for i in range(3)]
        names = ("w_hi w_lo carry init delta_done xf_done hi_x lo_x k_ready r_ready kr_done ka_done hi_k lo_k "
                 "sr_done v_ready t1_done t2_done x4_done")
        s = {n: sem("c_" + n) for n in names.split()}
        block = ctx.enter_context(nc.Block())
        w_sync, w_scalar, w_vector = mixing_weights(nc, (d["w4k"], d["w4r"], d["w4v"]), wh, wl, raw, w_in, s["w_hi"], s["w_lo"])

        @block.sync
        def _(sp):
            w_sync(sp)
            with sp.Fori(0, GROUPS) as G:
                sp.wait_ge(s["x4_done"], START + (G + 1) * GT)
                sp.dma_start(d["out"][bass.ds(G, 1)].rearrange("o (t p) d -> p (o t) d", p=P),
                             k.x[:, bass.ds(G * GT, GT), :]).then_inc(k.stored, 16)
            sp.wait_ge(k.stored, GROUPS * 16)

        @block.gpsimd
        def _(pool):
            begin(pool, s["init"], s["carry"], s["delta_done"], s["ka_done"], s["t2_done"], s["x4_done"], norm.ve_done,
                  norm.rstd_done)
            with pool.Fori(0, B) as b:
                pool.wait_ge(s["xf_done"], START + b * GPB * 2)
                apart(k, pool)
                nc.gpsimd.memset(h[:, :, 0:1], 0.0).then_inc(s["init"], 1)
                for g in range(GPB):
                    G = b * GPB + g
                    norm.gpsimd(pool, G)
                    if g > 0:
                        pool.wait_ge(s["xf_done"], START + G * 2)
                        apart(k, pool)
                        nc.gpsimd.tensor_copy(h[:, :, 0:1], h[:, :, GW:GW + 1]).then_inc(s["carry"], 1)
                    pool.wait_ge(norm.h_done, START + (G + 1) * KC)
                    if g > 0:
                        pool.wait_ge(s["carry"], START + b * (GPB - 1) + g)
                    else:
                        pool.wait_ge(s["init"], START + b + 1)
                    nc.gpsimd.tensor_tensor(delta[:], h[:, :, 1:GW + 1], h[:, :, 0:GW], ALU.subtract).then_inc(s["delta_done"], 1)
                    for c in range(KC):
                        pool.wait_ge(s["kr_done"], START + G * KC + c + 1)
                        pool.wait_ge(s["lo_k"], START + G * KC)
                        nc.gpsimd.tensor_tensor(ka[:, c], kr[:, c], kr[:, c], ALU.mult).then_inc(s["ka_done"], 1)
                    for j in range(GT):
                        pool.wait_ge(s["t1_done"], START + G * GT + j + 1)
                        apart(k, pool)
                        nc.gpsimd.tensor_tensor(t2[:, j], t1[:, j], k.gate[:, bass.ds(b + 6, 1), :].rearrange("p o d -> p (o d)"),
                                                ALU.mult).then_inc(s["t2_done"], 1)
                        pool.wait_ge(s["t2_done"], START + G * GT + j + 1)
                        xt = norm.tile(G * GT + j)
                        apart(k, pool)
                        nc.gpsimd.tensor_tensor(xt, xt, t2[:, j], ALU.add).then_inc(s["x4_done"], 1)

        @block.scalar
        def _(act):
            begin(act, s["hi_x"], s["kr_done"], s["hi_k"], s["sr_done"], s["w_hi"], norm.h_done)
            for i in range(3):
                w_scalar(act, i)
            with act.Fori(0, B) as b:
                for g in range(GPB):
                    G = b * GPB + g
                    for c in range(KC):
                        act.wait_ge(s["delta_done"], START + G)
                        act.wait_ge(s["xf_done"], START + G * 2)
                        act.wait_ge(s["carry"], START + b * (GPB - 1) + g)
                        norm.scalar(act, G, c, zt[:, c], h[:, c, 1:GW + 1], b)
                    for i in range(2):
                        act.wait_ge(s["xf_done"], START + G * 2 + i + 1)
                        act.wait_ge(s["r_ready"], START + G * 2)
                        nc.scalar.copy(xh[:, i], xf[:, i]).then_inc(s["hi_x"], 1)
                    for c in range(KC):
                        act.wait_ge(s["k_ready"], START + G * KC + c + 1)
                        act.wait_ge(s["ka_done"], START + G * KC)
                        nc.scalar.activation(kr[:, c], kp[:, c], ACT.Relu).then_inc(s["kr_done"], 1)
                    for c in range(KC):
                        act.wait_ge(s["ka_done"], START + G * KC + c + 1)
                        act.wait_ge(s["v_ready"], START + G * 2)
                        nc.scalar.copy(kah[:, c], ka[:, c]).then_inc(s["hi_k"], 1)
                    for i in range(2):
                        act.wait_ge(s["r_ready"], START + G * 2 + i + 1)
                        act.wait_ge(s["t1_done"], START + G * GT)
                        nc.scalar.activation(sr[:, 2 * i:2 * i + 2].rearrange("p t d -> p (t d)"), rp[:, i], ACT.Sigmoid).then_inc(s["sr_done"], 1)

        @block.vector
        def _(v):
            begin(v, s["xf_done"], s["lo_x"], s["lo_k"], s["t1_done"], s["w_lo"], norm.bn_done, norm.stats, norm.z_done)
            for i in range(3):
                w_vector(v, i)
            with v.Fori(0, B) as b:
                for g in range(GPB):
                    G = b * GPB + g
                    norm.vector_stats(v, G, G * GT)
                    norm.vector_z(v, G, G * GT)
                    v.wait_ge(s["delta_done"], START + G + 1)
                    v.wait_ge(s["lo_x"], START + G * 2)
                    for i, mix in enumerate(("mu_k", "mu_r")):
                        for c in range(KC):
                            last = nc.vector.scalar_tensor_tensor(out=xf[:, i, c], in0=delta[:, c], scalar=col(k, mix, c),
                                                                  in1=h[:, c, 0:GW], op0=ALU.mult, op1=ALU.add)
                        last.then_inc(s["xf_done"], 1)
                    for i in range(2):
                        v.wait_ge(s["hi_x"], START + G * 2 + i + 1)
                        nc.vector.tensor_tensor(xl[:, i], xf[:, i], xh[:, i], ALU.subtract).then_inc(s["lo_x"], 1)
                    for c in range(KC):
                        v.wait_ge(s["hi_k"], START + G * KC + c + 1)
                        nc.vector.tensor_tensor(kal[:, c], ka[:, c], kah[:, c], ALU.subtract).then_inc(s["lo_k"], 1)
                    for i in range(2):
                        v.wait_ge(s["sr_done"], START + G * 2 + i + 1)
                        v.wait_ge(s["v_ready"], START + G * 2 + i + 1)
                        v.wait_ge(s["t2_done"], START + G * GT)
                        for j in (2 * i, 2 * i + 1):
                            nc.vector.tensor_tensor(t1[:, j], sr[:, j], vp[:, i, (j % 2) * D:(j % 2 + 1) * D], ALU.mult).then_inc(s["t1_done"], 1)

        @block.tensor
        def _(pe):
            begin(pe, s["k_ready"], s["r_ready"], s["v_ready"], norm.zt_done)
            pe.wait_ge(s["w_lo"], START + 3)
            with pe.Fori(0, B) as b:
                for g in range(GPB):
                    G = b * GPB + g
                    pe.wait_ge(norm.h_done, START + G * KC)
                    for c in range(KC):
                        norm.tensor(pe, G, c, zt[:, c])
                    pe.wait_ge(s["lo_x"], START + G * 2 + 1)
                    pe.wait_ge(s["kr_done"], START + G * KC)
                    for c in range(KC):
                        m = slice(c * P, (c + 1) * P)
                        for kc in range(KC):
                            last = three(nc.tensor, kp[:, c], wh[:, 0, kc, m], wl[:, 0, kc, m], xh[:, 0, kc], xl[:, 0, kc],
                                         kc == 0, kc == KC - 1)
                        last.then_inc(s["k_ready"], 1)
                    pe.wait_ge(s["lo_x"], START + G * 2 + 2)
                    pe.wait_ge(s["sr_done"], START + G * 2)
                    for j in range(GT):
                        q = slice(j * P, (j + 1) * P)
                        for kc in range(KC):
                            last = three(nc.tensor, rp[:, j // 2, (j % 2) * D:(j % 2 + 1) * D], xh[:, 1, kc, q], xl[:, 1, kc, q],
                                         wh[:, 1, kc], wl[:, 1, kc], kc == 0, kc == KC - 1)
                        if j % 2:
                            last.then_inc(s["r_ready"], 1)
                    pe.wait_ge(s["lo_k"], START + (G + 1) * KC)
                    pe.wait_ge(s["t1_done"], START + G * GT)
                    for j in range(GT):
                        q = slice(j * P, (j + 1) * P)
                        for kc in range(KC):
                            last = three(nc.tensor, vp[:, j // 2, (j % 2) * D:(j % 2 + 1) * D], kah[:, kc, q], kal[:, kc, q],
                                         wh[:, 2, kc], wl[:, 2, kc], kc == 0, kc == KC - 1)
                        if j % 2:
                            last.then_inc(s["v_ready"], 1)


def program(nc, d, stages=4):
    with ExitStack() as ctx:
        sb = lambda n, s, t=F32: ctx.enter_context(nc.sbuf_tensor(n, s, t))
        k = Kept()
        k.sem = lambda n: ctx.enter_context(nc.semaphore(n))
        k.x = sb("x", [P, TILES, D])
        k.cols = sb("cols", [P, KC, len(COLS)])
        k.rows = sb("rows", [P, 2 * D + E])
        k.colmod = sb("colmod", [P, 2, 4, KC, B])
        k.gate = sb("gate", [P, 8, D])
        k.bo_gate = sb("bo_gate", [P, B, D])
        k.ident = sb("ident", [P, P])
        k.causal = sb("causal", [P, P])
        k.mhalf = sb("mhalf", [P, GT])
        k.consts, k.x1_done, k.x2_done, k.x3_done, k.stored = (k.sem(n) for n in ("consts", "x1_done", "x2_done", "x3_done", "stored"))
        k.passed = {nc.gpsimd.engine: k.sem("passed_gpsimd"), nc.vector.engine: k.sem("passed_vector"),
                    nc.scalar.engine: k.sem("passed_scalar")}
        setup(nc, k, d)
        if stages >= 1:
            attention(nc, k, d)
        if stages >= 2:
            experts(nc, k, d)
        if stages >= 3:
            time_mixing(nc, k, d)
        if stages >= 4:
            channel_mixing(nc, k, d)
        else:
            block = ctx.enter_context(nc.Block())

            @block.sync
            def _(sp):
                for G in range(GROUPS):
                    sp.wait_ge(k.x_in[G // GPB], 16 * GPB)
                    sp.dma_start(d["out"][G].rearrange("(t p) d -> p t d", p=P), k.x[:, G * GT:(G + 1) * GT, :]).then_inc(k.stored, 16)
                sp.wait_ge(k.stored, GROUPS * 16)


def layout(inputs):
    a = {n: np.asarray(v) for n, v in inputs.items()}
    vec = {"bq": "L0_attn_bq", "bk": "L0_attn_bk", "mix_k": "L1_attn_time_mix_k", "mix_v": "L1_attn_time_mix_v",
           "mix_r": "L1_attn_time_mix_r", "decay": "L1_attn_time_decay", "first": "L1_attn_time_first",
           "ln_g": "L1_attn_ln_g", "ln_b": "L1_attn_ln_b", "mu_r": "L1_ffn_mu_r", "mu_k": "L1_ffn_mu_k"}
    rows = [a[vec[n]].reshape(D) for n in COLS[:C0]] + [a[f"L{l}_c"][b] for l in range(2) for b in range(B)]
    out = {
        "x": a["L0_attn_y_all"].reshape(B * T, D),
        "cols": np.ascontiguousarray(np.stack(rows).reshape(len(COLS), KC, P).transpose(2, 1, 0)),
        "rows": np.concatenate([a["L0_attn_bv"], a["L0_attn_bo"], a["L0_ffn_expert_bias"]]).reshape(1, 2 * D + E),
        "wmod": np.stack([a["L0_wmod"], a["L1_wmod"]]),
        "wq": a["L0_attn_Wq"], "wk": a["L0_attn_Wk"], "wv": a["L0_attn_Wv"], "wo": a["L0_attn_Wo"],
        "router": a["L0_ffn_W_gate_router"], "wg": a["L0_ffn_Wg"], "wu": a["L0_ffn_Wu"], "wd": a["L0_ffn_Wd"],
        "wg_s": a["L0_ffn_Wg_s"], "wu_s": a["L0_ffn_Wu_s"], "wd_s": a["L0_ffn_Wd_s"],
    }
    for n, w in (("w3k", "L1_attn_Wk"), ("w3v", "L1_attn_Wv"), ("w3r", "L1_attn_Wr"), ("w3o", "L1_attn_Wo"),
                 ("w4k", "L1_ffn_W_k"), ("w4r", "L1_ffn_W_r"), ("w4v", "L1_ffn_W_v")):
        out[n] = a[w].T
    return {n: np.ascontiguousarray(v) for n, v in out.items()}


def kernel(**inputs):
    import concourse.bacc as bacc
    from concourse.bass_utils import run_bass_kernel_spmd

    arrays = layout(inputs)
    nc = bacc.Bacc("TRN2", target_bir_lowering=False, num_devices=1)
    d = {n: nc.dram_tensor("in_" + n, v.shape, mybir.dt.from_np(v.dtype), kind="ExternalInput").ap()
                     for n, v in arrays.items()}
    d["out"] = nc.dram_tensor("out", (GROUPS, GW, D), F32, kind="ExternalOutput").ap()
    program(nc, d)
    result = run_bass_kernel_spmd(nc, [{"in_" + n: v for n, v in arrays.items()}], core_ids=[0])
    return result.results[0]["out"].reshape(B, T, D)
```

```python
from contextlib import ExitStack

import numpy as np

import concourse.bass as bass
from concourse import mybir



class Kept:
    pass


ALU = mybir.AluOpType
ACT = mybir.ActivationFunctionType
AX = mybir.AxisListType
F32 = mybir.dt.float32
F32R = mybir.dt.float32r
U32 = mybir.dt.uint32

P = 128
B, T, D = 2, 2048, 256
KC = D // P
TILES = B * T // P
TPB = T // P
GT = 4
GROUPS = TILES // GT
GPB = GROUPS // B
GW = GT * P
EPS = 1e-5
E = 8
F = 192
NEG = -1e30

COLS = ["bq", "bk", "mix_k", "mix_v", "mix_r", "decay", "first", "ln_g", "ln_b", "mu_r", "mu_k",
        "c00", "c01", "c10", "c11"]
COL = {n: i for i, n in enumerate(COLS)}
C0 = COL["c00"]
SHIFT_A, SCALE_A, GATE_A, SHIFT_B, SCALE_B, GATE_B = range(6)
COLKINDS = [SHIFT_A, SCALE_A, SHIFT_B, SCALE_B]


START = 1


def begin(eng, *sems):
    for sem in sems:
        eng.sem_inc(sem, START)


class Counted:

    def __init__(self, eng, sem, base=0):
        self.eng, self.sem, self.base, self.n = eng, sem, base, 0

    def link(self, ins, k=None):
        ins.then_inc(self.sem, 1)
        self.n += 1
        self.eng.wait_ge(self.sem, START + self.base + self.n)
        if k:
            apart(k, self.eng)


def three(eng, out, lh, ll, rh, rl, first, last):
    eng.matmul(out, lh, rh, start=first, stop=False)
    eng.matmul(out, lh, rl, start=False, stop=False)
    return eng.matmul(out, ll, rh, start=False, stop=last)


def apart(k, eng):
    eng.sem_inc(k.passed[eng.engine], 1)


def col(k, name, c):
    return k.cols[:, c, COL[name]:COL[name] + 1]


def setup(nc, k, d):
    with ExitStack() as ctx:
        sb = lambda n, s, t=F32: ctx.enter_context(nc.sbuf_tensor(n, s, t))
        sem = lambda n: ctx.enter_context(nc.semaphore(n))
        KINDS = 6
        ROWS = 3 * B
        wmod = sb("wmod", [P, 2, KC, KINDS * D])
        silu_c = sb("silu_c", [P, KC, 4])
        silu_t = sb("silu_t", [P, KC, 4])
        graw = sb("graw", [P, 2, 2, KC, B])
        gabs = sb("gabs", [P, 2, 2, KC, B])
        gate_bc = sb("gate_bc", [P, ROWS, KC, P])
        colp = ctx.enter_context(nc.psum_tensor("colp", [P, 2, KINDS, KC, B], F32))
        rowp = ctx.enter_context(nc.psum_tensor("rowp", [P, ROWS, D], F32))
        small_in, wmod_in, silu_e, dve, bc_ready, cols_done, rows_done, rows_out, id0 = (
            sem(n) for n in ("small_in", "wmod_in", "silu_e", "s0_dve", "bc_ready",
                             "cols_done", "rows_done", "rows_out", "id0"))
        k.x_in = [k.sem(f"x_in{b}") for b in range(B)]
        block = ctx.enter_context(nc.Block())

        @block.sync
        def _(sp):
            sp.dma_start(k.cols[:], d["cols"]).then_inc(small_in, 16)
            for l in range(2):
                sp.dma_start(wmod[:, l], d["wmod"][l].rearrange("(c p) n -> p c n", p=P)).then_inc(wmod_in, 16)
            sp.dma_start(k.rows[:], d["rows"].to_broadcast([P, 2 * D + E])).then_inc(small_in, 16)
            for g in range(GROUPS):
                sp.dma_start(k.x[:, g * GT:(g + 1) * GT, :],
                             d["x"][g * GW:(g + 1) * GW, :].rearrange("(t p) d -> p t d", p=P)).then_inc(k.x_in[g // GPB], 16)

        @block.gpsimd
        def _(pool):
            nc.gpsimd.memset(k.ident[:], 0.0).then_inc(id0, 1)
            nc.gpsimd.memset(k.causal[:], 0.0).then_inc(id0, 1)
            nc.gpsimd.memset(k.mhalf[:], -0.5)
            pool.wait_ge(id0, 2)
            nc.gpsimd.affine_select(out=k.ident[:], in_=k.ident[:], compare_op=ALU.not_equal, fill=1.0,
                                    base=0, pattern=[[-1, P]], channel_multiplier=1)
            nc.gpsimd.affine_select(out=k.causal[:], in_=k.causal[:], compare_op=ALU.is_ge, fill=NEG,
                                    base=0, pattern=[[-1, P]], channel_multiplier=1).then_inc(k.consts, 1)

        @block.scalar
        def _(act):
            act.wait_ge(small_in, 32)
            nc.scalar.activation(silu_t[:], k.cols[:, :, C0:C0 + 4], ACT.Exp, scale=-1.0).then_inc(silu_e, 1)
            act.wait_ge(rows_done, 1)
            nc.scalar.copy(k.gate[:], rowp[:]).then_inc(rows_out, 1)

        @block.vector
        def _(v):
            c = Counted(v, dve, -START)
            v.wait_ge(silu_e, 1)
            c.link(nc.vector.tensor_scalar_add(silu_t[:], silu_t[:], 1.0))
            c.link(nc.vector.reciprocal(silu_t[:], silu_t[:]))
            nc.vector.tensor_tensor(silu_c[:], silu_t[:], k.cols[:, :, C0:C0 + 4], ALU.mult).then_inc(bc_ready, 1)
            v.wait_ge(cols_done, 1)
            for l in range(2):
                for i, kind in enumerate(COLKINDS):
                    add = 1.0 if kind in (SCALE_A, SCALE_B) else 0.0
                    nc.vector.tensor_scalar_add(k.colmod[:, l, i], colp[:, l, kind], add)
            for l in range(2):
                for i, kind in enumerate((GATE_A, GATE_B)):
                    last = nc.vector.tensor_copy(graw[:, l, i], colp[:, l, kind])
            c.link(last)
            c.link(nc.vector.tensor_scalar(gabs[:], graw[:], -1.0, None, ALU.mult))
            c.link(nc.vector.tensor_tensor(gabs[:], gabs[:], graw[:], ALU.max))
            c.link(nc.vector.tensor_scalar(graw[:], graw[:], 0.0, 2.0, ALU.is_ge, ALU.mult))
            c.link(nc.vector.tensor_scalar(graw[:], graw[:], -1.0, None, ALU.add))
            c.link(nc.vector.tensor_scalar(gabs[:], gabs[:], 0.25, None, ALU.max))
            c.link(nc.vector.tensor_tensor(k.gatecol[:], gabs[:], graw[:], ALU.mult))
            for r in range(ROWS):
                for kc in range(KC):
                    last = nc.vector.tensor_copy(gate_bc[:, r, kc],
                                                 k.gatecol[:, r // 4, r // B % 2, kc, r % B:r % B + 1].to_broadcast([P, P]))
            last.then_inc(bc_ready, 1)
            v.wait_ge(rows_out, 1)
            for b in range(B):
                nc.vector.tensor_tensor(k.bo_gate[:, b], k.gate[:, b], k.rows[:, D:2 * D], ALU.mult)

        @block.tensor
        def _(pe):
            pe.wait_ge(wmod_in, 32)
            pe.wait_ge(bc_ready, 1)
            for l in range(2):
                for kind in range(KINDS):
                    for c in range(KC):
                        for kc in range(KC):
                            o = kind * D + c * P
                            last = nc.tensor.matmul(colp[:, l, kind, c], wmod[:, l, kc, o:o + P],
                                                    silu_c[:, kc, 2 * l:2 * l + 2], start=(kc == 0), stop=(kc == KC - 1))
            last.then_inc(cols_done, 1)
            pe.wait_ge(k.consts, 1)
            pe.wait_ge(bc_ready, 2)
            for r in range(ROWS):
                for kc in range(KC):
                    last = nc.tensor.transpose(rowp[:, r, kc * P:(kc + 1) * P], gate_bc[:, r, kc], k.ident[:])
            last.then_inc(rows_done, 1)


class Norm:

    def __init__(self, nc, k, ctx, name, layer, shift):
        self.nc, self.k, self.layer, self.shift = nc, k, layer, shift
        sb = lambda n, s, t=F32: ctx.enter_context(nc.sbuf_tensor(name + n, s, t))
        sem = lambda n: ctx.enter_context(nc.semaphore(name + n))
        self.bn = sb("bn", [P, GT, 6])
        self.mv = sb("mv", [P, GT, 2])
        self.ve = sb("ve", [P, GT])
        self.rstd = sb("rstd", [P, GT])
        self.z = sb("z", [P, GT, D])
        self.bn_done, self.stats, self.ve_done, self.rstd_done, self.z_done, self.zt_done = (
            sem(n) for n in ("bn_done", "stats", "ve_done", "rstd_done", "z_done", "zt_done"))

    def tile(self, t):
        return self.k.x[:, bass.ds(t, 1), :].rearrange("p o d -> p (o d)")

    def vector_stats(self, v, step, first):
        nc = self.nc
        for j in range(GT):
            last = nc.vector.bn_stats(self.bn[:, j], self.tile(first + j))
        last.then_inc(self.bn_done, 1)
        v.wait_ge(self.bn_done, START + step + 1)
        apart(self.k, v)
        for j in range(GT):
            last = nc.vector.bn_aggr(self.mv[:, j], self.bn[:, j])
        last.then_inc(self.stats, 1)

    def vector_z(self, v, step, first):
        nc = self.nc
        v.wait_ge(self.stats, START + step + 1)
        v.wait_ge(self.rstd_done, START + step + 1)
        v.wait_ge(self.zt_done, START + step * KC)
        for j in range(GT):
            last = nc.vector.tensor_scalar(self.z[:, j], self.tile(first + j), self.mv[:, j, 0:1],
                                           self.rstd[:, j:j + 1], ALU.subtract, ALU.mult)
        last.then_inc(self.z_done, 1)

    def gpsimd(self, pool, step):
        nc = self.nc
        pool.wait_ge(self.stats, START + step + 1)
        apart(self.k, pool)
        nc.gpsimd.tensor_scalar_add(self.ve[:], self.mv[:, :, 1], EPS).then_inc(self.ve_done, 1)
        pool.wait_ge(self.ve_done, START + step + 1)
        pool.wait_ge(self.z_done, START + step)
        nc.gpsimd.tensor_tensor(self.rstd[:], self.ve[:], self.k.mhalf[:, 0:GT], ALU.pow).then_inc(self.rstd_done, 1)

    def tensor(self, pe, step, c, zt):
        if c == 0:
            pe.wait_ge(self.z_done, START + step + 1)
        for j in range(GT):
            last = self.nc.tensor.transpose(zt[:, j * P:(j + 1) * P], self.z[:, j, c * P:(c + 1) * P], self.k.ident[:])
        last.then_inc(self.zt_done, 1)

    def scalar(self, act, step, c, zt, h, b):
        act.wait_ge(self.zt_done, START + step * KC + c + 1)
        m = self.k.colmod
        scale = m[:, self.layer, self.shift + 1, c, bass.ds(b, 1)]
        shift = m[:, self.layer, self.shift, c, bass.ds(b, 1)]
        apart(self.k, act)
        self.nc.scalar.activation(h, zt, ACT.Identity, bias=shift, scale=scale).then_inc(self.h_done, 1)


def attention(nc, k, d):
    with ExitStack() as ctx:
        sb = lambda n, s, t=F32: ctx.enter_context(nc.sbuf_tensor(n, s, t))
        sem = lambda n: ctx.enter_context(nc.semaphore(n))
        ps = lambda n, s: ctx.enter_context(nc.psum_tensor(n, s, F32))
        WQ, WK, WV, WO = range(4)
        RING = 2
        wh = sb("wh", [P, 4, KC, D], F32R)
        wl = sb("wl", [P, 4, KC, D], F32R)
        qh, ql = sb("qh", [P, KC, T], F32R), sb("ql", [P, KC, T], F32R)
        kh, kl = sb("kh", [P, KC, T], F32R), sb("kl", [P, KC, T], F32R)
        vh, vl = sb("vh", [P, TPB, D], F32R), sb("vl", [P, TPB, D], F32R)
        hh, hl = sb("hh", [P, 2, KC, GW], F32R), sb("hl", [P, 2, KC, GW], F32R)
        qkb = sb("qkb", [P, 2, KC, B])
        vb = sb("vb", [P, B, D])
        prob = sb("prob", [P, 2, T])
        pth, ptl = sb("pth", [P, RING, GW], F32R), sb("ptl", [P, RING, GW], F32R)
        mxc, mx, nmx = sb("mxc", [P, TPB, 4]), sb("mx", [P, TPB]), sb("nmx", [P, TPB])
        rsc, rsum, rinv = sb("rsc", [P, TPB, 4]), sb("rsum", [P, TPB]), sb("rinv", [P, TPB])
        cn = sb("cn", [P, D])
        cth, ctl = sb("cth", [P, KC, P], F32R), sb("ctl", [P, KC, P], F32R)
        y = sb("y1", [P, 2, D])
        bn, mv = sb("bn1", [P, TPB, 6]), sb("mv1", [P, TILES, 2])
        ve, rstd = sb("ve1", [P, TILES]), sb("rstd1", [P, TILES])
        z = prob[:, 1].rearrange("p (a t d) -> p a t d", a=2, t=GT)
        sc = ps("sc", [P, 4, 512])
        tp = ps("tp", [P, 2, 512])
        cx = ps("cx", [P, 512])
        pj = ps("pj", [P, 512])
        w_in = [sem(f"a_w_in{i}") for i in range(4)]
        names = ("w_hi w_lo shift_bc bias_ready bias_done hi_h lo_h qk_ready v_ready qk_hi qk_lo v_hi v_lo "
                 "s_ready dve1 nmax_done exp_done pt_ready pt_hi pt_lo pv_done cn_done ct_ready ct_hi "
                 "ct_lo pj_ready y_done bo_done bn_done stats ve_done rstd_done z_done zt_done")
        s = {n: sem("a_" + n) for n in names.split()}
        UNITS = [[(t, 0)] for t in range(15, 11, -1)] + [[(11 - i, 0), (3 - i, 3)] for i in range(4)] + [[(7, 0), (6, 2)], [(5, 0), (4, 2)]]
        ORDER = [t for u in UNITS for t, _ in u]
        BANK = {t: o for u in UNITS for t, o in u}
        UNIT = {t: i for i, u in enumerate(UNITS) for t, _ in u}
        FROM = [sum(len(x) for x in UNITS[:i]) for i in range(len(UNITS) + 1)]
        NU = len(UNITS)
        NCH = {t: (t + GT) // GT for t in range(TPB)}
        OFF = [sum(NCH[t] for t in ORDER[:i]) for i in range(TPB + 1)]
        CHB = OFF[-1]
        SEQ = [(i, ch) for i, t in enumerate(ORDER) for ch in range(NCH[t])]
        UNIT_OF = [UNIT[ORDER[i]] for i, _ in SEQ]
        STEP = [m - OFF[FROM[u]] for m, u in enumerate(UNIT_OF)]

        def chunks(u, half=None):
            if u >= NU:
                return range(0)
            a, z = OFF[FROM[u]], OFF[FROM[u + 1]]
            h = a + (z - a + 1) // 2
            return range(*((a, z), (a, h), (h, z))[0 if half is None else half + 1])

        def score_bank(m):
            return BANK[ORDER[SEQ[m][0]]] + SEQ[m][1]

        def freed(m):
            return max([j + 1 for j in range(chunks(UNIT_OF[m])[0]) if score_bank(j) == score_bank(m)], default=0)

        TURN = []
        for i in range(TPB):
            TURN.append(max(OFF[i + 1], TURN[i - 1] + 2 if i else 0))
            assert i == 0 or TURN[i - 1] <= OFF[i + 1] - 1, "the context before is transposed before the next one is done"
        TURNED = {m: i for i, m in enumerate(TURN)}
        PROJECTED = {m + 1: i for i, m in enumerate(TURN)}
        END = TURN[-1] + 2

        block = ctx.enter_context(nc.Block())
        raw = prob[:, 0].rearrange("p (w n) -> p w n", w=4)
        shift_bc = prob[:, 1, 0:KC * B * P].rearrange("p (c b n) -> p c b n", c=KC, b=B)

        def width(t, ch):
            return min(GW, (t + 1) * P - ch * GW)

        def row(a, b):
            return a[:, bass.ds(b, 1), :].rearrange("p o d -> p (o d)")

        @block.sync
        def _(sp):
            for i, w in enumerate((d["wq"], d["wk"], d["wv"], d["wo"])):
                sp.dma_start(raw[:, i].rearrange("p (c n) -> p c n", c=KC),
                             w.rearrange("(c p) n -> p c n", p=P)).then_inc(w_in[i], 16)

        @block.gpsimd
        def _(pool):
            begin(pool, s["bo_done"], s["ve_done"], s["rstd_done"], k.x1_done)
            for b in range(B):
                pool.wait_ge(s["stats"], START + b + 1)
                q = slice(b * TPB, (b + 1) * TPB)
                nc.gpsimd.tensor_scalar_add(ve[:, q], mv[:, q, 1], EPS).then_inc(s["ve_done"], 1)
                pool.wait_ge(s["ve_done"], START + b + 1)
                nc.gpsimd.tensor_tensor(rstd[:, q], ve[:, q], k.mhalf[:], ALU.pow).then_inc(s["rstd_done"], 1)
            with pool.Fori(0, B) as b:
                for g in range(GPB):
                    G = b * GPB + g
                    pool.wait_ge(s["z_done"], START + G + 1)
                    apart(k, pool)
                    for j in range(GT):
                        xt = row(k.x, G * GT + j)
                        last = nc.gpsimd.tensor_tensor(xt, xt, row(k.bo_gate, b), ALU.add)
                    last.then_inc(s["bo_done"], 1)
                pool.wait_ge(s["bo_done"], START + (b + 1) * GPB)
                for i, t in enumerate(ORDER):
                    pool.wait_ge(s["y_done"], START + b * TPB + i + 1)
                    xt = row(k.x, b * TPB + t)
                    apart(k, pool)
                    nc.gpsimd.tensor_tensor(xt, xt, y[:, i % 2], ALU.add).then_inc(k.x1_done, 1)

        @block.scalar
        def _(act):
            begin(act, s["w_hi"], s["hi_h"], s["qk_hi"], s["v_hi"], s["ct_hi"], s["exp_done"], s["pt_hi"])
            for i in range(4):
                act.wait_ge(w_in[i], 16)
                nc.scalar.copy(wh[:, i].rearrange("p c n -> p (c n)"), raw[:, i]).then_inc(s["w_hi"], 1)
            act.wait_ge(s["bias_done"], START + 1)

            def h_hi(b, g):
                G = b * GPB + g
                if g >= 2:
                    act.wait_ge(s["v_ready"], START + (G - 1) * 2)
                else:
                    act.wait_ge(s["v_ready"], START + b * GPB * 2)
                for c in range(KC):
                    act.wait_ge(s["zt_done"], START + G * KC + c + 1)
                    apart(k, act)
                    nc.scalar.activation(hh[:, g % 2, c], tp[:, c], ACT.Identity,
                                         scale=k.colmod[:, 0, 1, c, bass.ds(b, 1)]).then_inc(s["hi_h"], 1)

            def exp_of(b, m):
                i, ch = SEQ[m]
                t = ORDER[i]
                u, w = UNIT[t], width(t, ch)
                act.wait_ge(s["nmax_done"], START + b * TPB + i + 1)
                act.wait_ge(s["pt_ready"], START + b * CHB + (OFF[FROM[u - 1]] if u else 0))
                o = score_bank(m) * GW
                nc.scalar.activation(prob[:, u % 2, o:o + w], sc[:, score_bank(m), 0:w], ACT.Exp, bias=nmx[:, t:t + 1],
                                     scale=1.0 / 16, accum_out=rsc[:, t, ch:ch + 1]).then_inc(s["exp_done"], 1)

            with act.Fori(0, B) as b:
                h_hi(b, 0)
                for g in range(GPB):
                    G = b * GPB + g
                    if g + 1 < GPB:
                        h_hi(b, g + 1)
                    for i in range(4):
                        act.wait_ge(s["qk_ready"], START + G * 4 + i + 1)
                        act.wait_ge(s["s_ready"], START + b * CHB)
                        dst = (qh, kh)[i // 2][:, i % 2, g * GW:(g + 1) * GW]
                        apart(k, act)
                        nc.scalar.activation(dst, sc[:, i], ACT.Identity,
                                             bias=qkb[:, i // 2, i % 2, bass.ds(b, 1)]).then_inc(s["qk_hi"], 1)
                    for i in range(2):
                        act.wait_ge(s["pv_done"], START + b * CHB)
                        act.wait_ge(s["v_ready"], START + G * 2 + i + 1)
                        a = g * GT + 2 * i
                        nc.scalar.copy(vh[:, a:a + 2].rearrange("p t d -> p (t d)"), (cx, pj)[i][:]).then_inc(s["v_hi"], 1)

                def ct_hi(i):
                    act.wait_ge(s["ct_ready"], START + b * TPB + i + 1)
                    nc.scalar.copy(cth[:].rearrange("p c n -> p (c n)"), pj[:, 0:D]).then_inc(s["ct_hi"], 1)

                def pt_hi(m):
                    i, ch = SEQ[m]
                    w = width(ORDER[i], ch)
                    act.wait_ge(s["pt_ready"], START + b * CHB + m + 1)
                    act.wait_ge(s["pv_done"], START + b * CHB + max(m + 1 - RING, 0))
                    nc.scalar.copy(pth[:, m % RING, 0:w], tp[:, m % 2, 0:w]).then_inc(s["pt_hi"], 1)

                for m in chunks(0):
                    exp_of(b, m)
                pt_hi(0)
                for m in range(END):
                    if m + 1 < CHB:
                        pt_hi(m + 1)
                    if m in TURNED:
                        ct_hi(TURNED[m])
                    if m < CHB and STEP[m] in (1, 2):
                        for m2 in chunks(UNIT_OF[m] + 1, STEP[m] - 1):
                            exp_of(b, m2)

        @block.vector
        def _(v):
            begin(v, s["w_lo"], s["shift_bc"], s["bias_done"], s["dve1"], s["nmax_done"], s["ct_lo"], s["y_done"],
                  s["lo_h"], s["qk_lo"], s["v_lo"], s["pt_lo"], s["cn_done"], s["bn_done"], s["stats"], s["z_done"])
            DV = 5 * TPB
            for c in range(KC):
                for b in range(B):
                    last = nc.vector.tensor_copy(shift_bc[:, c, b], k.colmod[:, 0, 0, c, b:b + 1].to_broadcast([P, P]))
            last.then_inc(s["shift_bc"], 1)

            def statistics(b):
                v.wait_ge(k.x_in[b], 16 * GPB)
                for t in range(TPB):
                    last = nc.vector.bn_stats(bn[:, t], k.x[:, b * TPB + t])
                last.then_inc(s["bn_done"], 1)
                v.wait_ge(s["bn_done"], START + b + 1)
                for t in range(TPB):
                    last = nc.vector.bn_aggr(mv[:, b * TPB + t], bn[:, t])
                last.then_inc(s["stats"], 1)

            statistics(0)
            for i in range(4):
                v.wait_ge(s["w_hi"], START + i + 1)
                nc.vector.tensor_tensor(wl[:, i].rearrange("p c n -> p (c n)"), raw[:, i],
                                        wh[:, i].rearrange("p c n -> p (c n)"), ALU.subtract).then_inc(s["w_lo"], 1)
            v.wait_ge(s["stats"], START + 1)
            statistics(1)
            v.wait_ge(s["stats"], START + B)
            v.wait_ge(s["rstd_done"], START + B)
            v.wait_ge(s["bias_ready"], START + 1)
            for i, name in enumerate(("bq", "bk")):
                for c in range(KC):
                    nc.vector.tensor_scalar(qkb[:, i, c], sc[:, 0, (i * KC + c) * B:(i * KC + c + 1) * B], col(k, name, c), None, ALU.add)
            for b in range(B):
                last = nc.vector.tensor_tensor(vb[:, b], sc[:, 1, b * D:(b + 1) * D], k.rows[:, 0:D], ALU.add)
            last.then_inc(s["bias_done"], 1)

            with v.Fori(0, B) as b:
                chain = Counted(v, s["dve1"], b * DV)

                def h_lo(g):
                    for c in range(KC):
                        v.wait_ge(s["hi_h"], START + (b * GPB + g) * KC + c + 1)
                        nc.vector.scalar_tensor_tensor(out=hl[:, g % 2, c], in0=tp[:, c], scalar=k.colmod[:, 0, 1, c, bass.ds(b, 1)],
                                                       in1=hh[:, g % 2, c], op0=ALU.mult, op1=ALU.subtract).then_inc(s["lo_h"], 1)

                def normalise(g):
                    G = b * GPB + g
                    v.wait_ge(s["zt_done"], START + (b * GPB + max(g - 1, 0)) * KC)
                    for j in range(GT):
                        t = G * GT + j
                        last = nc.vector.tensor_scalar(z[:, g % 2, j], row(k.x, t), mv[:, bass.ds(t, 1), 0],
                                                       rstd[:, bass.ds(t, 1)], ALU.subtract, ALU.mult)
                    last.then_inc(s["z_done"], 1)

                normalise(0)
                normalise(1)
                h_lo(0)
                for g in range(GPB):
                    G = b * GPB + g
                    if g + 1 < GPB:
                        h_lo(g + 1)
                    for i in range(4):
                        v.wait_ge(s["qk_hi"], START + G * 4 + i + 1)
                        hi, lo = ((qh, ql), (kh, kl))[i // 2]
                        q = slice(g * GW, (g + 1) * GW)
                        nc.vector.scalar_tensor_tensor(out=lo[:, i % 2, q], in0=sc[:, i], scalar=qkb[:, i // 2, i % 2, bass.ds(b, 1)],
                                                       in1=hi[:, i % 2, q], op0=ALU.add, op1=ALU.subtract).then_inc(s["qk_lo"], 1)
                    for i in range(2):
                        v.wait_ge(s["v_hi"], START + G * 2 + i + 1)
                        a = g * GT + 2 * i
                        nc.vector.tensor_tensor(vl[:, a:a + 2].rearrange("p t d -> p (t d)"), (cx, pj)[i][:],
                                                vh[:, a:a + 2].rearrange("p t d -> p (t d)"), ALU.subtract).then_inc(s["v_lo"], 1)
                    if g + 2 < GPB:
                        normalise(g + 2)

                def maximum(m):
                    i, ch = SEQ[m]
                    t = ORDER[i]
                    v.wait_ge(s["s_ready"], START + b * CHB + m + 1)
                    if ch < NCH[t] - 1:
                        nc.vector.tensor_reduce(mxc[:, t, ch:ch + 1], sc[:, score_bank(m)], AX.X, ALU.max)
                        return
                    diag = sc[:, score_bank(m), (t % GT) * P:(t % GT + 1) * P]
                    chain.link(nc.vector.tensor_tensor(diag, diag, k.causal[:], ALU.add))
                    chain.link(nc.vector.tensor_reduce(mxc[:, t, ch:ch + 1], sc[:, score_bank(m), 0:width(t, ch)], AX.X, ALU.max))
                    chain.link(nc.vector.tensor_reduce(mx[:, t:t + 1], mxc[:, t, 0:NCH[t]], AX.X, ALU.max))
                    nc.vector.tensor_scalar(nmx[:, t:t + 1], mx[:, t:t + 1], -1.0 / 16, None, ALU.mult).then_inc(s["nmax_done"], 1)

                def ct_lo(i):
                    v.wait_ge(s["ct_hi"], START + b * TPB + i + 1)
                    nc.vector.tensor_tensor(ctl[:].rearrange("p c n -> p (c n)"), pj[:, 0:D],
                                            cth[:].rearrange("p c n -> p (c n)"), ALU.subtract).then_inc(s["ct_lo"], 1)

                def gated(i):
                    v.wait_ge(s["pj_ready"], START + b * TPB + i + 1)
                    v.wait_ge(k.x1_done, START + b * TPB + max(i - 1, 0))
                    nc.vector.tensor_tensor(y[:, i % 2], pj[:, 0:D], row(k.gate, b), ALU.mult).then_inc(s["y_done"], 1)

                def pt_lo(m):
                    i, ch = SEQ[m]
                    w = width(ORDER[i], ch)
                    v.wait_ge(s["pt_hi"], START + b * CHB + m + 1)
                    nc.vector.tensor_tensor(ptl[:, m % RING, 0:w], tp[:, m % 2, 0:w], pth[:, m % RING, 0:w],
                                            ALU.subtract).then_inc(s["pt_lo"], 1)

                for m in chunks(0):
                    maximum(m)
                pt_lo(0)
                for m in range(END):
                    if m < CHB and STEP[m] in (0, 1):
                        for m2 in chunks(UNIT_OF[m] + 1, STEP[m]):
                            maximum(m2)
                    if m + 1 < CHB:
                        pt_lo(m + 1)
                    if m in PROJECTED:
                        gated(PROJECTED[m])
                    if m in TURNED:
                        ct_lo(TURNED[m])
                    if m + 1 in OFF[1:]:
                        i = OFF.index(m + 1) - 1
                        t = ORDER[i]
                        v.wait_ge(s["exp_done"], START + b * CHB + OFF[i + 1])
                        chain.link(nc.vector.tensor_reduce(rsum[:, t:t + 1], rsc[:, t, 0:NCH[t]], AX.X, ALU.add))
                        chain.link(nc.vector.reciprocal(rinv[:, t:t + 1], rsum[:, t:t + 1]))
                        v.wait_ge(s["pv_done"], START + b * CHB + OFF[i + 1])
                        v.wait_ge(s["ct_ready"], START + b * TPB + i)
                        nc.vector.scalar_tensor_tensor(out=cn[:], in0=cx[:, 0:D], scalar=rinv[:, t:t + 1], in1=row(vb, b),
                                                       op0=ALU.mult, op1=ALU.add).then_inc(s["cn_done"], 1)
                assert chain.n == DV

        @block.tensor
        def _(pe):
            begin(pe, s["bias_ready"], s["s_ready"], s["ct_ready"], s["pj_ready"], s["pt_ready"], s["pv_done"],
                  s["qk_ready"], s["v_ready"], s["zt_done"])
            pe.wait_ge(s["shift_bc"], START + 1)
            for w in w_in[0:3]:
                pe.wait_ge(w, 16)
            for i in (WQ, WK):
                for c in range(KC):
                    for kc in range(KC):
                        o = (i * KC + c) * B
                        nc.tensor.matmul(sc[:, 0, o:o + B], raw[:, i, kc * D + c * P:kc * D + (c + 1) * P], k.colmod[:, 0, 0, kc],
                                         start=(kc == 0), stop=(kc == KC - 1))
            for b in range(B):
                for kc in range(KC):
                    last = nc.tensor.matmul(sc[:, 1, b * D:(b + 1) * D], shift_bc[:, kc, b], raw[:, WV, kc * D:(kc + 1) * D],
                                            start=(kc == 0), stop=(kc == KC - 1))
            last.then_inc(s["bias_ready"], 1)
            pe.wait_ge(s["bias_done"], START + 1)
            with pe.Fori(0, B) as b:
                def zt(g):
                    G = b * GPB + g
                    pe.wait_ge(s["lo_h"], START + G * KC)
                    if g == 0:
                        pe.wait_ge(s["pt_lo"], START + b * CHB)
                    for c in range(KC):
                        if c == 0:
                            pe.wait_ge(s["z_done"], START + G + 1)
                        for j in range(GT):
                            last = nc.tensor.transpose(tp[:, c, j * P:(j + 1) * P], z[:, g % 2, j, c * P:(c + 1) * P], k.ident[:])
                        last.then_inc(s["zt_done"], 1)

                zt(0)
                for g in range(GPB):
                    G = b * GPB + g
                    if g + 1 < GPB:
                        zt(g + 1)
                    pe.wait_ge(s["lo_h"], START + (G + 1) * KC)
                    if g == 0:
                        pe.wait_ge(s["exp_done"], START + b * CHB)
                        pe.wait_ge(s["w_lo"], START + 4)
                    hg, lg = hh[:, g % 2], hl[:, g % 2]
                    for i in range(4):
                        c = i % 2
                        pe.wait_ge(s["qk_lo"], START + G * 4 - 3 + i if g else START + b * GPB * 4)
                        for kc in range(KC):
                            m = slice(c * P, (c + 1) * P)
                            w = (WQ, WK)[i // 2]
                            last = three(nc.tensor, sc[:, i], wh[:, w, kc, m], wl[:, w, kc, m], hg[:, kc], lg[:, kc],
                                         kc == 0, kc == KC - 1)
                        last.then_inc(s["qk_ready"], 1)
                    if g == 0:
                        pe.wait_ge(s["y_done"], START + b * TPB)
                    for i in range(2):
                        pe.wait_ge(s["v_lo"], START + (G - 1) * 2 + i + 1 if g else START + b * GPB * 2)
                        bank = (cx, pj)[i]
                        for j in range(2):
                            q = slice((2 * i + j) * P, (2 * i + j + 1) * P)
                            for kc in range(KC):
                                last = three(nc.tensor, bank[:, j * D:(j + 1) * D], hg[:, kc, q], lg[:, kc, q],
                                             wh[:, WV, kc], wl[:, WV, kc], kc == 0, kc == KC - 1)
                        last.then_inc(s["v_ready"], 1)
                pe.wait_ge(s["qk_lo"], START + (b + 1) * GPB * 4)

                def scores(m):
                    i, ch = SEQ[m]
                    t = ORDER[i]
                    w = width(t, ch)
                    pe.wait_ge(s["exp_done"], START + b * CHB + freed(m))
                    for kc in range(KC):
                        q = slice(t * P, (t + 1) * P)
                        kk = slice(ch * GW, ch * GW + w)
                        last = three(nc.tensor, sc[:, score_bank(m), 0:w], qh[:, kc, q], ql[:, kc, q], kh[:, kc, kk], kl[:, kc, kk],
                                     kc == 0, kc == KC - 1)
                    last.then_inc(s["s_ready"], 1)

                def ct(i):
                    pe.wait_ge(s["cn_done"], START + b * TPB + i + 1)
                    pe.wait_ge(s["y_done"], START + b * TPB + i)
                    if i == 0:
                        pe.wait_ge(s["v_lo"], START + (b + 1) * GPB * 2)
                    for c in range(KC):
                        last = nc.tensor.transpose(pj[:, c * P:(c + 1) * P], cn[:, c * P:(c + 1) * P], k.ident[:])
                    last.then_inc(s["ct_ready"], 1)

                def project(i):
                    pe.wait_ge(s["ct_lo"], START + b * TPB + i + 1)
                    for kc in range(KC):
                        last = three(nc.tensor, pj[:, 0:D], cth[:, kc], ctl[:, kc], wh[:, WO, kc], wl[:, WO, kc],
                                     kc == 0, kc == KC - 1)
                    last.then_inc(s["pj_ready"], 1)

                def turn(m):
                    i, ch = SEQ[m]
                    pe.wait_ge(s["exp_done"], START + b * CHB + m + 1)
                    pe.wait_ge(s["pt_lo"], START + b * CHB + max(m - 1, 0))
                    for j in range(width(ORDER[i], ch) // P):
                        a = score_bank(m) * GW + j * P
                        last = nc.tensor.transpose(tp[:, m % 2, j * P:(j + 1) * P], prob[:, UNIT_OF[m] % 2, a:a + P], k.ident[:])
                    last.then_inc(s["pt_ready"], 1)

                def values(m):
                    i, ch = SEQ[m]
                    t = ORDER[i]
                    pe.wait_ge(s["pt_lo"], START + b * CHB + m + 1)
                    if ch == 0:
                        pe.wait_ge(s["cn_done"], START + b * TPB + i)
                        if i == 0:
                            pe.wait_ge(s["v_lo"], START + (b + 1) * GPB * 2)
                    nj = width(t, ch) // P
                    for j in range(nj):
                        a = ch * GT + j
                        q = slice(j * P, (j + 1) * P)
                        last = three(nc.tensor, cx[:, 0:D], pth[:, m % RING, q], ptl[:, m % RING, q], vh[:, a], vl[:, a],
                                     ch == 0 and j == 0, ch == NCH[t] - 1 and j == nj - 1)
                    last.then_inc(s["pv_done"], 1)

                for m in chunks(0):
                    scores(m)
                turn(0)
                for m in range(END):
                    if m < CHB and STEP[m] in (0, 1):
                        for m2 in chunks(UNIT_OF[m] + 1, STEP[m]):
                            scores(m2)
                    if m + 1 < CHB:
                        turn(m + 1)
                    if m < CHB:
                        values(m)
                    if m in PROJECTED:
                        project(PROJECTED[m])
                    if m in TURNED:
                        ct(TURNED[m])


def experts(nc, k, d):
    PAIR = 2 * F
    STEPS = E // 2 + 1
    GS = GT * STEPS
    HID = (E + 1) * F
    HC = PAIR // P
    DCH = -(-HID // P)
    TAIL = HID - (DCH - 1) * P
    LAST = GROUPS - 1
    with ExitStack() as ctx:
        sb = lambda n, s, t=F32: ctx.enter_context(nc.sbuf_tensor(n, s, t))
        sem = lambda n: ctx.enter_context(nc.semaphore(n))
        ps = lambda n, s: ctx.enter_context(nc.psum_tensor(n, s, F32))
        raw = [sb("raw_gate", [P, KC, HID]), sb("raw_up", [P, KC, HID]), sb("raw_down", [P, DCH, D])]
        high = [sb("gate_h", [P, KC, HID], F32R), sb("up_h", [P, KC, HID], F32R), sb("down_h", [P, DCH, D], F32R)]
        low = [sb("gate_l", [P, KC, HID], F32R), sb("up_l", [P, KC, HID], F32R), sb("down_l", [P, DCH, D], F32R)]
        router = sb("router", [P, KC, E])
        hf = sb("hf2", [P, KC, GW])
        hh, hl = sb("hh2", [P, GT, KC, P], F32R), sb("hl2", [P, GT, KC, P], F32R)
        act_g = sb("act_g", [P, 2, PAIR])
        hid = sb("hid", [P, 2, PAIR])
        hth, htl = sb("hth", [P, 2, PAIR], F32R), sb("htl", [P, 2, PAIR], F32R)
        y = sb("y2", [P, 2, D])
        iota = sb("iota", [P, GT, E])
        sig, sel, pick, second = (sb(n, [P, GT, E]) for n in ("sig", "sel", "pick", "second"))
        best = sb("best", [P, GT, 8])
        place = sb("place", [P, GT, 8], U32)
        placef = sb("placef", [P, GT, 2])
        total = sb("total", [P, GT])
        w = sb("w", [P, GT, E])
        norm = Norm(nc, k, ctx, "n2", 0, 2)
        norm.h_done = sem("n2h_done")
        gp = ps("gp", [P, 2, 512])
        up = ps("up", [P, 2, 512])
        tp = ps("tp2", [P, 2, 512])
        dp = ps("dp", [P, 512])
        mp = ps("mp", [P, 512])
        w_in = [sem(f"m_w_in{i}") for i in range(3)]
        names = ("w_hi w_lo r_in iota_done hi_h lo_h g_ready u_ready silu_done hid_done ht_ready ht_hi ht_lo "
                 "d_done y_done logits sig_done route dve2")
        s = {n: sem("m_" + n) for n in names.split()}
        block = ctx.enter_context(nc.Block())
        ROUTE = 10
        pieces = [(slice(0, P), 0, slice(0, KC)), (slice(0, P), 1, slice(0, KC)), (slice(0, P), 2, slice(0, DCH - 1)),
                  (slice(0, TAIL), 2, slice(DCH - 1, DCH))]

        def hidden(n):
            return PAIR if n % STEPS < STEPS - 1 else F

        @block.sync
        def _(sp):
            sp.dma_start(router[:], d["router"].rearrange("(c p) e -> p c e", p=P)).then_inc(s["r_in"], 16)
            for i, (we, ws) in enumerate(((d["wg"], d["wg_s"]), (d["wu"], d["wu_s"]))):
                for c in range(KC):
                    sp.dma_start(raw[i][:, c, 0:E * F].rearrange("p (e f) -> p e f", e=E),
                                 we[:, c * P:(c + 1) * P, :].rearrange("e p f -> p e f")).then_inc(w_in[i], 16)
                    sp.dma_start(raw[i][:, c, E * F:HID], ws[c * P:(c + 1) * P, :]).then_inc(w_in[i], 16)
            n = E * F // P
            sp.dma_start(raw[2][:, 0:n, :], d["wd"].rearrange("e f d -> (e f) d").rearrange("(c p) d -> p c d", p=P)).then_inc(w_in[2], 16)
            sp.dma_start(raw[2][:, n, :], d["wd_s"][0:P, :]).then_inc(w_in[2], 16)
            sp.dma_start(raw[2][0:TAIL, n + 1, :], d["wd_s"][P:F, :]).then_inc(w_in[2], 16)

        def loaded(eng, i):
            eng.wait_ge(w_in[pieces[i][1]], (64, 64, 48)[pieces[i][1]])

        def groups(eng, body):
            body(0, True)
            with eng.Fori(1, LAST) as G:
                body(G, False)
            body(LAST, False)

        @block.gpsimd
        def _(pool):
            begin(pool, s["iota_done"], s["hi_h"], norm.ve_done, norm.rstd_done, k.x2_done)
            nc.gpsimd.iota(place[:], pattern=[[0, GT], [1, E]], base=0, channel_multiplier=0).then_inc(s["iota_done"], 1)
            pool.wait_ge(s["iota_done"], START + 1)
            nc.gpsimd.tensor_copy(iota[:], place[:]).then_inc(s["iota_done"], 1)

            def split_hi(G, j):
                pool.wait_ge(norm.h_done, START + (G + 1) * KC)
                if not (isinstance(G, int) and G == 0):
                    pool.wait_ge(s["u_ready"], START + (G - 1) * GS + (j + 1) * STEPS)
                apart(k, pool)
                nc.gpsimd.tensor_copy(hh[:, j], hf[:, :, j * P:(j + 1) * P]).then_inc(s["hi_h"], 1)

            def add(G, j):
                pool.wait_ge(s["y_done"], START + G * GT + j + 1)
                xt = norm.tile(G * GT + j)
                apart(k, pool)
                nc.gpsimd.tensor_tensor(xt, xt, y[:, j % 2], ALU.add).then_inc(k.x2_done, 1)

            norm.gpsimd(pool, 0)
            for j in range(GT):
                split_hi(0, j)

            def body(G, first):
                last = isinstance(G, int) and G == LAST
                if not first:
                    split_hi(G, GT - 1)
                    add(G - 1, GT - 1)
                if not last:
                    norm.gpsimd(pool, G + 1)
                add(G, 0)
                if not last:
                    split_hi(G + 1, 0)
                    split_hi(G + 1, 1)
                add(G, 1)
                if not last:
                    split_hi(G + 1, 2)
                add(G, 2)

            groups(pool, body)
            add(LAST, GT - 1)

        @block.scalar
        def _(act):
            begin(act, s["w_hi"], s["sig_done"], s["silu_done"], s["ht_hi"], norm.h_done)
            for i, (p, t, c) in enumerate(pieces):
                loaded(act, i)
                nc.scalar.copy(high[t][p, c], raw[t][p, c]).then_inc(s["w_hi"], 1)

            def h_of(G, c):
                if isinstance(G, int) and G == 0:
                    norm.scalar(act, G, c, mp[:], hf[:, c], 0)
                else:
                    act.wait_ge(s["lo_h"], START + G * GT)
                    act.wait_ge(s["logits"], START + G)
                    norm.scalar(act, G, c, mp[:], hf[:, c], G // GPB)

            def sigmoid(G):
                act.wait_ge(s["logits"], START + G + 1)
                if not (isinstance(G, int) and G == 0):
                    act.wait_ge(s["route"], START + G * ROUTE)
                nc.scalar.activation(sig[:].rearrange("p t e -> p (t e)"), mp[:, 0:GT * E], ACT.Sigmoid).then_inc(s["sig_done"], 1)

            def silu(G, n):
                S = G * GS + n
                act.wait_ge(s["g_ready"], START + S + 1)
                if not (isinstance(G, int) and G == 0 and n < 2):
                    act.wait_ge(s["hid_done"], START + S - 1)
                nc.scalar.activation(act_g[:, n % 2, 0:hidden(n)], gp[:, n % 2, 0:hidden(n)], ACT.Silu).then_inc(s["silu_done"], 1)

            def ht_hi(G, n):
                S = G * GS + n
                act.wait_ge(s["ht_ready"], START + S + 1)
                if not (isinstance(G, int) and G == 0 and n < 2):
                    act.wait_ge(s["d_done"], START + S - 1)
                wd = PAIR if n % STEPS < STEPS - 1 else 2 * P
                nc.scalar.copy(hth[:, n % 2, 0:wd], tp[:, n % 2, 0:wd]).then_inc(s["ht_hi"], 1)

            h_of(0, 0)
            h_of(0, 1)
            sigmoid(0)

            def body(G, first):
                last = isinstance(G, int) and G == LAST
                for n in range(GS):
                    silu(G, n)
                    if n > 0:
                        ht_hi(G, n - 1)
                    elif not first:
                        ht_hi(G - 1, GS - 1)
                    if not last:
                        if n == 7:
                            h_of(G + 1, 0)
                        if n == 9:
                            h_of(G + 1, 1)
                        if n == 13:
                            sigmoid(G + 1)

            groups(act, body)
            ht_hi(LAST, GS - 1)

        @block.vector
        def _(v):
            begin(v, s["lo_h"], s["route"], s["dve2"], s["hid_done"], s["ht_lo"], s["y_done"], s["w_lo"], norm.bn_done,
                  norm.stats, norm.z_done)
            def split_lo(G, j):
                v.wait_ge(s["hi_h"], START + G * GT + j + 1)
                nc.vector.tensor_tensor(hl[:, j], hf[:, :, j * P:(j + 1) * P], hh[:, j], ALU.subtract).then_inc(s["lo_h"], 1)

            def route(G):
                c = Counted(v, s["route"], G * ROUTE)
                v.wait_ge(s["sig_done"], START + G + 1)
                c.link(nc.vector.tensor_tensor(sel[:], sig[:], k.rows[:, 2 * D:2 * D + E].unsqueeze(1).to_broadcast([P, GT, E]), ALU.add), k)
                for j in range(GT):
                    last = nc.vector.max(best[:, j], sel[:, j])
                c.link(last, k)
                for j in range(GT):
                    last = nc.vector.max_index(place[:, j], best[:, j], sel[:, j])
                c.link(last)
                c.link(nc.vector.tensor_copy(placef[:], place[:, :, 0:2]))
                for i, o in enumerate((pick, second)):
                    last = nc.vector.tensor_tensor(o[:], iota[:], placef[:, :, i:i + 1].to_broadcast([P, GT, E]), ALU.is_equal)
                c.link(last)
                c.link(nc.vector.tensor_tensor(pick[:], pick[:], second[:], ALU.add))
                c.link(nc.vector.tensor_tensor(pick[:], pick[:], sig[:], ALU.mult))
                c.link(nc.vector.tensor_reduce(total[:], pick[:], AX.X, ALU.add))
                c.link(nc.vector.tensor_scalar_add(total[:], total[:], 1e-20))
                nc.vector.reciprocal(total[:], total[:]).then_inc(s["dve2"], 1)
                v.wait_ge(s["dve2"], START + G + 1)
                c.link(nc.vector.tensor_tensor(w[:], pick[:], total[:].unsqueeze(2).to_broadcast([P, GT, E]), ALU.mult))
                assert c.n == ROUTE

            def weigh(G, n):
                S = G * GS + n
                j, p = divmod(n, STEPS)
                v.wait_ge(s["silu_done"], START + S + 1)
                v.wait_ge(s["u_ready"], START + S + 1)
                if not (isinstance(G, int) and G == 0 and n < 2):
                    v.wait_ge(s["ht_ready"], START + S - 1)
                if p < STEPS - 1:
                    for i in range(2):
                        f = slice(i * F, (i + 1) * F)
                        last = nc.vector.scalar_tensor_tensor(out=hid[:, n % 2, f], in0=act_g[:, n % 2, f],
                                                              scalar=w[:, j, 2 * p + i:2 * p + i + 1],
                                                              in1=up[:, n % 2, f], op0=ALU.mult, op1=ALU.mult)
                else:
                    last = nc.vector.tensor_tensor(hid[:, n % 2, 0:F], act_g[:, n % 2, 0:F], up[:, n % 2, 0:F], ALU.mult)
                last.then_inc(s["hid_done"], 1)

            def ht_lo(G, n):
                v.wait_ge(s["ht_hi"], START + G * GS + n + 1)
                wd = PAIR if n % STEPS < STEPS - 1 else 2 * P
                nc.vector.tensor_tensor(htl[:, n % 2, 0:wd], tp[:, n % 2, 0:wd], hth[:, n % 2, 0:wd], ALU.subtract).then_inc(s["ht_lo"], 1)

            def gated(G, j):
                v.wait_ge(s["d_done"], START + G * GS + (j + 1) * STEPS)
                if not (isinstance(G, int) and G == 0 and j < 2):
                    v.wait_ge(k.x2_done, START + G * GT + j - 1)
                b = G // GPB
                nc.vector.tensor_tensor(y[:, j % 2], dp[:, 0:D], k.gate[:, bass.ds(b + 2, 1), :].rearrange("p o d -> p (o d)"),
                                        ALU.mult).then_inc(s["y_done"], 1)

            norm.vector_stats(v, 0, 0)
            norm.vector_z(v, 0, 0)
            for i, (p, t, c) in enumerate(pieces):
                v.wait_ge(s["w_hi"], START + i + 1)
                nc.vector.tensor_tensor(low[t][p, c], raw[t][p, c], high[t][p, c], ALU.subtract).then_inc(s["w_lo"], 1)
            for j in range(GT):
                split_lo(0, j)
            v.wait_ge(s["iota_done"], START + 2)
            route(0)

            def body(G, first):
                last = isinstance(G, int) and G == LAST
                for n in range(GS):
                    weigh(G, n)
                    if n > 0:
                        ht_lo(G, n - 1)
                    elif not first:
                        ht_lo(G - 1, GS - 1)
                    if n == 1 and not first:
                        gated(G - 1, GT - 1)
                        split_lo(G, GT - 1)
                    if n > STEPS and n % STEPS == 1:
                        gated(G, n // STEPS - 1)
                    if not last:
                        if n == 2:
                            norm.vector_stats(v, G + 1, (G + 1) * GT)
                        if n == 5:
                            norm.vector_z(v, G + 1, (G + 1) * GT)
                        if n in (11, 12, 16):
                            split_lo(G + 1, (11, 12, 16).index(n))
                        if n == GS - 1:
                            route(G + 1)

            groups(v, body)
            ht_lo(LAST, GS - 1)
            gated(LAST, GT - 1)

        @block.tensor
        def _(pe):
            begin(pe, s["logits"], s["ht_ready"], s["d_done"], s["g_ready"], s["u_ready"], norm.zt_done)
            def zt(G, c):
                if not (isinstance(G, int) and G == 0):
                    pe.wait_ge(s["sig_done"], START + G)
                if c == 1:
                    pe.wait_ge(norm.h_done, START + G * KC + 1)
                norm.tensor(pe, G, c, mp)

            def logits(G):
                pe.wait_ge(norm.h_done, START + (G + 1) * KC)
                for j in range(GT):
                    for kc in range(KC):
                        last = nc.tensor.matmul(mp[:, j * E:(j + 1) * E], hf[:, kc, j * P:(j + 1) * P], router[:, kc],
                                                start=(kc == 0), stop=(kc == KC - 1))
                last.then_inc(s["logits"], 1)

            def gate_up(G, n):
                S = G * GS + n
                j, p = divmod(n, STEPS)
                if p == 0:
                    pe.wait_ge(s["lo_h"], START + G * GT + j + 1)
                if not (isinstance(G, int) and G == 0 and n < 2):
                    pe.wait_ge(s["hid_done"], START + S - 1)
                f = slice(p * PAIR, p * PAIR + hidden(n))
                for i, (bank, done) in enumerate(((gp, s["g_ready"]), (up, s["u_ready"]))):
                    for kc in range(KC):
                        last = three(nc.tensor, bank[:, n % 2, 0:hidden(n)], hh[:, j, kc], hl[:, j, kc],
                                     high[i][:, kc, f], low[i][:, kc, f], kc == 0, kc == KC - 1)
                    last.then_inc(done, 1)

            def turn(G, n):
                S = G * GS + n
                pe.wait_ge(s["hid_done"], START + S + 1)
                if not (isinstance(G, int) and G == 0 and n < 2):
                    pe.wait_ge(s["ht_lo"], START + S - 1)
                for c in range(-(-hidden(n) // P)):
                    m = min(P, hidden(n) - c * P)
                    last = nc.tensor.transpose(tp[0:m, n % 2, c * P:(c + 1) * P], hid[:, n % 2, c * P:c * P + m], k.ident[:])
                last.then_inc(s["ht_ready"], 1)

            def down(G, n):
                S = G * GS + n
                j, p = divmod(n, STEPS)
                pe.wait_ge(s["ht_lo"], START + S + 1)
                if p == 0:
                    pe.wait_ge(s["y_done"], START + G * GT + j)
                nch = -(-hidden(n) // P)
                for c in range(nch):
                    m = min(P, hidden(n) - c * P)
                    q = slice(c * P, (c + 1) * P)
                    last = three(nc.tensor, dp[:, 0:D], hth[0:m, n % 2, q], htl[0:m, n % 2, q],
                                 high[2][0:m, p * HC + c], low[2][0:m, p * HC + c],
                                 p == 0 and c == 0, p == STEPS - 1 and c == nch - 1)
                last.then_inc(s["d_done"], 1)

            zt(0, 0)
            zt(0, 1)
            pe.wait_ge(s["r_in"], 16)
            logits(0)
            pe.wait_ge(s["w_lo"], START + len(pieces))

            def body(G, first):
                last = isinstance(G, int) and G == LAST
                for n in range(GS):
                    gate_up(G, n)
                    if n >= 1:
                        turn(G, n - 1)
                    elif not first:
                        turn(G - 1, GS - 1)
                    if n >= 2:
                        down(G, n - 2)
                    elif not first:
                        down(G - 1, GS - 2 + n)
                    if not last:
                        if n == 7:
                            zt(G + 1, 0)
                        if n == 9:
                            zt(G + 1, 1)
                        if n == 12:
                            logits(G + 1)

            groups(pe, body)
            turn(LAST, GS - 1)
            down(LAST, GS - 2)
            down(LAST, GS - 1)


def near(G):
    if isinstance(G, int):
        return G > 0, G + 1 < GROUPS, G + 2 < GROUPS
    return True, True, True


def through_groups(eng, body):
    body(0, *near(0))
    with eng.Fori(1, GROUPS - 2) as G:
        body(G, *near(G))
    for G in (GROUPS - 2, GROUPS - 1):
        body(G, *near(G))


def first_column(G):
    return (G % GPB) * GW


class Shifted:

    def __init__(self, nc, k, ctx, name, mixes):
        self.nc, self.k, self.mixes = nc, k, mixes
        sb = lambda n, s, t=F32: ctx.enter_context(nc.sbuf_tensor(n + name, s, t))
        n = len(mixes)
        self.one_minus = sb("one_minus", [P, KC, n])
        self.scaled = sb("scaled", [P, n, 2, KC, D])
        self.wh, self.wl = sb("wmh", [P, n, 2, KC, D], F32R), sb("wml", [P, n, 2, KC, D], F32R)
        self.hh, self.hl = sb("hh", [P, KC, T + 1], F32R), sb("hl", [P, KC, T + 1], F32R)
        self.h = sb("h", [P, KC, GW])
        self.zero = sb("zero", [P, KC])
        sem = lambda n: ctx.enter_context(nc.semaphore(n + name))
        self.om_done, self.scaled_done, self.w_hi, self.w_lo, self.zeroed, self.hi_h, self.lo_h = (
            sem(n) for n in ("om_done", "scaled_done", "w_hi", "w_lo", "zeroed", "hi_h", "lo_h"))

    def gpsimd(self, pool, raw, w_in):
        nc = self.nc
        nc.gpsimd.memset(self.zero[:], 0.0).then_inc(self.zeroed, 1)
        for i, mix in enumerate(self.mixes):
            last = nc.gpsimd.tensor_scalar(self.one_minus[:, :, i:i + 1], self.k.cols[:, :, COL[mix]:COL[mix] + 1], -1.0, 1.0,
                                           ALU.mult, ALU.add)
        last.then_inc(self.om_done, 1)
        pool.wait_ge(self.om_done, START + 1)
        for i, mix in enumerate(self.mixes):
            pool.wait_ge(w_in[i], 16)
            for c in range(KC):
                nc.gpsimd.tensor_scalar_mul(self.scaled[:, i, 0, c], raw[:, i, c], col(self.k, mix, c))
                last = nc.gpsimd.tensor_scalar_mul(self.scaled[:, i, 1, c], raw[:, i, c], self.one_minus[:, c, i:i + 1])
            last.then_inc(self.scaled_done, 1)

    def scalar_weights(self, act, i):
        act.wait_ge(self.scaled_done, START + i + 1)
        self.nc.scalar.copy(self.wh[:, i], self.scaled[:, i]).then_inc(self.w_hi, 1)

    def scalar_zero(self, act):
        act.wait_ge(self.zeroed, START + 1)
        self.nc.scalar.copy(self.hh[:, :, 0], self.zero[:])
        self.nc.scalar.copy(self.hl[:, :, 0], self.zero[:]).then_inc(self.zeroed, 1)

    def vector_weights(self, v, i):
        v.wait_ge(self.w_hi, START + i + 1)
        self.nc.vector.tensor_tensor(self.wl[:, i], self.scaled[:, i], self.wh[:, i], ALU.subtract).then_inc(self.w_lo, 1)

    def modulation(self, norm, G, c):
        m = self.k.colmod
        if isinstance(G, int):
            b = G // GPB
            return [m[:, norm.layer, norm.shift + i, c, b:b + 1] for i in range(2)]
        return [m[:, norm.layer, norm.shift + i, c, bass.ds(G // GPB, 1)] for i in range(2)]

    def place(self, a, c, G, ahead):
        return a[:, c, bass.ds(first_column(G) + ahead, GW)]

    def scalar_h(self, act, norm, G, c, zt):
        act.wait_ge(norm.zt_done, START + G * KC + c + 1)
        act.wait_ge(self.lo_h, START + G * KC)
        shift, scale = self.modulation(norm, G, c)
        apart(self.k, act)
        self.nc.scalar.activation(self.h[:, c], zt, ACT.Identity, bias=shift, scale=scale)
        self.nc.scalar.activation(self.place(self.hh, c, G, 1), zt, ACT.Identity, bias=shift, scale=scale).then_inc(self.hi_h, 1)

    def vector_h(self, v, G, c):
        v.wait_ge(self.hi_h, START + G * KC + c + 1)
        apart(self.k, v)
        self.nc.vector.tensor_tensor(self.place(self.hl, c, G, 1), self.h[:, c], self.place(self.hh, c, G, 1),
                                     ALU.subtract).then_inc(self.lo_h, 1)

    def tensor(self, out, i, m, G):
        for kc in range(KC):
            for which, ahead in ((0, 1), (1, 0)):
                last = three(self.nc.tensor, out, self.wh[:, i, which, kc, m], self.wl[:, i, which, kc, m],
                             self.place(self.hh, kc, G, ahead), self.place(self.hl, kc, G, ahead),
                             kc == 0 and which == 0, kc == KC - 1 and which == 1)
        return last


def time_mixing(nc, k, d):
    with ExitStack() as ctx:
        sb = lambda n, s, t=F32: ctx.enter_context(nc.sbuf_tensor(n, s, t))
        sem = lambda n: ctx.enter_context(nc.semaphore(n))
        ps = lambda n, s: ctx.enter_context(nc.psum_tensor(n, s, F32))
        K_, V_, R_ = range(3)
        raw = sb("raw3", [P, 4, KC, D])
        mix = Shifted(nc, k, ctx, "3", ("mix_k", "mix_v", "mix_r"))
        wo = sb("wo3", [P, KC, D])
        wog = sb("wog3", [P, B, KC, D])
        woh, wol = sb("woh3", [P, B, KC, D], F32R), sb("wol3", [P, B, KC, D], F32R)
        ones = sb("ones3", [P, P])
        lnb = sb("lnb3", [P, KC, P])
        bias = sb("bias3", [P, B, D])
        ks = sb("ks3", [P, KC, GW])
        kv = sb("kv3", [P, GW])
        st = sb("st3", [P, GW])
        states = sb("states3", [P, KC, GROUPS + B])
        dec = sb("dec3", [P, KC])
        fo = sb("fo3", [P, GW])
        o = sb("o3", [P, KC, GW])
        oh, ol = sb("oh3", [P, KC, GW], F32R), sb("ol3", [P, KC, GW], F32R)
        obn, omv, ove, orstd = sb("obn3", [P, GT, 6]), sb("omv3", [P, GT, 2]), sb("ove3", [P, GT]), sb("orstd3", [P, GT])
        norm = Norm(nc, k, ctx, "n3", 1, 0)
        kvr = ps("kvr", [P, 6, 512])
        ring = ps("ring3", [P, 2, 512])
        w_in = [sem(f"t_w_in{i}") for i in range(4)]
        names = ("wog_done centred ones_done sums_ready wo_hi wo_lo dec_done kvr_ready ks_done kv_done o_done "
                 "hi_o lo_o ot_ready obn_done ostats ove_done orstd_done out_ready bias_added dve3 init3")
        s = {n: sem("t_" + n) for n in names.split()}
        block = ctx.enter_context(nc.Block())
        row = lambda a, i: a[:, bass.ds(i, 1), :].rearrange("p o d -> p (o d)")
        slot = lambda c, G, ahead: states[:, c, bass.ds(G + G // GPB + ahead, 1)]

        @block.sync
        def _(sp):
            for i, w in enumerate((d["w3k"], d["w3v"], d["w3r"], d["w3o"])):
                sp.dma_start(raw[:, i], w.rearrange("(c p) n -> p c n", p=P)).then_inc(w_in[i], 16)

        @block.gpsimd
        def _(pool):
            begin(pool, mix.om_done, mix.scaled_done, mix.zeroed, s["ones_done"], s["init3"], s["bias_added"], s["ove_done"],
                  s["orstd_done"], norm.ve_done, norm.rstd_done)
            nc.gpsimd.memset(ones[:], 1.0).then_inc(s["ones_done"], 1)
            nc.gpsimd.memset(states[:], 0.0).then_inc(s["init3"], 1)
            norm.gpsimd(pool, 0)
            mix.gpsimd(pool, raw, w_in)
            pool.wait_ge(s["ones_done"], START + 1)
            for c in range(KC):
                last = nc.gpsimd.tensor_scalar_mul(lnb[:, c], ones[:], col(k, "ln_b", c))
            last.then_inc(s["ones_done"], 1)

            def add_bias(G):
                pool.wait_ge(norm.z_done, START + G + 1)
                apart(k, pool)
                for j in range(GT):
                    xt = norm.tile(G * GT + j)
                    last = nc.gpsimd.tensor_tensor(xt, xt, row(bias, G // GPB), ALU.add)
                last.then_inc(s["bias_added"], 1)

            norm.gpsimd(pool, 1)
            pool.wait_ge(s["centred"], START + 1)
            add_bias(0)

            def body(G, prev, nxt, nxt2):
                if nxt:
                    add_bias(G + 1)
                if prev:
                    out_rstd(G - 1)
                if nxt2:
                    norm.gpsimd(pool, G + 2)

            def out_rstd(G):
                pool.wait_ge(s["ostats"], START + G + 1)
                apart(k, pool)
                nc.gpsimd.tensor_scalar_add(ove[:], omv[:, :, 1], EPS).then_inc(s["ove_done"], 1)
                pool.wait_ge(s["ove_done"], START + G + 1)
                pool.wait_ge(k.x3_done, START + G * 2)
                nc.gpsimd.tensor_tensor(orstd[:], ove[:], k.mhalf[:, 0:GT], ALU.pow).then_inc(s["orstd_done"], 1)

            through_groups(pool, body)
            out_rstd(GROUPS - 1)

        @block.scalar
        def _(act):
            begin(act, s["dec_done"], s["wo_hi"], mix.w_hi, mix.hi_h, s["ks_done"], s["hi_o"])
            nc.scalar.activation(dec[:], k.cols[:, :, COL["decay"]], ACT.Exp).then_inc(s["dec_done"], 1)
            mix.scalar_zero(act)
            for c in range(KC):
                mix.scalar_h(act, norm, 0, c, ring[:, c])
            for i in range(3):
                mix.scalar_weights(act, i)
            act.wait_ge(s["wog_done"], START + 3)
            nc.scalar.copy(woh[:], wog[:]).then_inc(s["wo_hi"], 1)

            def ks_of(G, c):
                act.wait_ge(s["kvr_ready"], START + G * 6 + 3 * c + 1)
                if not isinstance(G, int) or G:
                    act.wait_ge(s["kv_done"], START + (G - 1) * KC + c + 1)
                nc.scalar.copy(ks[:, c], kvr[:, 3 * c]).then_inc(s["ks_done"], 1)

            def o_hi(G, c):
                act.wait_ge(s["o_done"], START + G * KC + c + 1)
                act.wait_ge(s["out_ready"], START + G * 2)
                nc.scalar.copy(oh[:, c], o[:, c]).then_inc(s["hi_o"], 1)

            def body(G, prev, nxt, nxt2):
                if prev:
                    o_hi(G - 1, 1)
                ks_of(G, 0)
                if nxt:
                    for c in range(KC):
                        mix.scalar_h(act, norm, G + 1, c, ring[:, c])
                ks_of(G, 1)
                o_hi(G, 0)

            through_groups(act, body)
            o_hi(GROUPS - 1, 1)

        @block.vector
        def _(v):
            begin(v, s["wog_done"], s["centred"], s["wo_lo"], mix.w_lo, mix.lo_h, s["dve3"], s["kv_done"],
                  s["o_done"], s["lo_o"], s["obn_done"], s["ostats"], norm.bn_done, norm.stats, norm.z_done, k.x3_done)
            norm.vector_stats(v, 0, 0)
            norm.vector_z(v, 0, 0)
            v.wait_ge(w_in[3], 16)
            for c in range(KC):
                last = nc.vector.tensor_scalar(wo[:, c], raw[:, 3, c], col(k, "ln_g", c), None, ALU.mult)
            last.then_inc(s["wog_done"], 1)
            v.wait_ge(s["wog_done"], START + 1)
            for b in range(B):
                for c in range(KC):
                    last = nc.vector.tensor_tensor(wog[:, b, c], wo[:, c], k.gate[:, 4 + b], ALU.mult)
            last.then_inc(s["wog_done"], 1)
            norm.vector_stats(v, 1, GT)
            for c in range(KC):
                mix.vector_h(v, 0, c)
            v.wait_ge(s["sums_ready"], START + 1)
            for b in range(B):
                for c in range(KC):
                    last = nc.vector.scalar_tensor_tensor(out=wog[:, b, c], in0=kvr[:, 0, b * D:(b + 1) * D], scalar=-1.0 / D,
                                                          in1=wog[:, b, c], op0=ALU.mult, op1=ALU.add)
            last.then_inc(s["wog_done"], 1)
            for b in range(B):
                last = nc.vector.tensor_tensor(bias[:, b], kvr[:, 1, 0:D], k.gate[:, 4 + b], ALU.mult)
            last.then_inc(s["centred"], 1)
            for i in range(3):
                mix.vector_weights(v, i)
            norm.vector_z(v, 1, GT)
            v.wait_ge(s["wo_hi"], START + 1)
            nc.vector.tensor_tensor(wol[:], wog[:], woh[:], ALU.subtract).then_inc(s["wo_lo"], 1)
            v.wait_ge(s["dec_done"], START + 1)
            v.wait_ge(s["init3"], START + 1)
            PER = 2

            def scan(G, c):
                chain = Counted(v, s["dve3"], (G * KC + c) * PER)
                v.wait_ge(s["ks_done"], START + G * KC + c + 1)
                v.wait_ge(s["kvr_ready"], START + G * 6 + 3 * c + 2)
                nc.vector.tensor_tensor(kv[:], ks[:, c], kvr[:, 3 * c + V_], ALU.mult).then_inc(s["kv_done"], 1)
                v.wait_ge(s["kv_done"], START + G * KC + c + 1)
                apart(k, v)
                chain.link(nc.vector.tensor_tensor_scan(st[:], dec[:, c:c + 1].to_broadcast([P, GW]), kv[:],
                                                        slot(c, G, 0), ALU.mult, ALU.add), k)
                nc.vector.tensor_copy(slot(c, G, 1), st[:, GW - 1:GW])
                chain.link(nc.vector.scalar_tensor_tensor(out=fo[:], in0=kv[:], scalar=col(k, "first", c), in1=st[:],
                                                          op0=ALU.mult, op1=ALU.add))
                v.wait_ge(s["kvr_ready"], START + G * 6 + 3 * c + 3)
                v.wait_ge(s["ot_ready"], START + G * 2)
                nc.vector.tensor_tensor(o[:, c], fo[:], kvr[:, 3 * c + R_], ALU.mult).then_inc(s["o_done"], 1)

            def o_lo(G, c):
                v.wait_ge(s["hi_o"], START + G * KC + c + 1)
                nc.vector.tensor_tensor(ol[:, c], o[:, c], oh[:, c], ALU.subtract).then_inc(s["lo_o"], 1)

            def out_stats(G):
                for i in range(2):
                    v.wait_ge(s["ot_ready"], START + G * 2 + i + 1)
                    apart(k, v)
                    for j in range(2):
                        last = nc.vector.bn_stats(obn[:, 2 * i + j], ring[:, 1 - i, j * D:(j + 1) * D])
                    last.then_inc(s["obn_done"], 1)
                v.wait_ge(s["obn_done"], START + G * 2 + 2)
                apart(k, v)
                for j in range(GT):
                    last = nc.vector.bn_aggr(omv[:, j], obn[:, j])
                last.then_inc(s["ostats"], 1)

            def final(G):
                v.wait_ge(s["orstd_done"], START + G + 1)
                v.wait_ge(s["bias_added"], START + G + 1)
                for i in range(2):
                    v.wait_ge(s["out_ready"], START + G * 2 + i + 1)
                    for j in (2 * i, 2 * i + 1):
                        xt = norm.tile(G * GT + j)
                        last = nc.vector.scalar_tensor_tensor(out=xt, in0=ring[:, i, (j % 2) * D:(j % 2 + 1) * D],
                                                              scalar=orstd[:, j:j + 1], in1=xt, op0=ALU.mult, op1=ALU.add)
                    last.then_inc(k.x3_done, 1)

            def body(G, prev, nxt, nxt2):
                if prev:
                    scan(G - 1, 1)
                    o_lo(G - 1, 0)
                    o_lo(G - 1, 1)
                if nxt:
                    mix.vector_h(v, G + 1, 0)
                if prev:
                    out_stats(G - 1)
                scan(G, 0)
                if nxt:
                    mix.vector_h(v, G + 1, 1)
                if nxt2:
                    norm.vector_stats(v, G + 2, (G + 2) * GT)
                if prev:
                    final(G - 1)
                if nxt2:
                    norm.vector_z(v, G + 2, (G + 2) * GT)

            through_groups(v, body)
            scan(GROUPS - 1, 1)
            o_lo(GROUPS - 1, 0)
            o_lo(GROUPS - 1, 1)
            out_stats(GROUPS - 1)
            final(GROUPS - 1)

        @block.tensor
        def _(pe):
            begin(pe, s["sums_ready"], s["kvr_ready"], s["ot_ready"], s["out_ready"], norm.zt_done)
            pe.wait_ge(s["ones_done"], START + 1)
            for c in range(KC):
                norm.tensor(pe, 0, c, ring[:, c])
            pe.wait_ge(s["wog_done"], START + 2)
            for b in range(B):
                for c in range(KC):
                    nc.tensor.matmul(kvr[:, 0, b * D:(b + 1) * D], ones[:], wog[:, b, c], start=(c == 0), stop=(c == KC - 1))
            pe.wait_ge(s["ones_done"], START + 2)
            for c in range(KC):
                last = nc.tensor.matmul(kvr[:, 1, 0:D], lnb[:, c], raw[:, 3, c], start=(c == 0), stop=(c == KC - 1))
            last.then_inc(s["sums_ready"], 1)
            pe.wait_ge(mix.zeroed, START + 2)
            pe.wait_ge(s["centred"], START + 1)

            def piece(G, c, i, prev):
                if i == 0:
                    if c == 0:
                        pe.wait_ge(mix.lo_h, START + (G + 1) * KC)
                    if prev:
                        pe.wait_ge(s["o_done"], START + (G - 1) * KC + c + 1)
                if not prev and c == 0:
                    pe.wait_ge(mix.w_lo, START + i + 1)
                last = mix.tensor(kvr[:, 3 * c + i], i, slice(c * P, (c + 1) * P), G)
                last.then_inc(s["kvr_ready"], 1)

            def turn_z(G, c):
                if isinstance(G, int) and G < 2:
                    pe.wait_ge(mix.hi_h, START + G * KC)
                elif c == 0:
                    pe.wait_ge(mix.hi_h, START + G * KC)
                    pe.wait_ge(k.x3_done, START + (G - 2) * 2)
                else:
                    pe.wait_ge(s["obn_done"], START + (G - 2) * 2 + 1)
                norm.tensor(pe, G, c, ring[:, c])

            def turn_o(G, i, nxt):
                if i == 0:
                    pe.wait_ge(s["o_done"], START + (G + 1) * KC)
                    pe.wait_ge(k.x3_done, START + G * 2)
                elif nxt:
                    pe.wait_ge(mix.hi_h, START + (G + 2) * KC + 1)
                for j in (2 * i, 2 * i + 1):
                    for c in range(KC):
                        a = (j % 2) * D + c * P
                        last = nc.tensor.transpose(ring[:, 1 - i, a:a + P], o[:, c, j * P:(j + 1) * P], k.ident[:])
                last.then_inc(s["ot_ready"], 1)

            def output(G, i, nxt):
                if i == 0:
                    pe.wait_ge(s["obn_done"], START + G * 2 + 2)
                    pe.wait_ge(s["lo_o"], START + (G + 1) * KC)
                    pe.wait_ge(s["wo_lo"], START + 1)
                elif nxt:
                    pe.wait_ge(mix.hi_h, START + (G + 3) * KC)
                for j in (2 * i, 2 * i + 1):
                    q = slice(j * P, (j + 1) * P)
                    for c in range(KC):
                        last = three_b(nc.tensor, ring[:, i, (j % 2) * D:(j % 2 + 1) * D], oh[:, c, q], ol[:, c, q],
                                       woh, wol, G // GPB, c)
                last.then_inc(s["out_ready"], 1)

            def body(G, prev, nxt, nxt2):
                piece(G, 0, K_, prev)
                if nxt:
                    turn_z(G + 1, 0)
                piece(G, 0, V_, prev)
                if prev:
                    turn_o(G - 1, 0, nxt)
                    turn_o(G - 1, 1, nxt)
                piece(G, 0, R_, prev)
                if nxt:
                    turn_z(G + 1, 1)
                piece(G, 1, K_, prev)
                if prev:
                    output(G - 1, 0, nxt)
                piece(G, 1, V_, prev)
                if prev:
                    output(G - 1, 1, nxt)
                piece(G, 1, R_, prev)

            through_groups(pe, body)
            for i in range(2):
                turn_o(GROUPS - 1, i, False)
            for i in range(2):
                output(GROUPS - 1, i, False)


def three_b(eng, out, lh, ll, rh, rl, b, c):
    pick = lambda r: r[:, bass.ds(b, 1), c, :].rearrange("p o d -> p (o d)")
    return three(eng, out, lh, ll, pick(rh), pick(rl), c == 0, c == KC - 1)


def channel_mixing(nc, k, d):
    with ExitStack() as ctx:
        sb = lambda n, s, t=F32: ctx.enter_context(nc.sbuf_tensor(n, s, t))
        sem = lambda n: ctx.enter_context(nc.semaphore(n))
        ps = lambda n, s: ctx.enter_context(nc.psum_tensor(n, s, F32))
        K_, R_ = range(2)
        raw = sb("raw4", [P, 3, KC, D])
        mix = Shifted(nc, k, ctx, "4", ("mu_k", "mu_r"))
        wvh, wvl = sb("wvh4", [P, KC, D], F32R), sb("wvl4", [P, KC, D], F32R)
        kr = sb("kr4", [P, KC, GW])
        ka = sb("ka4", [P, KC, GW])
        kah, kal = sb("kah4", [P, KC, GW], F32R), sb("kal4", [P, KC, GW], F32R)
        sr = sb("sr4", [P, KC, GW])
        rv = sb("rv4", [P, KC, GW])
        norm = Norm(nc, k, ctx, "n4", 1, 2)
        kp, rp, vp, ring = (ps(n, [P, KC, 512]) for n in ("kp4", "rp4", "vp4", "ring4"))
        w_in = [sem(f"c_w_in{i}") for i in range(3)]
        names = ("wv_hi wv_lo k_ready r_ready kr_done ka_done hi_k lo_k sr_done v_ready rv_done yt_ready x4_done")
        s = {n: sem("c_" + n) for n in names.split()}
        block = ctx.enter_context(nc.Block())

        @block.sync
        def _(sp):
            for i, w in enumerate((d["w4k"], d["w4r"], d["w4v"])):
                sp.dma_start(raw[:, i], w.rearrange("(c p) n -> p c n", p=P)).then_inc(w_in[i], 16)
            with sp.Fori(0, GROUPS) as G:
                sp.wait_ge(s["x4_done"], START + (G + 1) * 2)
                sp.dma_start(d["out"][bass.ds(G, 1)].rearrange("o (t p) d -> p (o t) d", p=P),
                             k.x[:, bass.ds(G * GT, GT), :]).then_inc(k.stored, 16)
            sp.wait_ge(k.stored, GROUPS * 16)

        @block.gpsimd
        def _(pool):
            begin(pool, mix.om_done, mix.scaled_done, mix.zeroed, s["ka_done"], norm.ve_done, norm.rstd_done)
            norm.gpsimd(pool, 0)
            mix.gpsimd(pool, raw, w_in)
            norm.gpsimd(pool, 1)

            def body(G, prev, nxt, nxt2):
                for c in range(KC):
                    pool.wait_ge(s["kr_done"], START + G * KC + c + 1)
                    pool.wait_ge(s["lo_k"], START + G * KC)
                    nc.gpsimd.tensor_tensor(ka[:, c], kr[:, c], kr[:, c], ALU.mult).then_inc(s["ka_done"], 1)
                if nxt2:
                    norm.gpsimd(pool, G + 2)

            through_groups(pool, body)

        @block.scalar
        def _(act):
            begin(act, s["wv_hi"], mix.w_hi, mix.hi_h, s["kr_done"], s["hi_k"], s["sr_done"])
            mix.scalar_zero(act)
            for c in range(KC):
                mix.scalar_h(act, norm, 0, c, ring[:, c])
            for i in range(2):
                mix.scalar_weights(act, i)
            act.wait_ge(w_in[2], 16)
            nc.scalar.copy(wvh[:], raw[:, 2]).then_inc(s["wv_hi"], 1)

            def relu(G, c):
                act.wait_ge(s["k_ready"], START + G * KC + c + 1)
                act.wait_ge(s["ka_done"], START + G * KC)
                nc.scalar.activation(kr[:, c], kp[:, c], ACT.Relu).then_inc(s["kr_done"], 1)

            def body(G, prev, nxt, nxt2):
                relu(G, 0)
                if nxt:
                    mix.scalar_h(act, norm, G + 1, 0, ring[:, 0])
                relu(G, 1)
                if nxt:
                    mix.scalar_h(act, norm, G + 1, 1, ring[:, 1])
                for c in range(KC):
                    act.wait_ge(s["ka_done"], START + G * KC + c + 1)
                    act.wait_ge(s["v_ready"], START + G * KC)
                    nc.scalar.copy(kah[:, c], ka[:, c]).then_inc(s["hi_k"], 1)
                for c in range(KC):
                    act.wait_ge(s["r_ready"], START + G * KC + c + 1)
                    act.wait_ge(s["rv_done"], START + G * KC)
                    nc.scalar.activation(sr[:, c], rp[:, c], ACT.Sigmoid).then_inc(s["sr_done"], 1)

            through_groups(act, body)

        @block.vector
        def _(v):
            begin(v, s["wv_lo"], mix.w_lo, mix.lo_h, s["lo_k"], s["rv_done"], s["x4_done"], norm.bn_done, norm.stats, norm.z_done)
            norm.vector_stats(v, 0, 0)
            norm.vector_z(v, 0, 0)
            norm.vector_stats(v, 1, GT)
            for c in range(KC):
                mix.vector_h(v, 0, c)
            for i in range(2):
                mix.vector_weights(v, i)
            norm.vector_z(v, 1, GT)
            v.wait_ge(s["wv_hi"], START + 1)
            nc.vector.tensor_tensor(wvl[:], raw[:, 2], wvh[:], ALU.subtract).then_inc(s["wv_lo"], 1)

            def product(G):
                b = G // GPB
                for c in range(KC):
                    v.wait_ge(s["sr_done"], START + G * KC + c + 1)
                    v.wait_ge(s["v_ready"], START + G * KC + c + 1)
                    v.wait_ge(s["yt_ready"], START + G * 2)
                    gate = k.gatecol[:, 1, 1, c, b:b + 1] if isinstance(G, int) else k.gatecol[:, 1, 1, c, bass.ds(b, 1)]
                    nc.vector.scalar_tensor_tensor(out=rv[:, c], in0=sr[:, c], scalar=gate, in1=vp[:, c],
                                                   op0=ALU.mult, op1=ALU.mult).then_inc(s["rv_done"], 1)

            def final(G, i):
                v.wait_ge(s["yt_ready"], START + G * 2 + i + 1)
                apart(k, v)
                xt = k.x[:, bass.ds(G * GT + 2 * i, 2), :].rearrange("p t d -> p (t d)")
                nc.vector.tensor_tensor(xt, xt, ring[:, i], ALU.add).then_inc(s["x4_done"], 1)

            def body(G, prev, nxt, nxt2):
                if prev:
                    product(G - 1)
                if nxt:
                    for c in range(KC):
                        mix.vector_h(v, G + 1, c)
                if nxt2:
                    norm.vector_stats(v, G + 2, (G + 2) * GT)
                for c in range(KC):
                    v.wait_ge(s["hi_k"], START + G * KC + c + 1)
                    nc.vector.tensor_tensor(kal[:, c], ka[:, c], kah[:, c], ALU.subtract).then_inc(s["lo_k"], 1)
                if nxt2:
                    norm.vector_z(v, G + 2, (G + 2) * GT)
                if prev:
                    final(G - 1, 0)
                    final(G - 1, 1)

            through_groups(v, body)
            product(GROUPS - 1)
            final(GROUPS - 1, 0)
            final(GROUPS - 1, 1)

        @block.tensor
        def _(pe):
            begin(pe, s["k_ready"], s["r_ready"], s["v_ready"], s["yt_ready"], norm.zt_done)

            def turn_z(G, c):
                pe.wait_ge(mix.hi_h, START + G * KC)
                if not isinstance(G, int) or G >= 2:
                    pe.wait_ge(s["x4_done"], START + (G - 2) * 2)
                norm.tensor(pe, G, c, ring[:, c])

            def k_of(G, c, prev):
                if c == 0:
                    pe.wait_ge(mix.lo_h, START + (G + 1) * KC)
                if not prev:
                    pe.wait_ge(mix.w_lo, START + 1)
                pe.wait_ge(s["kr_done"], START + G * KC)
                mix.tensor(kp[:, c], K_, slice(c * P, (c + 1) * P), G).then_inc(s["k_ready"], 1)

            def r_of(G, c, prev):
                if not prev:
                    pe.wait_ge(mix.w_lo, START + 2)
                pe.wait_ge(s["sr_done"], START + G * KC)
                mix.tensor(rp[:, c], R_, slice(c * P, (c + 1) * P), G).then_inc(s["r_ready"], 1)

            def v_of(G, c):
                if c == 0:
                    pe.wait_ge(s["wv_lo"], START + 1)
                    pe.wait_ge(s["lo_k"], START + (G + 1) * KC)
                    pe.wait_ge(s["rv_done"], START + G * KC)
                m = slice(c * P, (c + 1) * P)
                for kc in range(KC):
                    last = three(nc.tensor, vp[:, c], wvh[:, kc, m], wvl[:, kc, m], kah[:, kc], kal[:, kc], kc == 0, kc == KC - 1)
                last.then_inc(s["v_ready"], 1)

            def turn_back(G, i, nxt):
                if i == 0:
                    pe.wait_ge(s["rv_done"], START + (G + 1) * KC)
                    pe.wait_ge(s["x4_done"], START + G * 2)
                if nxt:
                    pe.wait_ge(mix.hi_h, START + (G + 2) * KC + i + 1)
                for j in range(2):
                    for c in range(KC):
                        a = j * D + c * P
                        q = slice((2 * i + j) * P, (2 * i + j + 1) * P)
                        last = nc.tensor.transpose(ring[:, i, a:a + P], rv[:, c, q], k.ident[:])
                last.then_inc(s["yt_ready"], 1)

            for c in range(KC):
                if c == 0:
                    pe.wait_ge(norm.z_done, START + 1)
                norm.tensor(pe, 0, c, ring[:, c])

            def body(G, prev, nxt, nxt2):
                k_of(G, 0, prev)
                if nxt:
                    turn_z(G + 1, 0)
                k_of(G, 1, prev)
                if nxt:
                    turn_z(G + 1, 1)
                r_of(G, 0, prev)
                if prev:
                    turn_back(G - 1, 0, nxt)
                r_of(G, 1, prev)
                if prev:
                    turn_back(G - 1, 1, nxt)
                v_of(G, 0)
                v_of(G, 1)

            through_groups(pe, body)
            turn_back(GROUPS - 1, 0, False)
            turn_back(GROUPS - 1, 1, False)


def program(nc, d, stages=4):
    with ExitStack() as ctx:
        sb = lambda n, s, t=F32: ctx.enter_context(nc.sbuf_tensor(n, s, t))
        k = Kept()
        k.sem = lambda n: ctx.enter_context(nc.semaphore(n))
        k.x = sb("x", [P, TILES, D])
        k.cols = sb("cols", [P, KC, len(COLS)])
        k.rows = sb("rows", [P, 2 * D + E])
        k.colmod = sb("colmod", [P, 2, 4, KC, B])
        k.gatecol = sb("gatecol", [P, 2, 2, KC, B])
        k.gate = sb("gate", [P, 3 * B, D])
        k.bo_gate = sb("bo_gate", [P, B, D])
        k.ident = sb("ident", [P, P])
        k.causal = sb("causal", [P, P])
        k.mhalf = sb("mhalf", [P, TPB])
        k.consts, k.x1_done, k.x2_done, k.x3_done, k.stored = (k.sem(n) for n in ("consts", "x1_done", "x2_done", "x3_done", "stored"))
        k.passed = {nc.gpsimd.engine: k.sem("passed_gpsimd"), nc.vector.engine: k.sem("passed_vector"),
                    nc.scalar.engine: k.sem("passed_scalar")}
        setup(nc, k, d)
        if stages >= 1:
            attention(nc, k, d)
        if stages >= 2:
            experts(nc, k, d)
        if stages >= 3:
            time_mixing(nc, k, d)
        if stages >= 4:
            channel_mixing(nc, k, d)
        else:
            block = ctx.enter_context(nc.Block())

            @block.sync
            def _(sp):
                for G in range(GROUPS):
                    sp.wait_ge(k.x_in[G // GPB], 16 * GPB)
                    sp.dma_start(d["out"][G].rearrange("(t p) d -> p t d", p=P), k.x[:, G * GT:(G + 1) * GT, :]).then_inc(k.stored, 16)
                sp.wait_ge(k.stored, GROUPS * 16)


def layout(inputs):
    a = {n: np.asarray(v) for n, v in inputs.items()}
    vec = {"bq": "L0_attn_bq", "bk": "L0_attn_bk", "mix_k": "L1_attn_time_mix_k", "mix_v": "L1_attn_time_mix_v",
           "mix_r": "L1_attn_time_mix_r", "decay": "L1_attn_time_decay", "first": "L1_attn_time_first",
           "ln_g": "L1_attn_ln_g", "ln_b": "L1_attn_ln_b", "mu_r": "L1_ffn_mu_r", "mu_k": "L1_ffn_mu_k"}
    rows = [a[vec[n]].reshape(D) for n in COLS[:C0]] + [a[f"L{l}_c"][b] for l in range(2) for b in range(B)]
    out = {
        "x": a["L0_attn_y_all"].reshape(B * T, D),
        "cols": np.ascontiguousarray(np.stack(rows).reshape(len(COLS), KC, P).transpose(2, 1, 0)),
        "rows": np.concatenate([a["L0_attn_bv"], a["L0_attn_bo"], a["L0_ffn_expert_bias"]]).reshape(1, 2 * D + E),
        "wmod": np.stack([a["L0_wmod"], a["L1_wmod"]]),
        "wq": a["L0_attn_Wq"], "wk": a["L0_attn_Wk"], "wv": a["L0_attn_Wv"], "wo": a["L0_attn_Wo"],
        "router": a["L0_ffn_W_gate_router"], "wg": a["L0_ffn_Wg"], "wu": a["L0_ffn_Wu"], "wd": a["L0_ffn_Wd"],
        "wg_s": a["L0_ffn_Wg_s"], "wu_s": a["L0_ffn_Wu_s"], "wd_s": a["L0_ffn_Wd_s"],
    }
    for n, w in (("w3k", "L1_attn_Wk"), ("w3v", "L1_attn_Wv"), ("w3r", "L1_attn_Wr"), ("w3o", "L1_attn_Wo"),
                 ("w4k", "L1_ffn_W_k"), ("w4r", "L1_ffn_W_r"), ("w4v", "L1_ffn_W_v")):
        out[n] = a[w].T
    return {n: np.ascontiguousarray(v) for n, v in out.items()}


def kernel(**inputs):
    import concourse.bacc as bacc
    from concourse.bass_utils import run_bass_kernel_spmd

    arrays = layout(inputs)
    nc = bacc.Bacc("TRN2", target_bir_lowering=False, num_devices=1)
    d = {n: nc.dram_tensor("in_" + n, v.shape, mybir.dt.from_np(v.dtype), kind="ExternalInput").ap()
                     for n, v in arrays.items()}
    d["out"] = nc.dram_tensor("out", (GROUPS, GW, D), F32, kind="ExternalOutput").ap()
    program(nc, d)
    result = run_bass_kernel_spmd(nc, [{"in_" + n: v for n, v in arrays.items()}], core_ids=[0])
    return result.results[0]["out"].reshape(B, T, D)
```

```python
from contextlib import ExitStack

import numpy as np

import concourse.bass as bass
from concourse import mybir



class Kept:

    def stage_sem(self, nc, name):
        sem = nc.alloc_semaphore(name)
        self.stage_sems.append(sem)
        return sem


ALU = mybir.AluOpType
ACT = mybir.ActivationFunctionType
AX = mybir.AxisListType
F32 = mybir.dt.float32
F32R = mybir.dt.float32r
U32 = mybir.dt.uint32

P = 128
B, T, D = 2, 2048, 256
KC = D // P
TILES = B * T // P
TPB = T // P
GT = 4
GROUPS = TILES // GT
GPB = GROUPS // B
GW = GT * P
EPS = 1e-5
E = 8
F = 192
NEG = -1e30

COLS = ["bq", "bk", "mix_k", "mix_v", "mix_r", "decay", "first", "ln_g", "ln_b", "mu_r", "mu_k",
        "c00", "c01", "c10", "c11"]
COL = {n: i for i, n in enumerate(COLS)}
C0 = COL["c00"]
SHIFT_A, SCALE_A, GATE_A, SHIFT_B, SCALE_B, GATE_B = range(6)
COLKINDS = [SHIFT_A, SCALE_A, SHIFT_B, SCALE_B]


START = 1


def begin(eng, *sems):
    for sem in sems:
        eng.sem_inc(sem, START)


class Counted:

    def __init__(self, eng, sem, base=0):
        self.eng, self.sem, self.base, self.n = eng, sem, base, 0

    def link(self, ins, k=None):
        ins.then_inc(self.sem, 1)
        self.n += 1
        self.eng.wait_ge(self.sem, START + self.base + self.n)
        if k:
            apart(k, self.eng)


def three(eng, out, lh, ll, rh, rl, first, last):
    eng.matmul(out, lh, rh, start=first, stop=False)
    eng.matmul(out, lh, rl, start=False, stop=False)
    return eng.matmul(out, ll, rh, start=False, stop=last)


def apart(k, eng):
    eng.sem_inc(k.passed[eng.engine], 1)


def col(k, name, c):
    return k.cols[:, c, COL[name]:COL[name] + 1]


def statistics(nc, k, v, b):
    v.wait_ge(k.x_in[b], 16 * GPB)
    if b:
        v.wait_ge(k.stats, START + b)
    for t in range(TPB):
        last = nc.vector.bn_stats(k.bn[:, t], k.x[:, b * TPB + t])
    last.then_inc(k.bn_done, 1)
    v.wait_ge(k.bn_done, START + b + 1)
    for t in range(TPB):
        last = nc.vector.bn_aggr(k.mv[:, b * TPB + t], k.bn[:, t])
    last.then_inc(k.stats, 1)


def setup(nc, k, d):
    with ExitStack() as ctx:
        sb = lambda n, s, t=F32: ctx.enter_context(nc.sbuf_tensor(n, s, t))
        sem = lambda n: ctx.enter_context(nc.semaphore(n))
        KINDS = 6
        ROWS = 3 * B
        wmod = sb("wmod", [P, 2, KC, KINDS * D])
        silu_c = sb("silu_c", [P, KC, 4])
        silu_t = sb("silu_t", [P, KC, 4])
        graw = sb("graw", [P, 2, 2, KC, B])
        gabs = sb("gabs", [P, 2, 2, KC, B])
        gate_bc = sb("gate_bc", [P, ROWS, KC, P])
        colp = ctx.enter_context(nc.psum_tensor("colp", [P, 2, KINDS, KC, B], F32))
        rowp = ctx.enter_context(nc.psum_tensor("rowp", [P, ROWS, D], F32))
        wmod_in = [sem(f"wmod_in{i}") for i in range(2)]
        k.w_in = [k.stage_sem(nc, f"a_w_in{i}") for i in range(4)]
        small_in, rows_in, silu_e, dve, bc_ready, cols_done, rows_done, rows_out, id0 = (
            sem(n) for n in ("small_in", "rows_in", "silu_e", "s0_dve", "bc_ready",
                             "cols_done", "rows_done", "rows_out", "id0"))
        k.x_in = [k.sem(f"x_in{b}") for b in range(B)]
        k.bn_done, k.stats = k.stage_sem(nc, "a_bn_done"), k.stage_sem(nc, "a_stats")
        block = ctx.enter_context(nc.Block())

        @block.sync
        def _(sp):
            sp.dma_start(k.cols[:], d["cols"]).then_inc(small_in, 16)
            sp.dma_start(wmod[:, 0], d["wmod"][0].rearrange("(c p) n -> p c n", p=P)).then_inc(wmod_in[0], 16)
            sp.dma_start(wmod[:, 1], d["wmod"][1].rearrange("(c p) n -> p c n", p=P)).then_inc(wmod_in[1], 16)
            sp.dma_start(k.rows[:], d["rows"].to_broadcast([P, 2 * D + E])).then_inc(rows_in, 16)
            for i, w in enumerate((d["wq"], d["wk"], d["wv"], d["wo"])):
                sp.dma_start(k.raw[:, i].rearrange("p (c n) -> p c n", c=KC),
                             w.rearrange("(c p) n -> p c n", p=P)).then_inc(k.w_in[i], 16)
            for g in range(GROUPS):
                sp.dma_start(k.x[:, g * GT:(g + 1) * GT, :],
                             d["x"][g * GW:(g + 1) * GW, :].rearrange("(t p) d -> p t d", p=P)).then_inc(k.x_in[g // GPB], 16)

        @block.gpsimd
        def _(pool):
            nc.gpsimd.memset(k.ident[:], 0.0).then_inc(id0, 1)
            nc.gpsimd.memset(k.causal[:], 0.0).then_inc(id0, 1)
            nc.gpsimd.memset(k.mhalf[:], -0.5)
            pool.wait_ge(id0, 2)
            nc.gpsimd.affine_select(out=k.ident[:], in_=k.ident[:], compare_op=ALU.not_equal, fill=1.0,
                                    base=0, pattern=[[-1, P]], channel_multiplier=1)
            nc.gpsimd.affine_select(out=k.causal[:], in_=k.causal[:], compare_op=ALU.is_ge, fill=NEG,
                                    base=0, pattern=[[-1, P]], channel_multiplier=1).then_inc(k.consts, 1)

        @block.scalar
        def _(act):
            act.wait_ge(small_in, 16)
            nc.scalar.activation(silu_t[:], k.cols[:, :, C0:C0 + 4], ACT.Exp, scale=-1.0).then_inc(silu_e, 1)
            act.wait_ge(rows_done, 1)
            nc.scalar.copy(k.gate[:], rowp[:]).then_inc(rows_out, 1)

        @block.vector
        def _(v):
            begin(v, k.bn_done, k.stats)
            c = Counted(v, dve, -START)
            v.wait_ge(silu_e, 1)
            c.link(nc.vector.tensor_scalar_add(silu_t[:], silu_t[:], 1.0))
            c.link(nc.vector.reciprocal(silu_t[:], silu_t[:]))
            nc.vector.tensor_tensor(silu_c[:], silu_t[:], k.cols[:, :, C0:C0 + 4], ALU.mult).then_inc(bc_ready, 1)
            statistics(nc, k, v, 0)
            v.wait_ge(cols_done, 1)
            for l in range(2):
                for i, kind in enumerate(COLKINDS):
                    add = 1.0 if kind in (SCALE_A, SCALE_B) else 0.0
                    nc.vector.tensor_scalar_add(k.colmod[:, l, i], colp[:, l, kind], add)
            for l in range(2):
                for i, kind in enumerate((GATE_A, GATE_B)):
                    last = nc.vector.tensor_copy(graw[:, l, i], colp[:, l, kind])
            c.link(last)
            c.link(nc.vector.tensor_scalar(gabs[:], graw[:], -1.0, None, ALU.mult))
            c.link(nc.vector.tensor_tensor(gabs[:], gabs[:], graw[:], ALU.max))
            c.link(nc.vector.tensor_scalar(graw[:], graw[:], 0.0, 2.0, ALU.is_ge, ALU.mult))
            c.link(nc.vector.tensor_scalar(graw[:], graw[:], -1.0, None, ALU.add))
            c.link(nc.vector.tensor_scalar(gabs[:], gabs[:], 0.25, None, ALU.max))
            c.link(nc.vector.tensor_tensor(k.gatecol[:], gabs[:], graw[:], ALU.mult))
            for r in range(ROWS):
                for kc in range(KC):
                    last = nc.vector.tensor_copy(gate_bc[:, r, kc],
                                                 k.gatecol[:, r // 4, r // B % 2, kc, r % B:r % B + 1].to_broadcast([P, P]))
            last.then_inc(bc_ready, 1)
            statistics(nc, k, v, 1)
            v.wait_ge(rows_in, 16)
            v.wait_ge(rows_out, 1)
            for b in range(B):
                nc.vector.tensor_tensor(k.bo_gate[:, b], k.gate[:, b], k.rows[:, D:2 * D], ALU.mult)

        @block.tensor
        def _(pe):
            pe.wait_ge(bc_ready, 1)
            for l in range(2):
                pe.wait_ge(wmod_in[l], 16)
                for kind in range(KINDS):
                    for c in range(KC):
                        for kc in range(KC):
                            o = kind * D + c * P
                            last = nc.tensor.matmul(colp[:, l, kind, c], wmod[:, l, kc, o:o + P],
                                                    silu_c[:, kc, 2 * l:2 * l + 2], start=(kc == 0), stop=(kc == KC - 1))
            last.then_inc(cols_done, 1)
            pe.wait_ge(k.consts, 1)
            pe.wait_ge(bc_ready, 2)
            for r in range(ROWS):
                for kc in range(KC):
                    last = nc.tensor.transpose(rowp[:, r, kc * P:(kc + 1) * P], gate_bc[:, r, kc], k.ident[:])
            last.then_inc(rows_done, 1)


def near(G):
    if isinstance(G, int):
        return G > 0, G + 1 < GROUPS, G + 2 < GROUPS
    return True, True, True


def through_groups(eng, body):
    body(0, *near(0))
    with eng.Fori(1, GROUPS - 2) as G:
        body(G, *near(G))
    for G in (GROUPS - 2, GROUPS - 1):
        body(G, *near(G))


class Norm:

    def __init__(self, nc, k, ctx, name, layer, shift, z=None):
        self.nc, self.k, self.layer, self.shift = nc, k, layer, shift
        sb = lambda n, s, t=F32: ctx.enter_context(nc.sbuf_tensor(name + n, s, t))
        sem = lambda n: ctx.enter_context(nc.semaphore(name + n))
        self.bn = sb("bn", [P, GT, 6])
        self.mv = sb("mv", [P, GT, 2])
        self.ve = sb("ve", [P, GT])
        self.rstd = sb("rstd", [P, GT])
        self.z = sb("z", [P, GT, D]) if z is None else z
        self.bn_done, self.stats, self.ve_done, self.rstd_done, self.z_done, self.zt_done = (
            sem(n) for n in ("bn_done", "stats", "ve_done", "rstd_done", "z_done", "zt_done"))

    def tile(self, t):
        return self.k.x[:, bass.ds(t, 1), :].rearrange("p o d -> p (o d)")

    def vector_stats(self, v, step, first):
        nc = self.nc
        for j in range(GT):
            last = nc.vector.bn_stats(self.bn[:, j], self.tile(first + j))
        last.then_inc(self.bn_done, 1)
        v.wait_ge(self.bn_done, START + step + 1)
        apart(self.k, v)
        for j in range(GT):
            last = nc.vector.bn_aggr(self.mv[:, j], self.bn[:, j])
        last.then_inc(self.stats, 1)

    def vector_z(self, v, step, first):
        nc = self.nc
        v.wait_ge(self.stats, START + step + 1)
        v.wait_ge(self.rstd_done, START + step + 1)
        v.wait_ge(self.zt_done, START + step * KC)
        for j in range(GT):
            last = nc.vector.tensor_scalar(self.z[:, j], self.tile(first + j), self.mv[:, j, 0:1],
                                           self.rstd[:, j:j + 1], ALU.subtract, ALU.mult)
        last.then_inc(self.z_done, 1)

    def gpsimd(self, pool, step):
        nc = self.nc
        pool.wait_ge(self.stats, START + step + 1)
        apart(self.k, pool)
        nc.gpsimd.tensor_scalar_add(self.ve[:], self.mv[:, :, 1], EPS).then_inc(self.ve_done, 1)
        pool.wait_ge(self.ve_done, START + step + 1)
        pool.wait_ge(self.z_done, START + step)
        nc.gpsimd.tensor_tensor(self.rstd[:], self.ve[:], self.k.mhalf[:, 0:GT], ALU.pow).then_inc(self.rstd_done, 1)

    def tensor(self, pe, step, c, zt):
        if c == 0:
            pe.wait_ge(self.z_done, START + step + 1)
        for j in range(GT):
            last = self.nc.tensor.transpose(zt[:, j * P:(j + 1) * P], self.z[:, j, c * P:(c + 1) * P], self.k.ident[:])
        last.then_inc(self.zt_done, 1)

    def scalar(self, act, step, c, zt, h, b):
        act.wait_ge(self.zt_done, START + step * KC + c + 1)
        m = self.k.colmod
        scale = m[:, self.layer, self.shift + 1, c, bass.ds(b, 1)]
        shift = m[:, self.layer, self.shift, c, bass.ds(b, 1)]
        apart(self.k, act)
        self.nc.scalar.activation(h, zt, ACT.Identity, bias=shift, scale=scale).then_inc(self.h_done, 1)


def attention(nc, k, d):
    with ExitStack() as ctx:
        sb = lambda n, s, t=F32: ctx.enter_context(nc.sbuf_tensor(n, s, t))
        sem = lambda n: k.stage_sem(nc, n)
        ps = lambda n, s: ctx.enter_context(nc.psum_tensor(n, s, F32))
        WQ, WK, WV, WO = range(4)
        RING = 2
        wh = sb("wh", [P, 4, KC, D], F32R)
        wl = sb("wl", [P, 4, KC, D], F32R)
        qh, ql = sb("qh", [P, KC, T], F32R), sb("ql", [P, KC, T], F32R)
        kh, kl = sb("kh", [P, KC, T], F32R), sb("kl", [P, KC, T], F32R)
        vh, vl = sb("vh", [P, TPB, D], F32R), sb("vl", [P, TPB, D], F32R)
        hh, hl = sb("hh", [P, 2, KC, GW], F32R), sb("hl", [P, 2, KC, GW], F32R)
        qkb = sb("qkb", [P, 2, KC, B])
        vb = sb("vb", [P, B, D])
        prob = k.prob
        pth, ptl = sb("pth", [P, RING, GW], F32R), sb("ptl", [P, RING, GW], F32R)
        mxc, mx, nmx = sb("mxc", [P, TPB, 4]), sb("mx", [P, TPB]), sb("nmx", [P, TPB])
        rsc, rsum, rinv = sb("rsc", [P, TPB, 4]), sb("rsum", [P, TPB]), sb("rinv", [P, TPB])
        cn = sb("cn", [P, D])
        cth, ctl = sb("cth", [P, KC, P], F32R), sb("ctl", [P, KC, P], F32R)
        y = sb("y1", [P, 2, D])
        mv = k.mv
        ve, rstd = sb("ve1", [P, TILES]), sb("rstd1", [P, TILES])
        z = prob[:, 1].rearrange("p (a t d) -> p a t d", a=2, t=GT)
        sc = ps("sc", [P, 4, 512])
        tp = ps("tp", [P, 2, 512])
        cx = ps("cx", [P, 512])
        pj = ps("pj", [P, 512])
        w_in = k.w_in
        names = ("w_hi w_lo shift_bc bias_ready bias_done hi_h lo_h qk_ready v_ready qk_hi qk_lo v_hi v_lo "
                 "s_ready dve1 nmax_done exp_done pt_ready pt_hi pt_lo pv_done cn_done ct_ready ct_hi "
                 "ct_lo pj_ready y_done bo_done ve_done rstd_done z_done zt_done")
        s = {n: sem("a_" + n) for n in names.split()}
        UNITS = [[(t, 0)] for t in range(15, 11, -1)] + [[(11 - i, 0), (3 - i, 3)] for i in range(4)] + [[(7, 0), (6, 2)], [(5, 0), (4, 2)]]
        ORDER = [t for u in UNITS for t, _ in u]
        BANK = {t: o for u in UNITS for t, o in u}
        UNIT = {t: i for i, u in enumerate(UNITS) for t, _ in u}
        FROM = [sum(len(x) for x in UNITS[:i]) for i in range(len(UNITS) + 1)]
        NU = len(UNITS)
        NCH = {t: (t + GT) // GT for t in range(TPB)}
        OFF = [sum(NCH[t] for t in ORDER[:i]) for i in range(TPB + 1)]
        CHB = OFF[-1]
        SEQ = [(i, ch) for i, t in enumerate(ORDER) for ch in range(NCH[t])]
        UNIT_OF = [UNIT[ORDER[i]] for i, _ in SEQ]
        STEP = [m - OFF[FROM[u]] for m, u in enumerate(UNIT_OF)]

        def chunks(u, half=None):
            if u >= NU:
                return range(0)
            a, z = OFF[FROM[u]], OFF[FROM[u + 1]]
            h = a + (z - a + 1) // 2
            return range(*((a, z), (a, h), (h, z))[0 if half is None else half + 1])

        def score_bank(m):
            return BANK[ORDER[SEQ[m][0]]] + SEQ[m][1]

        def freed(m):
            return max([j + 1 for j in range(chunks(UNIT_OF[m])[0]) if score_bank(j) == score_bank(m)], default=0)

        TURN = []
        for i in range(TPB):
            TURN.append(max(OFF[i + 1], TURN[i - 1] + 2 if i else 0))
            assert i == 0 or TURN[i - 1] <= OFF[i + 1] - 1, "the context before is transposed before the next one is done"
        TURNED = {m: i for i, m in enumerate(TURN)}
        PROJECTED = {m + 1: i for i, m in enumerate(TURN)}
        END = TURN[-1] + 2

        block = ctx.enter_context(nc.Block())
        raw = k.raw
        shift_bc = prob[:, 1, 0:KC * B * P].rearrange("p (c b n) -> p c b n", c=KC, b=B)

        def width(t, ch):
            return min(GW, (t + 1) * P - ch * GW)

        def row(a, b):
            return a[:, bass.ds(b, 1), :].rearrange("p o d -> p (o d)")

        @block.gpsimd
        def _(pool):
            begin(pool, s["bo_done"], s["ve_done"], s["rstd_done"], k.x1_done)
            for b in range(B):
                pool.wait_ge(k.stats, START + b + 1)
                q = slice(b * TPB, (b + 1) * TPB)
                nc.gpsimd.tensor_scalar_add(ve[:, q], mv[:, q, 1], EPS).then_inc(s["ve_done"], 1)
                pool.wait_ge(s["ve_done"], START + b + 1)
                nc.gpsimd.tensor_tensor(rstd[:, q], ve[:, q], k.mhalf[:], ALU.pow).then_inc(s["rstd_done"], 1)
            with pool.Fori(0, B) as b:
                for g in range(GPB):
                    G = b * GPB + g
                    pool.wait_ge(s["z_done"], START + G + 1)
                    apart(k, pool)
                    for j in range(GT):
                        xt = row(k.x, G * GT + j)
                        last = nc.gpsimd.tensor_tensor(xt, xt, row(k.bo_gate, b), ALU.add)
                    last.then_inc(s["bo_done"], 1)
                pool.wait_ge(s["bo_done"], START + (b + 1) * GPB)
                for i, t in enumerate(ORDER):
                    pool.wait_ge(s["y_done"], START + b * TPB + i + 1)
                    xt = row(k.x, b * TPB + t)
                    apart(k, pool)
                    nc.gpsimd.tensor_tensor(xt, xt, y[:, i % 2], ALU.add).then_inc(k.x1_done, 1)

        @block.scalar
        def _(act):
            begin(act, s["w_hi"], s["hi_h"], s["qk_hi"], s["v_hi"], s["ct_hi"], s["exp_done"], s["pt_hi"])
            for i in range(4):
                act.wait_ge(w_in[i], 16)
                nc.scalar.copy(wh[:, i].rearrange("p c n -> p (c n)"), raw[:, i]).then_inc(s["w_hi"], 1)
            act.wait_ge(s["bias_done"], START + 1)

            def h_hi(b, g):
                G = b * GPB + g
                if g >= 2:
                    act.wait_ge(s["v_ready"], START + (G - 1) * 2)
                else:
                    act.wait_ge(s["v_ready"], START + b * GPB * 2)
                for c in range(KC):
                    act.wait_ge(s["zt_done"], START + G * KC + c + 1)
                    apart(k, act)
                    nc.scalar.activation(hh[:, g % 2, c], tp[:, c], ACT.Identity,
                                         scale=k.colmod[:, 0, 1, c, bass.ds(b, 1)]).then_inc(s["hi_h"], 1)

            def exp_of(b, m):
                i, ch = SEQ[m]
                t = ORDER[i]
                u, w = UNIT[t], width(t, ch)
                act.wait_ge(s["nmax_done"], START + b * TPB + i + 1)
                act.wait_ge(s["pt_ready"], START + b * CHB + (OFF[FROM[u - 1]] if u else 0))
                o = score_bank(m) * GW
                nc.scalar.activation(prob[:, u % 2, o:o + w], sc[:, score_bank(m), 0:w], ACT.Exp, bias=nmx[:, t:t + 1],
                                     scale=1.0 / 16, accum_out=rsc[:, t, ch:ch + 1]).then_inc(s["exp_done"], 1)

            with act.Fori(0, B) as b:
                h_hi(b, 0)
                for g in range(GPB):
                    G = b * GPB + g
                    if g + 1 < GPB:
                        h_hi(b, g + 1)
                    for i in range(4):
                        act.wait_ge(s["qk_ready"], START + G * 4 + i + 1)
                        act.wait_ge(s["s_ready"], START + b * CHB)
                        dst = (qh, kh)[i // 2][:, i % 2, g * GW:(g + 1) * GW]
                        apart(k, act)
                        nc.scalar.activation(dst, sc[:, i], ACT.Identity,
                                             bias=qkb[:, i // 2, i % 2, bass.ds(b, 1)]).then_inc(s["qk_hi"], 1)
                    for i in range(2):
                        act.wait_ge(s["pv_done"], START + b * CHB)
                        act.wait_ge(s["v_ready"], START + G * 2 + i + 1)
                        a = g * GT + 2 * i
                        nc.scalar.copy(vh[:, a:a + 2].rearrange("p t d -> p (t d)"), (cx, pj)[i][:]).then_inc(s["v_hi"], 1)

                def ct_hi(i):
                    act.wait_ge(s["ct_ready"], START + b * TPB + i + 1)
                    nc.scalar.copy(cth[:].rearrange("p c n -> p (c n)"), pj[:, 0:D]).then_inc(s["ct_hi"], 1)

                def pt_hi(m):
                    i, ch = SEQ[m]
                    w = width(ORDER[i], ch)
                    act.wait_ge(s["pt_ready"], START + b * CHB + m + 1)
                    act.wait_ge(s["pv_done"], START + b * CHB + max(m + 1 - RING, 0))
                    nc.scalar.copy(pth[:, m % RING, 0:w], tp[:, m % 2, 0:w]).then_inc(s["pt_hi"], 1)

                for m in chunks(0):
                    exp_of(b, m)
                pt_hi(0)
                for m in range(END):
                    if m + 1 < CHB:
                        pt_hi(m + 1)
                    if m in TURNED:
                        ct_hi(TURNED[m])
                    if m < CHB and STEP[m] in (1, 2):
                        for m2 in chunks(UNIT_OF[m] + 1, STEP[m] - 1):
                            exp_of(b, m2)

        @block.vector
        def _(v):
            begin(v, s["w_lo"], s["shift_bc"], s["bias_done"], s["dve1"], s["nmax_done"], s["ct_lo"], s["y_done"],
                  s["lo_h"], s["qk_lo"], s["v_lo"], s["pt_lo"], s["cn_done"], s["z_done"])
            DV = 5 * TPB
            for c in range(KC):
                for b in range(B):
                    last = nc.vector.tensor_copy(shift_bc[:, c, b], k.colmod[:, 0, 0, c, b:b + 1].to_broadcast([P, P]))
            last.then_inc(s["shift_bc"], 1)

            for i in range(4):
                v.wait_ge(s["w_hi"], START + i + 1)
                nc.vector.tensor_tensor(wl[:, i].rearrange("p c n -> p (c n)"), raw[:, i],
                                        wh[:, i].rearrange("p c n -> p (c n)"), ALU.subtract).then_inc(s["w_lo"], 1)
            v.wait_ge(k.stats, START + B)
            v.wait_ge(s["rstd_done"], START + B)
            v.wait_ge(s["bias_ready"], START + 1)
            for i, name in enumerate(("bq", "bk")):
                for c in range(KC):
                    nc.vector.tensor_scalar(qkb[:, i, c], sc[:, 0, (i * KC + c) * B:(i * KC + c + 1) * B], col(k, name, c), None, ALU.add)
            for b in range(B):
                last = nc.vector.tensor_tensor(vb[:, b], sc[:, 1, b * D:(b + 1) * D], k.rows[:, 0:D], ALU.add)
            last.then_inc(s["bias_done"], 1)

            with v.Fori(0, B) as b:
                chain = Counted(v, s["dve1"], b * DV)

                def h_lo(g):
                    for c in range(KC):
                        v.wait_ge(s["hi_h"], START + (b * GPB + g) * KC + c + 1)
                        nc.vector.scalar_tensor_tensor(out=hl[:, g % 2, c], in0=tp[:, c], scalar=k.colmod[:, 0, 1, c, bass.ds(b, 1)],
                                                       in1=hh[:, g % 2, c], op0=ALU.mult, op1=ALU.subtract).then_inc(s["lo_h"], 1)

                def normalise(g):
                    G = b * GPB + g
                    v.wait_ge(s["zt_done"], START + (b * GPB + max(g - 1, 0)) * KC)
                    for j in range(GT):
                        t = G * GT + j
                        last = nc.vector.tensor_scalar(z[:, g % 2, j], row(k.x, t), mv[:, bass.ds(t, 1), 0],
                                                       rstd[:, bass.ds(t, 1)], ALU.subtract, ALU.mult)
                    last.then_inc(s["z_done"], 1)

                normalise(0)
                normalise(1)
                h_lo(0)
                for g in range(GPB):
                    G = b * GPB + g
                    if g + 1 < GPB:
                        h_lo(g + 1)
                    if g + 2 < GPB:
                        normalise(g + 2)
                    for i in range(4):
                        v.wait_ge(s["qk_hi"], START + G * 4 + i + 1)
                        hi, lo = ((qh, ql), (kh, kl))[i // 2]
                        q = slice(g * GW, (g + 1) * GW)
                        nc.vector.scalar_tensor_tensor(out=lo[:, i % 2, q], in0=sc[:, i], scalar=qkb[:, i // 2, i % 2, bass.ds(b, 1)],
                                                       in1=hi[:, i % 2, q], op0=ALU.add, op1=ALU.subtract).then_inc(s["qk_lo"], 1)
                    for i in range(2):
                        v.wait_ge(s["v_hi"], START + G * 2 + i + 1)
                        a = g * GT + 2 * i
                        nc.vector.tensor_tensor(vl[:, a:a + 2].rearrange("p t d -> p (t d)"), (cx, pj)[i][:],
                                                vh[:, a:a + 2].rearrange("p t d -> p (t d)"), ALU.subtract).then_inc(s["v_lo"], 1)

                def maximum(m):
                    i, ch = SEQ[m]
                    t = ORDER[i]
                    v.wait_ge(s["s_ready"], START + b * CHB + m + 1)
                    if ch < NCH[t] - 1:
                        nc.vector.tensor_reduce(mxc[:, t, ch:ch + 1], sc[:, score_bank(m)], AX.X, ALU.max)
                        return
                    diag = sc[:, score_bank(m), (t % GT) * P:(t % GT + 1) * P]
                    chain.link(nc.vector.tensor_tensor(diag, diag, k.causal[:], ALU.add))
                    chain.link(nc.vector.tensor_reduce(mxc[:, t, ch:ch + 1], sc[:, score_bank(m), 0:width(t, ch)], AX.X, ALU.max))
                    chain.link(nc.vector.tensor_reduce(mx[:, t:t + 1], mxc[:, t, 0:NCH[t]], AX.X, ALU.max))
                    nc.vector.tensor_scalar(nmx[:, t:t + 1], mx[:, t:t + 1], -1.0 / 16, None, ALU.mult).then_inc(s["nmax_done"], 1)

                def ct_lo(i):
                    v.wait_ge(s["ct_hi"], START + b * TPB + i + 1)
                    nc.vector.tensor_tensor(ctl[:].rearrange("p c n -> p (c n)"), pj[:, 0:D],
                                            cth[:].rearrange("p c n -> p (c n)"), ALU.subtract).then_inc(s["ct_lo"], 1)

                def gated(i):
                    v.wait_ge(s["pj_ready"], START + b * TPB + i + 1)
                    v.wait_ge(k.x1_done, START + b * TPB + max(i - 1, 0))
                    nc.vector.tensor_tensor(y[:, i % 2], pj[:, 0:D], row(k.gate, b), ALU.mult).then_inc(s["y_done"], 1)

                def pt_lo(m):
                    i, ch = SEQ[m]
                    w = width(ORDER[i], ch)
                    v.wait_ge(s["pt_hi"], START + b * CHB + m + 1)
                    nc.vector.tensor_tensor(ptl[:, m % RING, 0:w], tp[:, m % 2, 0:w], pth[:, m % RING, 0:w],
                                            ALU.subtract).then_inc(s["pt_lo"], 1)

                for m in chunks(0):
                    maximum(m)
                pt_lo(0)
                for m in range(END):
                    if m < CHB and STEP[m] in (0, 1):
                        for m2 in chunks(UNIT_OF[m] + 1, STEP[m]):
                            maximum(m2)
                    if m + 1 < CHB:
                        pt_lo(m + 1)
                    if m in PROJECTED:
                        gated(PROJECTED[m])
                    if m in TURNED:
                        ct_lo(TURNED[m])
                    if m + 1 in OFF[1:]:
                        i = OFF.index(m + 1) - 1
                        t = ORDER[i]
                        v.wait_ge(s["exp_done"], START + b * CHB + OFF[i + 1])
                        chain.link(nc.vector.tensor_reduce(rsum[:, t:t + 1], rsc[:, t, 0:NCH[t]], AX.X, ALU.add))
                        chain.link(nc.vector.reciprocal(rinv[:, t:t + 1], rsum[:, t:t + 1]))
                        v.wait_ge(s["pv_done"], START + b * CHB + OFF[i + 1])
                        v.wait_ge(s["ct_ready"], START + b * TPB + i)
                        nc.vector.scalar_tensor_tensor(out=cn[:], in0=cx[:, 0:D], scalar=rinv[:, t:t + 1], in1=row(vb, b),
                                                       op0=ALU.mult, op1=ALU.add).then_inc(s["cn_done"], 1)
                assert chain.n == DV

        @block.tensor
        def _(pe):
            begin(pe, s["bias_ready"], s["s_ready"], s["ct_ready"], s["pj_ready"], s["pt_ready"], s["pv_done"],
                  s["qk_ready"], s["v_ready"], s["zt_done"])
            pe.wait_ge(s["shift_bc"], START + 1)
            for w in w_in[0:3]:
                pe.wait_ge(w, 16)
            for i in (WQ, WK):
                for c in range(KC):
                    for kc in range(KC):
                        o = (i * KC + c) * B
                        nc.tensor.matmul(sc[:, 0, o:o + B], raw[:, i, kc * D + c * P:kc * D + (c + 1) * P], k.colmod[:, 0, 0, kc],
                                         start=(kc == 0), stop=(kc == KC - 1))
            for b in range(B):
                for kc in range(KC):
                    last = nc.tensor.matmul(sc[:, 1, b * D:(b + 1) * D], shift_bc[:, kc, b], raw[:, WV, kc * D:(kc + 1) * D],
                                            start=(kc == 0), stop=(kc == KC - 1))
            last.then_inc(s["bias_ready"], 1)
            pe.wait_ge(s["bias_done"], START + 1)
            with pe.Fori(0, B) as b:
                def zt(g):
                    G = b * GPB + g
                    pe.wait_ge(s["lo_h"], START + G * KC)
                    if g == 0:
                        pe.wait_ge(s["pt_lo"], START + b * CHB)
                    for c in range(KC):
                        if c == 0:
                            pe.wait_ge(s["z_done"], START + G + 1)
                        for j in range(GT):
                            last = nc.tensor.transpose(tp[:, c, j * P:(j + 1) * P], z[:, g % 2, j, c * P:(c + 1) * P], k.ident[:])
                        last.then_inc(s["zt_done"], 1)

                zt(0)
                for g in range(GPB):
                    G = b * GPB + g
                    if g + 1 < GPB:
                        zt(g + 1)
                    pe.wait_ge(s["lo_h"], START + (G + 1) * KC)
                    if g == 0:
                        pe.wait_ge(s["exp_done"], START + b * CHB)
                        pe.wait_ge(s["w_lo"], START + 4)
                    hg, lg = hh[:, g % 2], hl[:, g % 2]
                    for i in range(4):
                        c = i % 2
                        pe.wait_ge(s["qk_lo"], START + G * 4 - 3 + i if g else START + b * GPB * 4)
                        for kc in range(KC):
                            m = slice(c * P, (c + 1) * P)
                            w = (WQ, WK)[i // 2]
                            last = three(nc.tensor, sc[:, i], wh[:, w, kc, m], wl[:, w, kc, m], hg[:, kc], lg[:, kc],
                                         kc == 0, kc == KC - 1)
                        last.then_inc(s["qk_ready"], 1)
                    if g == 0:
                        pe.wait_ge(s["y_done"], START + b * TPB)
                    for i in range(2):
                        pe.wait_ge(s["v_lo"], START + (G - 1) * 2 + i + 1 if g else START + b * GPB * 2)
                        bank = (cx, pj)[i]
                        for j in range(2):
                            q = slice((2 * i + j) * P, (2 * i + j + 1) * P)
                            for kc in range(KC):
                                last = three(nc.tensor, bank[:, j * D:(j + 1) * D], hg[:, kc, q], lg[:, kc, q],
                                             wh[:, WV, kc], wl[:, WV, kc], kc == 0, kc == KC - 1)
                        last.then_inc(s["v_ready"], 1)
                pe.wait_ge(s["qk_lo"], START + (b + 1) * GPB * 4)

                def scores(m):
                    i, ch = SEQ[m]
                    t = ORDER[i]
                    w = width(t, ch)
                    pe.wait_ge(s["exp_done"], START + b * CHB + freed(m))
                    for kc in range(KC):
                        q = slice(t * P, (t + 1) * P)
                        kk = slice(ch * GW, ch * GW + w)
                        last = three(nc.tensor, sc[:, score_bank(m), 0:w], qh[:, kc, q], ql[:, kc, q], kh[:, kc, kk], kl[:, kc, kk],
                                     kc == 0, kc == KC - 1)
                    last.then_inc(s["s_ready"], 1)

                def ct(i):
                    pe.wait_ge(s["cn_done"], START + b * TPB + i + 1)
                    pe.wait_ge(s["y_done"], START + b * TPB + i)
                    if i == 0:
                        pe.wait_ge(s["v_lo"], START + (b + 1) * GPB * 2)
                    for c in range(KC):
                        last = nc.tensor.transpose(pj[:, c * P:(c + 1) * P], cn[:, c * P:(c + 1) * P], k.ident[:])
                    last.then_inc(s["ct_ready"], 1)

                def project(i):
                    pe.wait_ge(s["ct_lo"], START + b * TPB + i + 1)
                    for kc in range(KC):
                        last = three(nc.tensor, pj[:, 0:D], cth[:, kc], ctl[:, kc], wh[:, WO, kc], wl[:, WO, kc],
                                     kc == 0, kc == KC - 1)
                    last.then_inc(s["pj_ready"], 1)

                def turn(m):
                    i, ch = SEQ[m]
                    pe.wait_ge(s["exp_done"], START + b * CHB + m + 1)
                    pe.wait_ge(s["pt_lo"], START + b * CHB + max(m - 1, 0))
                    for j in range(width(ORDER[i], ch) // P):
                        a = score_bank(m) * GW + j * P
                        last = nc.tensor.transpose(tp[:, m % 2, j * P:(j + 1) * P], prob[:, UNIT_OF[m] % 2, a:a + P], k.ident[:])
                    last.then_inc(s["pt_ready"], 1)

                def values(m):
                    i, ch = SEQ[m]
                    t = ORDER[i]
                    pe.wait_ge(s["pt_lo"], START + b * CHB + m + 1)
                    if ch == 0:
                        pe.wait_ge(s["cn_done"], START + b * TPB + i)
                        if i == 0:
                            pe.wait_ge(s["v_lo"], START + (b + 1) * GPB * 2)
                    nj = width(t, ch) // P
                    for j in range(nj):
                        a = ch * GT + j
                        q = slice(j * P, (j + 1) * P)
                        last = three(nc.tensor, cx[:, 0:D], pth[:, m % RING, q], ptl[:, m % RING, q], vh[:, a], vl[:, a],
                                     ch == 0 and j == 0, ch == NCH[t] - 1 and j == nj - 1)
                    last.then_inc(s["pv_done"], 1)

                for m in chunks(0):
                    scores(m)
                turn(0)
                for m in range(END):
                    if m < CHB and STEP[m] in (0, 1):
                        for m2 in chunks(UNIT_OF[m] + 1, STEP[m]):
                            scores(m2)
                    if m + 1 < CHB:
                        turn(m + 1)
                    if m < CHB:
                        values(m)
                    if m in PROJECTED:
                        project(PROJECTED[m])
                    if m in TURNED:
                        ct(TURNED[m])


def experts(nc, k, d):
    TOKENS = B * T
    KS = 2
    SLOTS = (KS * TOKENS + E * (P - 1)) // P + 1
    RING = 12
    SLOTS = -(-SLOTS // RING) * RING
    TPE = TOKENS // P
    LCOLS = -(-((E - 1) * TPE + SLOTS - TPE + 1) // P) * P
    EMPTY = KS * TOKENS
    SH = E
    with ExitStack() as ctx:
        sb = lambda n, s, t=F32: ctx.enter_context(nc.sbuf_tensor(n, s, t))
        sem = lambda n: k.stage_sem(nc, n)
        ps = lambda n, s: ctx.enter_context(nc.psum_tensor(n, s, F32))
        rows = nc.dram_tensor("h_rows", (TOKENS, D), F32).ap()
        lists = nc.dram_tensor("lists", (LCOLS * P, 2), F32).ap()
        results = nc.dram_tensor("results", (KS * TOKENS, D), F32).ap()
        guh, gul = sb("guh", [P, E + 1, KC, 2 * F], F32R), sb("gul", [P, E + 1, KC, 2 * F], F32R)
        dnh, dnl = sb("dnh", [P, E + 1, 2, D], F32R), sb("dnl", [P, E + 1, 2, D], F32R)
        raw_gu, raw_dn = sb("raw_gu", [P, KC, 2 * F]), sb("raw_dn", [P, 2, D])
        router = sb("router", [P, KC, E])
        hh, hl = sb("hh2", [P, KC, GW], F32R), sb("hl2", [P, KC, GW], F32R)
        act_g = sb("act_g", [P, 2, F])
        hid = sb("hid", [P, 2, 2 * P])
        hth, htl = sb("hth", [P, 2, 2 * P], F32R), sb("htl", [P, 2, 2 * P], F32R)
        y = sb("y2", [P, 4, D])
        ones, tri = sb("ones2", [P, P]), sb("tri", [P, P])
        iota_e = sb("iota_e", [P, GT, E])
        iota_i = sb("iota_i", [P, 2 * LCOLS], U32)
        token = sb("token", [P, KS, TILES])
        ebase = sb("ebase", [P, E])
        sig, sel = sb("sig", [P, GT, E]), sb("sel", [P, GT, E])
        best = sb("best", [P, GT, 8])
        place = sb("place", [P, GT, 8], U32)
        placef = sb("placef", [P, GT, KS])
        pick = sb("pick", [P, KS, GT, E])
        both = sb("both", [P, GT, E])
        taken = sb("taken", [P, E])
        gsum = sb("gsum", [P, E])
        wts, total = sb("wts", [P, GT, E]), sb("total", [P, GT])
        rank = sb("rank", [P, GT, E])
        tmp = sb("tmp2", [P, KS, GT, E])
        posf, posu = sb("posf", [P, KS, GT]), sb("posu", [P, KS, GT], U32)
        pack = sb("pack", [P, KS, GT, 2])
        m128, jj = sb("m128", [P, TPE]), sb("jj", [P, SLOTS])
        n_e, tiles_e, upto = sb("n_e", [P, E]), sb("tiles_e", [P, E]), sb("upto", [P, E])
        many = sb("many", [P, E, TPE])
        past, pastw = sb("past", [P, SLOTS, E - 1]), sb("pastw", [P, SLOTS, E - 1])
        exf, before, colf = sb("exf", [P, SLOTS]), sb("before", [P, SLOTS]), sb("colf", [P, SLOTS])
        exu, colu = sb("exu", [P, SLOTS], U32), sb("colu", [P, SLOTS], U32)
        lt = sb("lt", [P, RING, 2])
        dst, src = sb("dst", [P, RING], U32), sb("src", [P, RING], U32)
        gt = sb("gt", [P, 4, D])
        yb = sb("yb", [P, 2, KS, GT * D])
        pairs = yb[:].rearrange("p a b n -> p (a b n)").rearrange("p (r c t d) -> p r c t d", r=4, c=KS, t=2)
        both_results = results.rearrange("(c t p) d -> p c t d", c=KS, p=P)
        z = yb[:, 0, 0].rearrange("p (t d) -> p t d", t=GT)
        hb = yb[:, 0, 1].rearrange("p (t d) -> p t d", t=GT)
        hf = yb[:, 1, 0].rearrange("p (c n) -> p c n", c=KC)
        fill = yb[:, 1, 1, 0:2 * LCOLS].rearrange("p (c w) -> p c w", w=2)
        norm = Norm(nc, k, ctx, "n2", 0, 2, z)
        zp = ps("zp2", [P, 2, 512])
        gu = ps("gu", [P, 2, 512])
        tp, dp, lg, bk = (ps(n, [P, 512]) for n in ("tp2", "dp", "lg", "bk"))
        wgu_in, wdn_in = sem("m_wgu_in"), sem("m_wdn_in")
        lt_in = [sem(f"m_lt_in{i}") for i in range(RING)]
        gt_in = [sem(f"m_gt_in{i}") for i in range(4)]
        y_out = [sem(f"m_y_out{i}") for i in range(4)]
        yb_in = [sem(f"m_yb_in{i}") for i in range(4)]
        names = ("w_hi w_lo r_in const1 const2 lists_set h_f hi_h lo_h logits sig_done route chose ranked listed stored "
                 "hb_ready hb_done rows_out gu_ready silu_done hid_done ht_ready ht_hi ht_lo d_done y_done counted "
                 "table tabled conv src_done z_turned w_out sum_done gsum_done")
        s = {n: sem("m_" + n) for n in names.split()}
        block = ctx.enter_context(nc.Block())
        N1 = GROUPS * GT
        STEPS_ = N1 + SLOTS
        flat = lambda a: a.rearrange("p a b -> p (a b)")
        known = lambda G: isinstance(G, int)
        ROUTE = 10

        def of_expert(w, e):
            return w[e] if known(e) else w[bass.ds(e, 1)].rearrange("o r n -> (o r) n")

        def on_chip(a, e):
            return a[:, e] if known(e) else a[:, bass.ds(e, 1)].rearrange("p o c n -> p (o c) n")

        def through_slots(eng, step, lag):
            for j in range(RING):
                step(0, j, lambda d, j=j: j + d >= 0)
            with eng.Fori(1, SLOTS // RING - 1) as i:
                for q in range(RING):
                    step(i, q, lambda d: True)
            for j in range(SLOTS - RING, SLOTS + lag):
                step(j // RING, j % RING, lambda d, j=j: j + d < SLOTS)

        @block.sync
        def _(sp):
            sp.dma_start(router[:], d["router"].rearrange("(c p) e -> p c e", p=P)).then_inc(s["r_in"], 16)

            def weights(i, g, u, dn):
                sp.wait_ge(s["w_lo"], START + 2 * i)
                for j, w in enumerate((g, u)):
                    sp.dma_start(raw_gu[:, :, j * F:(j + 1) * F], w.rearrange("(c p) f -> p c f", p=P)).then_inc(wgu_in, 16)
                sp.dma_start(raw_dn[:, 0], dn[0:P]).then_inc(wdn_in, 16)
                sp.dma_start(raw_dn[0:F - P, 1], dn[P:F]).then_inc(wdn_in, 16)

            weights(0, d["wg_s"], d["wu_s"], d["wd_s"])
            sp.wait_ge(s["const2"], START + 1)
            sp.dma_start(lists.rearrange("(p c) w -> p (c w)", p=P), yb[:, 1, 1, 0:2 * LCOLS]).then_inc(s["lists_set"], 16)

            def body(G, prev, nxt, nxt2):
                weights(G + 1, *(of_expert(d[w], G) for w in ("wg", "wu", "wd")))
                sp.wait_ge(s["hb_done"], START + (G + 1) * 2)
                sp.dma_start(rows[bass.ds(G * GW, GW)].rearrange("(t p) d -> p t d", p=P), hb).then_inc(s["rows_out"], 16)

            through_groups(sp, body)
            sp.wait_ge(s["tabled"], START + 1)
            sp.wait_ge(s["listed"], 16 * KS * TILES)
            def part_of_list(i, q, has):
                j = i * RING + q
                if not known(j) or j >= RING:
                    sp.wait_ge(s["w_out"], START + j - RING + 1)
                c = sp.value_load(colu[0:1, j:j + 1] if known(j) else colu[0:1, bass.ds(j, 1)], min_val=0, max_val=LCOLS - 1)
                sp.dma_start(lt[:, q], lists[bass.ds(c * P, P)]).then_inc(lt_in[q], 16)

            through_slots(sp, part_of_list, 0)
            for r in range(4):
                sp.wait_ge(y_out[r], 16 * (SLOTS // 4))
            with sp.Fori(0, GROUPS // 2) as i:
                for r in range(4):
                    h = i * 4 + r
                    sp.wait_ge(k.x2_done, START + N1 + h - 3)
                    for c in range(KS):
                        sp.dma_start(pairs[:, r, c], both_results[:, c, bass.ds(h * 2, 2)]).then_inc(yb_in[r], 16)

        @block.gpsimd
        def _(pool):
            begin(pool, s["const1"], s["const2"], s["stored"], norm.ve_done, norm.rstd_done, k.x2_done)
            g = nc.gpsimd
            g.memset(ones[:], 1.0)
            g.memset(tri[:], 1.0)
            g.memset(taken[:], 0.0)
            g.memset(fill, 0.0)
            g.memset(hid[:], 0.0)
            g.iota(iota_i[:, 0:GT * E], pattern=[[0, GT], [1, E]], base=0, channel_multiplier=0).then_inc(s["const1"], 1)
            pool.wait_ge(s["const1"], START + 1)
            g.tensor_copy(iota_e[:].rearrange("p t e -> p (t e)"), iota_i[:, 0:GT * E])
            g.affine_select(out=tri[:], in_=tri[:], compare_op=ALU.is_ge, fill=0.0, base=-1, pattern=[[1, P]],
                            channel_multiplier=-1).then_inc(s["const1"], 1)
            norm.gpsimd(pool, 0)
            pool.wait_ge(s["const1"], START + 2)
            g.iota(iota_i[:, 0:KS * TILES], pattern=[[TOKENS, KS], [P, TILES]], base=0, channel_multiplier=1).then_inc(s["const1"], 1)
            pool.wait_ge(s["const1"], START + 3)
            g.tensor_copy(token[:].rearrange("p c t -> p (c t)"), iota_i[:, 0:KS * TILES]).then_inc(s["const1"], 1)
            pool.wait_ge(s["const1"], START + 4)
            g.iota(iota_i[:, 0:E], pattern=[[TOKENS, E]], base=0, channel_multiplier=0)
            g.iota(iota_i[:, E:E + TPE], pattern=[[P, TPE]], base=0, channel_multiplier=0)
            g.iota(iota_i[:, E + TPE:E + TPE + SLOTS], pattern=[[1, SLOTS]], base=0, channel_multiplier=0).then_inc(s["const1"], 1)
            pool.wait_ge(s["const1"], START + 5)
            g.tensor_copy(ebase[:], iota_i[:, 0:E])
            g.tensor_copy(m128[:], iota_i[:, E:E + TPE])
            g.tensor_copy(jj[:], iota_i[:, E + TPE:E + TPE + SLOTS]).then_inc(s["const1"], 1)
            pool.wait_ge(s["const1"], START + 6)
            g.iota(iota_i[:, 0:LCOLS], pattern=[[0, LCOLS // P], [1, P]], base=EMPTY, channel_multiplier=0).then_inc(s["const1"], 1)
            pool.wait_ge(s["const1"], START + 7)
            g.tensor_copy(fill[:, :, 0], iota_i[:, 0:LCOLS]).then_inc(s["const2"], 1)
            norm.gpsimd(pool, 1)
            pool.wait_ge(s["lists_set"], 16)

            def add(G, j):
                pool.wait_ge(s["y_done"], START + G * GT + j + 1)
                xt = norm.tile(G * GT + j)
                apart(k, pool)
                nc.gpsimd.tensor_tensor(xt, xt, y[:, j], ALU.add).then_inc(k.x2_done, 1)

            def enlist(G):
                pool.wait_ge(s["ranked"], START + G + 1)
                apart(k, pool)
                for c in range(KS):
                    for j in range(GT):
                        nc.gpsimd.indirect_dma_start(lists, bass.IndirectOffsetOnAxis(ap=posu[:, c, j:j + 1], axis=0),
                                                     pack[:, c, j], None).then_inc(s["listed"], 16)

            def body(G, prev, nxt, nxt2):
                if prev:
                    enlist(G - 1)
                    add(G - 1, 2)
                    add(G - 1, 3)
                add(G, 0)
                if nxt2:
                    norm.gpsimd(pool, G + 2)
                add(G, 1)
                if prev:
                    pool.wait_ge(s["listed"], G * (16 * KS * GT))
                    pool.sem_inc(s["stored"], 1)

            through_groups(pool, body)
            enlist(GROUPS - 1)
            add(GROUPS - 1, 2)
            add(GROUPS - 1, 3)
            pool.wait_ge(s["rows_out"], 16 * GROUPS)

            def step(i, q, has):
                j = i * RING + q
                if has(3):
                    if has(-1):
                        pool.wait_ge(s["z_turned"], START + j)
                    pool.wait_ge(s["src_done"], START + j + 3 + 1)
                    apart(k, pool)
                    nc.gpsimd.indirect_dma_start(gt[:, (q + 3) % 4], None, rows,
                                                 bass.IndirectOffsetOnAxis(ap=src[:, (q + 3) % RING:(q + 3) % RING + 1], axis=0)
                                                 ).then_inc(gt_in[(q + 3) % 4], 16)
                if has(-3):
                    pool.wait_ge(s["w_out"], START + j - 3 + 1)
                    apart(k, pool)
                    r = (q - 3) % RING
                    nc.gpsimd.indirect_dma_start(results, bass.IndirectOffsetOnAxis(ap=dst[:, r:r + 1], axis=0), y[:, (q - 3) % 4], None,
                                                 bounds_check=KS * TOKENS - 1, oob_is_err=False).then_inc(y_out[(q - 3) % 4], 16)

            for j in range(3):
                pool.wait_ge(s["src_done"], START + j + 1)
                nc.gpsimd.indirect_dma_start(gt[:, j], None, rows, bass.IndirectOffsetOnAxis(ap=src[:, j:j + 1], axis=0)
                                             ).then_inc(gt_in[j], 16)
            through_slots(pool, step, 3)
            with pool.Fori(0, GROUPS // 2) as i:
                for r in range(4):
                    pool.wait_ge(s["gsum_done"], START + i * 4 + r + 1)
                    apart(k, pool)
                    xt = k.x[:, bass.ds(i * 8 + 2 * r, 2)]
                    nc.gpsimd.tensor_tensor(xt, xt, pairs[:, r, 0], ALU.add).then_inc(k.x2_done, 1)

        def hi_of_weights(act, i, e):
            act.wait_ge(wgu_in, 32 * (i + 1))
            nc.scalar.copy(on_chip(guh, e), raw_gu[:]).then_inc(s["w_hi"], 1)
            act.wait_ge(wdn_in, 32 * (i + 1))
            nc.scalar.copy(on_chip(dnh, e)[:, 0], raw_dn[:, 0])
            nc.scalar.copy(on_chip(dnh, e)[0:F - P, 1], raw_dn[0:F - P, 1]).then_inc(s["w_hi"], 1)

        def lo_of_weights(v, i, e):
            v.wait_ge(s["w_hi"], START + 2 * i + 1)
            nc.vector.tensor_tensor(on_chip(gul, e), raw_gu[:], on_chip(guh, e), ALU.subtract).then_inc(s["w_lo"], 1)
            v.wait_ge(s["w_hi"], START + 2 * i + 2)
            nc.vector.tensor_tensor(on_chip(dnl, e)[:, 0], raw_dn[:, 0], on_chip(dnh, e)[:, 0], ALU.subtract)
            m = F - P
            nc.vector.tensor_tensor(on_chip(dnl, e)[0:m, 1], raw_dn[0:m, 1], on_chip(dnh, e)[0:m, 1],
                                    ALU.subtract).then_inc(s["w_lo"], 1)

        @block.scalar
        def _(act):
            begin(act, s["w_hi"], s["h_f"], s["hi_h"], s["sig_done"], s["silu_done"], s["ht_hi"], s["hb_done"], s["w_out"])

            def silu(n, r, old):
                act.wait_ge(s["gu_ready"], START + n + 1)
                if old:
                    act.wait_ge(s["hid_done"], START + n - 1)
                nc.scalar.activation(act_g[:, r], gu[:, r, 0:F], ACT.Silu).then_inc(s["silu_done"], 1)

            def ht_hi(n, r, old):
                act.wait_ge(s["ht_ready"], START + n + 1)
                if old:
                    act.wait_ge(s["d_done"], START + n - 1)
                nc.scalar.copy(hth[:, r], tp[:, 0:2 * P]).then_inc(s["ht_hi"], 1)

            def h_of(G, c):
                act.wait_ge(norm.zt_done, START + G * KC + c + 1)
                act.wait_ge(s["lo_h"], START + G * KC)
                act.wait_ge(s["hb_ready"], START + G * 2)
                m = k.colmod
                b = G // GPB
                scale, shift = ((m[:, 0, 3, c, b:b + 1], m[:, 0, 2, c, b:b + 1]) if known(G) else
                                (m[:, 0, 3, c, bass.ds(b, 1)], m[:, 0, 2, c, bass.ds(b, 1)]))
                apart(k, act)
                nc.scalar.activation(hf[:, c], zp[:, c], ACT.Identity, bias=shift, scale=scale).then_inc(s["h_f"], 1)

            def sigmoid(G):
                act.wait_ge(s["logits"], START + G + 1)
                act.wait_ge(s["route"], START + G * ROUTE)
                nc.scalar.activation(sig[:].rearrange("p t e -> p (t e)"), bk[:, 0:GT * E], ACT.Sigmoid).then_inc(s["sig_done"], 1)

            h_of(0, 0)
            h_of(0, 1)
            hi_of_weights(act, 0, SH)

            def body(G, prev, nxt, nxt2):
                act.wait_ge(s["h_f"], START + (G + 1) * KC)
                for c in range(KC):
                    act.wait_ge(s["gu_ready"], START + G * GT)
                    nc.scalar.copy(hh[:, c], hf[:, c]).then_inc(s["hi_h"], 1)
                sigmoid(G)
                for i in range(2):
                    act.wait_ge(s["hb_ready"], START + G * 2 + i + 1)
                    if prev:
                        act.wait_ge(s["rows_out"], 16 * G)
                    nc.scalar.copy(hb[:, 2 * i:2 * i + 2].rearrange("p t d -> p (t d)"), bk[:]).then_inc(s["hb_done"], 1)
                for j in range(GT):
                    n = G * GT + j
                    silu(n, j % 2, prev or j >= 2)
                    if prev or j >= 1:
                        ht_hi(n - 1, (j - 1) % 2, prev or j >= 3)
                    if j == 0:
                        if nxt:
                            h_of(G + 1, 0)
                            h_of(G + 1, 1)
                    if j == 1:
                        hi_of_weights(act, G + 1, G)

            through_groups(act, body)
            ht_hi(N1 - 1, 1, True)

            def h_hi(j, q):
                act.wait_ge(s["z_turned"], START + j + 1)
                if not known(j) or j >= 2:
                    act.wait_ge(s["gu_ready"], START + N1 + j - 1)
                r = q % 2
                nc.scalar.copy(hh[:, :, r * P:(r + 1) * P], zp[:, r, 0:D].rearrange("p (c n) -> p c n", c=KC)).then_inc(s["hi_h"], 1)

            def step(i, q, has):
                j = i * RING + q
                if has(1):
                    h_hi(j + 1, q + 1)
                if has(0):
                    silu(N1 + j, q % 2, True)
                if has(-1):
                    ht_hi(N1 + j - 1, (q - 1) % 2, True)
                if has(-2):
                    act.wait_ge(s["d_done"], START + N1 + j - 2 + 1)
                    r = (q - 2) % 4
                    if not known(j) or j - 2 >= 4:
                        act.wait_ge(y_out[r], (i * (RING // 4) + (q - 2) // 4) * 16)
                    nc.scalar.activation(y[:, r], dp[:, 0:D], ACT.Identity, scale=lt[:, (q - 2) % RING, 1:2]).then_inc(s["w_out"], 1)

            act.wait_ge(k.x2_done, START + N1)
            h_hi(0, 0)
            through_slots(act, step, 2)

        @block.vector
        def _(v):
            begin(v, s["lo_h"], s["route"], s["chose"], s["ranked"], s["hid_done"], s["ht_lo"], s["y_done"],
                  s["w_lo"], s["table"], s["tabled"], s["conv"], s["src_done"], s["sum_done"], s["gsum_done"],
                  norm.bn_done, norm.stats, norm.z_done)
            vec = nc.vector

            def route1(G):
                c = Counted(v, s["route"], G * ROUTE)
                v.wait_ge(s["sig_done"], START + G + 1)
                v.wait_ge(s["ranked"], START + G)
                c.link(vec.tensor_tensor(sel[:], sig[:], k.rows[:, 2 * D:2 * D + E].unsqueeze(1).to_broadcast([P, GT, E]), ALU.add), k)
                for j in range(GT):
                    last = vec.max(best[:, j], sel[:, j])
                c.link(last, k)
                for j in range(GT):
                    last = vec.max_index(place[:, j], best[:, j], sel[:, j])
                c.link(last)
                c.link(vec.tensor_copy(placef[:], place[:, :, 0:KS]))
                for i in range(KS):
                    last = vec.tensor_tensor(pick[:, i], iota_e[:], placef[:, :, i:i + 1].to_broadcast([P, GT, E]), ALU.is_equal)
                c.link(last)
                vec.tensor_tensor(both[:], pick[:, 0], pick[:, 1], ALU.add).then_inc(s["chose"], 1)
                return c

            def route2(G, c):
                v.wait_ge(s["chose"], START + G + 1)
                c.link(vec.tensor_tensor(wts[:], both[:], sig[:], ALU.mult))
                c.link(vec.tensor_reduce(total[:], wts[:], AX.X, ALU.add))
                c.link(vec.tensor_scalar_add(total[:], total[:], 1e-20))
                c.link(vec.reciprocal(total[:], total[:]))
                c.link(vec.tensor_tensor(wts[:], wts[:], total[:].unsqueeze(2).to_broadcast([P, GT, E]), ALU.mult))
                assert c.n == ROUTE, c.n

            def rank_of(G):
                v.wait_ge(s["counted"], START + G + 1)
                c = Counted(v, s["conv"], G * 7)
                c.link(vec.tensor_tensor(tmp[:], pick[:], wts[:].unsqueeze(1).to_broadcast([P, KS, GT, E]), ALU.mult))
                v.wait_ge(s["stored"], START + G)
                apart(k, v)
                c.link(vec.tensor_reduce(pack[:, :, :, 1], tmp[:], AX.X, ALU.add))
                c.link(vec.tensor_tensor(rank[:], lg[:, 0:GT * E].rearrange("p (t e) -> p t e", t=GT),
                                         ebase[:].unsqueeze(1).to_broadcast([P, GT, E]), ALU.add))
                c.link(vec.tensor_tensor(tmp[:], pick[:], rank[:].unsqueeze(1).to_broadcast([P, KS, GT, E]), ALU.mult))
                c.link(vec.tensor_reduce(posf[:], tmp[:], AX.X, ALU.add))
                vec.tensor_copy(posu[:], posf[:])
                c.link(vec.tensor_copy(pack[:, :, :, 0], token[:, :, bass.ds(G * GT, GT)]))
                c.link(vec.tensor_reduce(gsum[:], both[:].rearrange("p t e -> p e t"), AX.X, ALU.add))
                vec.tensor_tensor(taken[:], taken[:], gsum[:], ALU.add).then_inc(s["ranked"], 1)
                v.wait_ge(s["ranked"], START + G + 1)

            def hl_of(G, c):
                v.wait_ge(s["hi_h"], START + G * KC + c + 1)
                vec.tensor_tensor(hl[:, c], hf[:, c], hh[:, c], ALU.subtract).then_inc(s["lo_h"], 1)

            def hidden(n, r, old):
                v.wait_ge(s["silu_done"], START + n + 1)
                if old:
                    v.wait_ge(s["ht_ready"], START + n - 1)
                vec.tensor_tensor(hid[:, r, 0:F], act_g[:, r], gu[:, r, F:2 * F], ALU.mult).then_inc(s["hid_done"], 1)

            def ht_lo(n, r):
                v.wait_ge(s["ht_hi"], START + n + 1)
                vec.tensor_tensor(htl[:, r], tp[:, 0:2 * P], hth[:, r], ALU.subtract).then_inc(s["ht_lo"], 1)

            def gated(G, j):
                v.wait_ge(s["d_done"], START + G * GT + j + 1)
                if not known(G) or G:
                    v.wait_ge(k.x2_done, START + G * GT + j - 2)
                b = G // GPB
                vec.tensor_tensor(y[:, j], dp[:, 0:D], k.gate[:, bass.ds(b + 2, 1), :].rearrange("p o d -> p (o d)"),
                                  ALU.mult).then_inc(s["y_done"], 1)

            norm.vector_stats(v, 0, 0)
            norm.vector_z(v, 0, 0)
            norm.vector_stats(v, 1, GT)
            lo_of_weights(v, 0, SH)
            norm.vector_z(v, 1, GT)
            v.wait_ge(s["const2"], START + 1)

            def body(G, prev, nxt, nxt2):
                hl_of(G, 0)
                hl_of(G, 1)
                if prev:
                    rank_of(G - 1)
                    if nxt:
                        norm.vector_z(v, G + 1, (G + 1) * GT)
                c = route1(G)
                for j in range(GT):
                    n = G * GT + j
                    hidden(n, j % 2, prev or j >= 2)
                    if prev or j >= 1:
                        ht_lo(n - 1, (j - 1) % 2)
                    if j >= 2:
                        gated(G, j - 2)
                    elif prev:
                        gated(G - 1, j + 2)
                    if j == 0:
                        route2(G, c)
                    if j == 1:
                        lo_of_weights(v, G + 1, G)
                    if j == 2 and nxt2:
                        norm.vector_stats(v, G + 2, (G + 2) * GT)

            through_groups(v, body)
            rank_of(GROUPS - 1)
            ht_lo(N1 - 1, 1)
            gated(GROUPS - 1, 2)
            gated(GROUPS - 1, 3)

            c = Counted(v, s["table"])
            v.wait_ge(s["counted"], START + GROUPS + 1)
            c.link(vec.tensor_copy(n_e[:], lg[:, 0:E]))
            c.link(vec.tensor_tensor(many[:], n_e[:].unsqueeze(2).to_broadcast([P, E, TPE]),
                                     m128[:].unsqueeze(1).to_broadcast([P, E, TPE]), ALU.is_gt))
            c.link(vec.tensor_reduce(tiles_e[:], many[:], AX.X, ALU.add))
            c.link(vec.tensor_tensor_scan(upto[:], ones[:, 0:E], tiles_e[:], 0.0, ALU.mult, ALU.add))
            c.link(vec.tensor_tensor(past[:], jj[:].unsqueeze(2).to_broadcast([P, SLOTS, E - 1]),
                                     upto[:, 0:E - 1].unsqueeze(1).to_broadcast([P, SLOTS, E - 1]), ALU.is_ge))
            vec.tensor_reduce(exf[:], past[:], AX.X, ALU.add)
            c.link(vec.tensor_tensor(pastw[:], past[:], tiles_e[:, 0:E - 1].unsqueeze(1).to_broadcast([P, SLOTS, E - 1]), ALU.mult))
            c.link(vec.tensor_reduce(before[:], pastw[:], AX.X, ALU.add))
            c.link(vec.scalar_tensor_tensor(out=colf[:], in0=exf[:], scalar=float(TPE), in1=jj[:], op0=ALU.mult, op1=ALU.add))
            c.link(vec.tensor_tensor(colf[:], colf[:], before[:], ALU.subtract))
            vec.tensor_copy(exu[:], exf[:])
            vec.tensor_copy(colu[:], colf[:]).then_inc(s["tabled"], 1)

            def convert(j, q):
                r = q % RING
                v.wait_ge(lt_in[r], 16 * (j // RING + 1))
                if not known(j) or j >= RING:
                    v.wait_ge(y_out[r % 4], 16 * ((j - RING) // 4 + 1))
                apart(k, v)
                vec.tensor_copy(dst[:, r:r + 1], lt[:, r, 0:1]).then_inc(s["sum_done"], 1)
                v.wait_ge(s["sum_done"], START + j + 1)
                vec.tensor_scalar(src[:, r:r + 1], dst[:, r:r + 1], TOKENS - 1, None, ALU.bitwise_and).then_inc(s["src_done"], 1)

            def h_lo(j, q):
                r = q % 2
                v.wait_ge(s["hi_h"], START + GROUPS * KC + j + 1)
                vec.tensor_tensor(hl[:, :, r * P:(r + 1) * P], zp[:, r, 0:D].rearrange("p (c n) -> p c n", c=KC),
                                  hh[:, :, r * P:(r + 1) * P], ALU.subtract).then_inc(s["lo_h"], 1)

            def step(i, q, has):
                j = i * RING + q
                if has(1):
                    h_lo(j + 1, q + 1)
                if has(0):
                    hidden(N1 + j, q % 2, True)
                if has(4):
                    convert(j + 4, q + 4)
                if has(-1):
                    ht_lo(N1 + j - 1, (q - 1) % 2)

            for j in range(4):
                convert(j, j)
            h_lo(0, 0)
            through_slots(v, step, 1)
            with v.Fori(0, GROUPS // 2) as i:
                for r in range(4):
                    v.wait_ge(yb_in[r], (i + 1) * (16 * KS))
                    apart(k, v)
                    vec.tensor_tensor(pairs[:, r, 0], pairs[:, r, 0], pairs[:, r, 1], ALU.add).then_inc(s["sum_done"], 1)
                    v.wait_ge(s["sum_done"], START + SLOTS + i * 4 + r + 1)
                    apart(k, v)
                    vec.tensor_tensor(pairs[:, r, 0], pairs[:, r, 0], k.gate[:, bass.ds(i // (GPB // 2) + 2, 1)].to_broadcast([P, 2, D]),
                                      ALU.mult).then_inc(s["gsum_done"], 1)

        @block.tensor
        def _(pe):
            begin(pe, s["logits"], s["counted"], s["hb_ready"], s["gu_ready"], s["ht_ready"], s["d_done"], s["z_turned"], norm.zt_done)

            def turn_z(G):
                for c in range(KC):
                    pe.wait_ge(s["h_f"], START + G * KC)
                    norm.tensor(pe, G, c, zp[:, c])

            def up(n, stat, e, r, old):
                if old:
                    pe.wait_ge(s["hid_done"], START + n - 1)
                for kc in range(KC):
                    w = [a[:, e, kc] if known(e) else a[:, bass.ds(e, 1), kc].rearrange("p o n -> p (o n)") for a in (guh, gul)]
                    last = three(nc.tensor, gu[:, r, 0:2 * F], hh[:, kc, stat], hl[:, kc, stat], w[0], w[1], kc == 0, kc == KC - 1)
                last.then_inc(s["gu_ready"], 1)

            def turn(n, r, old):
                pe.wait_ge(s["hid_done"], START + n + 1)
                if old:
                    pe.wait_ge(s["ht_lo"], START + n)
                nc.tensor.transpose(tp[:, 0:P], hid[:, r, 0:P], k.ident[:])
                nc.tensor.transpose(tp[:, P:2 * P], hid[:, r, P:2 * P], k.ident[:]).then_inc(s["ht_ready"], 1)

            def down(n, e, r, freed, count):
                pe.wait_ge(s["ht_lo"], START + n + 1)
                pe.wait_ge(freed, count)
                for c, m in enumerate((P, F - P)):
                    q = slice(c * P, (c + 1) * P)
                    w = [a[0:m, e, c] if known(e) else a[0:m, bass.ds(e, 1), c].rearrange("p o n -> p (o n)") for a in (dnh, dnl)]
                    last = three(nc.tensor, dp[:, 0:D], hth[0:m, r, q], htl[0:m, r, q], w[0], w[1], c == 0, c == 1)
                last.then_inc(s["d_done"], 1)

            pe.wait_ge(s["const1"], START + 2)
            def logits(G):
                pe.wait_ge(s["h_f"], START + (G + 1) * KC)
                pe.wait_ge(s["hb_done"], START + G * 2)
                for j in range(GT):
                    for kc in range(KC):
                        last = nc.tensor.matmul(bk[:, j * E:(j + 1) * E], hf[:, kc, j * P:(j + 1) * P], router[:, kc],
                                                start=(kc == 0), stop=(kc == KC - 1))
                last.then_inc(s["logits"], 1)

            turn_z(0)
            pe.wait_ge(s["r_in"], 16)
            logits(0)
            pe.wait_ge(s["w_lo"], START + 2)

            def body(G, prev, nxt, nxt2):
                for i in range(2):
                    pe.wait_ge(s["sig_done"], START + G + 1)
                    pe.wait_ge(s["hb_done"], START + G * 2 + i)
                    for j in range(2):
                        for c in range(KC):
                            t = 2 * i + j
                            last = nc.tensor.transpose(bk[:, j * D + c * P:j * D + (c + 1) * P], hf[:, c, t * P:(t + 1) * P], k.ident[:])
                    last.then_inc(s["hb_ready"], 1)
                pe.wait_ge(s["lo_h"], START + (G + 1) * KC)
                for j in range(GT):
                    n = G * GT + j
                    up(n, slice(j * P, (j + 1) * P), SH, j % 2, prev or j >= 2)
                    if prev or j >= 1:
                        turn(n - 1, (j - 1) % 2, prev or j >= 2)
                    if prev or j >= 2:
                        down(n - 2, SH, j % 2, s["y_done"], START + n - 2)
                    if j == 0 and nxt:
                        turn_z(G + 1)
                    if j == 2:
                        pe.wait_ge(s["chose"], START + G + 1)
                        pe.wait_ge(s["ranked"], START + G)
                        nc.tensor.matmul(lg[:, 0:GT * E], tri[:], both[:].rearrange("p t e -> p (t e)"), start=True, stop=False)
                        for t in range(GT - 1):
                            nc.tensor.matmul(lg[:, (t + 1) * E:GT * E], ones[:],
                                             both[:, t].unsqueeze(1).to_broadcast([P, GT - 1 - t, E]), start=False, stop=False)
                        nc.tensor.matmul(lg[:, 0:GT * E], ones[:], taken[:].unsqueeze(1).to_broadcast([P, GT, E]),
                                         start=False, stop=True).then_inc(s["counted"], 1)
                        if nxt:
                            logits(G + 1)

            through_groups(pe, body)
            pe.wait_ge(s["ranked"], START + GROUPS)
            nc.tensor.matmul(lg[:, 0:E], ones[:], taken[:], start=True, stop=True).then_inc(s["counted"], 1)
            turn(N1 - 1, 1, True)
            down(N1 - 2, SH, 0, s["y_done"], START + N1 - 2)
            down(N1 - 1, SH, 1, s["y_done"], START + N1 - 1)
            pe.wait_ge(s["tabled"], START + 1)
            pe.wait_ge(s["w_lo"], START + 2 * (E + 1))
            pe.wait_ge(s["y_done"], START + N1)

            def turn_g(j, q):
                pe.wait_ge(gt_in[q % 4], 16 * (j // 4 + 1))
                if not known(j) or j >= 2:
                    pe.wait_ge(s["lo_h"], START + GROUPS * KC + j - 1)
                for c in range(KC):
                    last = nc.tensor.transpose(zp[:, q % 2, c * P:(c + 1) * P], gt[:, q % 4, c * P:(c + 1) * P], k.ident[:])
                last.then_inc(s["z_turned"], 1)

            def expert(j):
                return pe.value_load(exu[0:1, j:j + 1] if known(j) else exu[0:1, bass.ds(j, 1)], min_val=0, max_val=E - 1)

            at = {}

            def step(i, q, has):
                j = i * RING + q
                if q == 0:
                    for d in (-2, -1, 0):
                        if has(d):
                            at[d] = expert(j + d)
                if has(1):
                    turn_g(j + 1, q + 1)
                if has(0):
                    pe.wait_ge(s["lo_h"], START + GROUPS * KC + j + 1)
                    up(N1 + j, slice(q % 2 * P, (q % 2 + 1) * P), at[q], q % 2, True)
                if has(1) and q + 1 < RING:
                    at[q + 1] = expert(j + 1)
                if has(-1):
                    turn(N1 + j - 1, (q - 1) % 2, True)
                if has(-2):
                    down(N1 + j - 2, at[q - 2], q % 2, s["w_out"], START + j - 2)

            turn_g(0, 0)
            through_slots(pe, step, 2)


def first_column(G):
    return (G % GPB) * GW


class Shifted:

    def __init__(self, nc, k, ctx, name, mixes):
        self.nc, self.k, self.mixes = nc, k, mixes
        sb = lambda n, s, t=F32: ctx.enter_context(nc.sbuf_tensor(n + name, s, t))
        n = len(mixes)
        self.one_minus = sb("one_minus", [P, KC, n])
        self.scaled = sb("scaled", [P, n, 2, KC, D])
        self.wh, self.wl = sb("wmh", [P, n, 2, KC, D], F32R), sb("wml", [P, n, 2, KC, D], F32R)
        self.hh, self.hl = sb("hh", [P, KC, T + 1], F32R), sb("hl", [P, KC, T + 1], F32R)
        self.h = sb("h", [P, KC, GW])
        self.zero = sb("zero", [P, KC])
        sem = lambda n: ctx.enter_context(nc.semaphore(n + name))
        self.om_done, self.scaled_done, self.w_hi, self.w_lo, self.zeroed, self.hi_h, self.lo_h = (
            sem(n) for n in ("om_done", "scaled_done", "w_hi", "w_lo", "zeroed", "hi_h", "lo_h"))

    def gpsimd(self, pool, raw, w_in):
        nc = self.nc
        nc.gpsimd.memset(self.zero[:], 0.0).then_inc(self.zeroed, 1)
        for i, mix in enumerate(self.mixes):
            last = nc.gpsimd.tensor_scalar(self.one_minus[:, :, i:i + 1], self.k.cols[:, :, COL[mix]:COL[mix] + 1], -1.0, 1.0,
                                           ALU.mult, ALU.add)
        last.then_inc(self.om_done, 1)
        pool.wait_ge(self.om_done, START + 1)
        for i, mix in enumerate(self.mixes):
            pool.wait_ge(w_in[i], 16)
            for c in range(KC):
                nc.gpsimd.tensor_scalar_mul(self.scaled[:, i, 0, c], raw[:, i, c], col(self.k, mix, c))
                last = nc.gpsimd.tensor_scalar_mul(self.scaled[:, i, 1, c], raw[:, i, c], self.one_minus[:, c, i:i + 1])
            last.then_inc(self.scaled_done, 1)

    def scalar_weights(self, act, i):
        act.wait_ge(self.scaled_done, START + i + 1)
        self.nc.scalar.copy(self.wh[:, i], self.scaled[:, i]).then_inc(self.w_hi, 1)

    def scalar_zero(self, act):
        act.wait_ge(self.zeroed, START + 1)
        self.nc.scalar.copy(self.hh[:, :, 0], self.zero[:])
        self.nc.scalar.copy(self.hl[:, :, 0], self.zero[:]).then_inc(self.zeroed, 1)

    def vector_weights(self, v, i):
        v.wait_ge(self.w_hi, START + i + 1)
        self.nc.vector.tensor_tensor(self.wl[:, i], self.scaled[:, i], self.wh[:, i], ALU.subtract).then_inc(self.w_lo, 1)

    def modulation(self, norm, G, c):
        m = self.k.colmod
        if isinstance(G, int):
            b = G // GPB
            return [m[:, norm.layer, norm.shift + i, c, b:b + 1] for i in range(2)]
        return [m[:, norm.layer, norm.shift + i, c, bass.ds(G // GPB, 1)] for i in range(2)]

    def place(self, a, c, G, ahead):
        return a[:, c, bass.ds(first_column(G) + ahead, GW)]

    def scalar_h(self, act, norm, G, c, zt):
        act.wait_ge(norm.zt_done, START + G * KC + c + 1)
        act.wait_ge(self.lo_h, START + G * KC)
        shift, scale = self.modulation(norm, G, c)
        apart(self.k, act)
        self.nc.scalar.activation(self.h[:, c], zt, ACT.Identity, bias=shift, scale=scale)
        self.nc.scalar.activation(self.place(self.hh, c, G, 1), zt, ACT.Identity, bias=shift, scale=scale).then_inc(self.hi_h, 1)

    def vector_h(self, v, G, c):
        v.wait_ge(self.hi_h, START + G * KC + c + 1)
        apart(self.k, v)
        self.nc.vector.tensor_tensor(self.place(self.hl, c, G, 1), self.h[:, c], self.place(self.hh, c, G, 1),
                                     ALU.subtract).then_inc(self.lo_h, 1)

    def tensor(self, out, i, m, G):
        for kc in range(KC):
            for which, ahead in ((0, 1), (1, 0)):
                last = three(self.nc.tensor, out, self.wh[:, i, which, kc, m], self.wl[:, i, which, kc, m],
                             self.place(self.hh, kc, G, ahead), self.place(self.hl, kc, G, ahead),
                             kc == 0 and which == 0, kc == KC - 1 and which == 1)
        return last


def time_mixing(nc, k, d):
    with ExitStack() as ctx:
        sb = lambda n, s, t=F32: ctx.enter_context(nc.sbuf_tensor(n, s, t))
        sem = lambda n: ctx.enter_context(nc.semaphore(n))
        ps = lambda n, s: ctx.enter_context(nc.psum_tensor(n, s, F32))
        K_, V_, R_ = range(3)
        raw = sb("raw3", [P, 4, KC, D])
        mix = Shifted(nc, k, ctx, "3", ("mix_k", "mix_v", "mix_r"))
        wo = sb("wo3", [P, KC, D])
        wog = sb("wog3", [P, B, KC, D])
        woh, wol = sb("woh3", [P, B, KC, D], F32R), sb("wol3", [P, B, KC, D], F32R)
        ones = sb("ones3", [P, P])
        lnb = sb("lnb3", [P, KC, P])
        bias = sb("bias3", [P, B, D])
        ks = sb("ks3", [P, KC, GW])
        kv = sb("kv3", [P, GW])
        st = sb("st3", [P, GW])
        states = sb("states3", [P, KC, GROUPS + B])
        dec = sb("dec3", [P, KC])
        fo = sb("fo3", [P, GW])
        o = sb("o3", [P, KC, GW])
        oh, ol = sb("oh3", [P, KC, GW], F32R), sb("ol3", [P, KC, GW], F32R)
        obn, omv, ove, orstd = sb("obn3", [P, GT, 6]), sb("omv3", [P, GT, 2]), sb("ove3", [P, GT]), sb("orstd3", [P, GT])
        norm = Norm(nc, k, ctx, "n3", 1, 0)
        kvr = ps("kvr", [P, 6, 512])
        ring = ps("ring3", [P, 2, 512])
        w_in = [sem(f"t_w_in{i}") for i in range(4)]
        names = ("wog_done centred ones_done sums_ready wo_hi wo_lo dec_done kvr_ready ks_done kv_done o_done "
                 "hi_o lo_o ot_ready obn_done ostats ove_done orstd_done out_ready bias_added dve3 init3")
        s = {n: sem("t_" + n) for n in names.split()}
        block = ctx.enter_context(nc.Block())
        row = lambda a, i: a[:, bass.ds(i, 1), :].rearrange("p o d -> p (o d)")
        slot = lambda c, G, ahead: states[:, c, bass.ds(G + G // GPB + ahead, 1)]

        @block.sync
        def _(sp):
            for i, w in enumerate((d["w3k"], d["w3v"], d["w3r"], d["w3o"])):
                sp.dma_start(raw[:, i], w.rearrange("(c p) n -> p c n", p=P)).then_inc(w_in[i], 16)

        @block.gpsimd
        def _(pool):
            begin(pool, mix.om_done, mix.scaled_done, mix.zeroed, s["ones_done"], s["init3"], s["bias_added"], s["ove_done"],
                  s["orstd_done"], norm.ve_done, norm.rstd_done)
            nc.gpsimd.memset(ones[:], 1.0).then_inc(s["ones_done"], 1)
            nc.gpsimd.memset(states[:], 0.0).then_inc(s["init3"], 1)
            norm.gpsimd(pool, 0)
            mix.gpsimd(pool, raw, w_in)
            pool.wait_ge(s["ones_done"], START + 1)
            for c in range(KC):
                last = nc.gpsimd.tensor_scalar_mul(lnb[:, c], ones[:], col(k, "ln_b", c))
            last.then_inc(s["ones_done"], 1)

            def add_bias(G):
                pool.wait_ge(norm.z_done, START + G + 1)
                apart(k, pool)
                for j in range(GT):
                    xt = norm.tile(G * GT + j)
                    last = nc.gpsimd.tensor_tensor(xt, xt, row(bias, G // GPB), ALU.add)
                last.then_inc(s["bias_added"], 1)

            norm.gpsimd(pool, 1)
            pool.wait_ge(s["centred"], START + 1)
            add_bias(0)

            def body(G, prev, nxt, nxt2):
                if nxt:
                    add_bias(G + 1)
                if prev:
                    out_rstd(G - 1)
                if nxt2:
                    norm.gpsimd(pool, G + 2)

            def out_rstd(G):
                pool.wait_ge(s["ostats"], START + G + 1)
                apart(k, pool)
                nc.gpsimd.tensor_scalar_add(ove[:], omv[:, :, 1], EPS).then_inc(s["ove_done"], 1)
                pool.wait_ge(s["ove_done"], START + G + 1)
                pool.wait_ge(k.x3_done, START + G * 2)
                nc.gpsimd.tensor_tensor(orstd[:], ove[:], k.mhalf[:, 0:GT], ALU.pow).then_inc(s["orstd_done"], 1)

            through_groups(pool, body)
            out_rstd(GROUPS - 1)

        @block.scalar
        def _(act):
            begin(act, s["dec_done"], s["wo_hi"], mix.w_hi, mix.hi_h, s["ks_done"], s["hi_o"])
            nc.scalar.activation(dec[:], k.cols[:, :, COL["decay"]], ACT.Exp).then_inc(s["dec_done"], 1)
            mix.scalar_zero(act)
            for c in range(KC):
                mix.scalar_h(act, norm, 0, c, ring[:, c])
            for i in range(3):
                mix.scalar_weights(act, i)
            act.wait_ge(s["wog_done"], START + 3)
            nc.scalar.copy(woh[:], wog[:]).then_inc(s["wo_hi"], 1)

            def ks_of(G, c):
                act.wait_ge(s["kvr_ready"], START + G * 6 + 3 * c + 1)
                if not isinstance(G, int) or G:
                    act.wait_ge(s["kv_done"], START + (G - 1) * KC + c + 1)
                nc.scalar.copy(ks[:, c], kvr[:, 3 * c]).then_inc(s["ks_done"], 1)

            def o_hi(G, c):
                act.wait_ge(s["o_done"], START + G * KC + c + 1)
                act.wait_ge(s["out_ready"], START + G * 2)
                nc.scalar.copy(oh[:, c], o[:, c]).then_inc(s["hi_o"], 1)

            def body(G, prev, nxt, nxt2):
                if prev:
                    o_hi(G - 1, 1)
                ks_of(G, 0)
                if nxt:
                    for c in range(KC):
                        mix.scalar_h(act, norm, G + 1, c, ring[:, c])
                ks_of(G, 1)
                o_hi(G, 0)

            through_groups(act, body)
            o_hi(GROUPS - 1, 1)

        @block.vector
        def _(v):
            begin(v, s["wog_done"], s["centred"], s["wo_lo"], mix.w_lo, mix.lo_h, s["dve3"], s["kv_done"],
                  s["o_done"], s["lo_o"], s["obn_done"], s["ostats"], norm.bn_done, norm.stats, norm.z_done, k.x3_done)
            norm.vector_stats(v, 0, 0)
            norm.vector_z(v, 0, 0)
            v.wait_ge(w_in[3], 16)
            for c in range(KC):
                last = nc.vector.tensor_scalar(wo[:, c], raw[:, 3, c], col(k, "ln_g", c), None, ALU.mult)
            last.then_inc(s["wog_done"], 1)
            v.wait_ge(s["wog_done"], START + 1)
            for b in range(B):
                for c in range(KC):
                    last = nc.vector.tensor_tensor(wog[:, b, c], wo[:, c], k.gate[:, 4 + b], ALU.mult)
            last.then_inc(s["wog_done"], 1)
            norm.vector_stats(v, 1, GT)
            for c in range(KC):
                mix.vector_h(v, 0, c)
            v.wait_ge(s["sums_ready"], START + 1)
            for b in range(B):
                for c in range(KC):
                    last = nc.vector.scalar_tensor_tensor(out=wog[:, b, c], in0=kvr[:, 0, b * D:(b + 1) * D], scalar=-1.0 / D,
                                                          in1=wog[:, b, c], op0=ALU.mult, op1=ALU.add)
            last.then_inc(s["wog_done"], 1)
            for b in range(B):
                last = nc.vector.tensor_tensor(bias[:, b], kvr[:, 1, 0:D], k.gate[:, 4 + b], ALU.mult)
            last.then_inc(s["centred"], 1)
            for i in range(3):
                mix.vector_weights(v, i)
            norm.vector_z(v, 1, GT)
            v.wait_ge(s["wo_hi"], START + 1)
            nc.vector.tensor_tensor(wol[:], wog[:], woh[:], ALU.subtract).then_inc(s["wo_lo"], 1)
            v.wait_ge(s["dec_done"], START + 1)
            v.wait_ge(s["init3"], START + 1)
            PER = 2

            def scan(G, c):
                chain = Counted(v, s["dve3"], (G * KC + c) * PER)
                v.wait_ge(s["ks_done"], START + G * KC + c + 1)
                v.wait_ge(s["kvr_ready"], START + G * 6 + 3 * c + 2)
                nc.vector.tensor_tensor(kv[:], ks[:, c], kvr[:, 3 * c + V_], ALU.mult).then_inc(s["kv_done"], 1)
                v.wait_ge(s["kv_done"], START + G * KC + c + 1)
                apart(k, v)
                chain.link(nc.vector.tensor_tensor_scan(st[:], dec[:, c:c + 1].to_broadcast([P, GW]), kv[:],
                                                        slot(c, G, 0), ALU.mult, ALU.add), k)
                nc.vector.tensor_copy(slot(c, G, 1), st[:, GW - 1:GW])
                chain.link(nc.vector.scalar_tensor_tensor(out=fo[:], in0=kv[:], scalar=col(k, "first", c), in1=st[:],
                                                          op0=ALU.mult, op1=ALU.add))
                v.wait_ge(s["kvr_ready"], START + G * 6 + 3 * c + 3)
                v.wait_ge(s["ot_ready"], START + G * 2)
                nc.vector.tensor_tensor(o[:, c], fo[:], kvr[:, 3 * c + R_], ALU.mult).then_inc(s["o_done"], 1)

            def o_lo(G, c):
                v.wait_ge(s["hi_o"], START + G * KC + c + 1)
                nc.vector.tensor_tensor(ol[:, c], o[:, c], oh[:, c], ALU.subtract).then_inc(s["lo_o"], 1)

            def out_stats(G):
                for i in range(2):
                    v.wait_ge(s["ot_ready"], START + G * 2 + i + 1)
                    apart(k, v)
                    for j in range(2):
                        last = nc.vector.bn_stats(obn[:, 2 * i + j], ring[:, 1 - i, j * D:(j + 1) * D])
                    last.then_inc(s["obn_done"], 1)
                v.wait_ge(s["obn_done"], START + G * 2 + 2)
                apart(k, v)
                for j in range(GT):
                    last = nc.vector.bn_aggr(omv[:, j], obn[:, j])
                last.then_inc(s["ostats"], 1)

            def final(G):
                v.wait_ge(s["orstd_done"], START + G + 1)
                v.wait_ge(s["bias_added"], START + G + 1)
                for i in range(2):
                    v.wait_ge(s["out_ready"], START + G * 2 + i + 1)
                    for j in (2 * i, 2 * i + 1):
                        xt = norm.tile(G * GT + j)
                        last = nc.vector.scalar_tensor_tensor(out=xt, in0=ring[:, i, (j % 2) * D:(j % 2 + 1) * D],
                                                              scalar=orstd[:, j:j + 1], in1=xt, op0=ALU.mult, op1=ALU.add)
                    last.then_inc(k.x3_done, 1)

            def body(G, prev, nxt, nxt2):
                if prev:
                    scan(G - 1, 1)
                    o_lo(G - 1, 0)
                    o_lo(G - 1, 1)
                if nxt:
                    mix.vector_h(v, G + 1, 0)
                if prev:
                    out_stats(G - 1)
                scan(G, 0)
                if nxt:
                    mix.vector_h(v, G + 1, 1)
                if nxt2:
                    norm.vector_stats(v, G + 2, (G + 2) * GT)
                if prev:
                    final(G - 1)
                if nxt2:
                    norm.vector_z(v, G + 2, (G + 2) * GT)

            through_groups(v, body)
            scan(GROUPS - 1, 1)
            o_lo(GROUPS - 1, 0)
            o_lo(GROUPS - 1, 1)
            out_stats(GROUPS - 1)
            final(GROUPS - 1)

        @block.tensor
        def _(pe):
            begin(pe, s["sums_ready"], s["kvr_ready"], s["ot_ready"], s["out_ready"], norm.zt_done)
            pe.wait_ge(s["ones_done"], START + 1)
            for c in range(KC):
                norm.tensor(pe, 0, c, ring[:, c])
            pe.wait_ge(s["wog_done"], START + 2)
            for b in range(B):
                for c in range(KC):
                    nc.tensor.matmul(kvr[:, 0, b * D:(b + 1) * D], ones[:], wog[:, b, c], start=(c == 0), stop=(c == KC - 1))
            pe.wait_ge(s["ones_done"], START + 2)
            for c in range(KC):
                last = nc.tensor.matmul(kvr[:, 1, 0:D], lnb[:, c], raw[:, 3, c], start=(c == 0), stop=(c == KC - 1))
            last.then_inc(s["sums_ready"], 1)
            pe.wait_ge(mix.zeroed, START + 2)
            pe.wait_ge(s["centred"], START + 1)

            def piece(G, c, i, prev):
                if i == 0:
                    if c == 0:
                        pe.wait_ge(mix.lo_h, START + (G + 1) * KC)
                    if prev:
                        pe.wait_ge(s["o_done"], START + (G - 1) * KC + c + 1)
                if not prev and c == 0:
                    pe.wait_ge(mix.w_lo, START + i + 1)
                last = mix.tensor(kvr[:, 3 * c + i], i, slice(c * P, (c + 1) * P), G)
                last.then_inc(s["kvr_ready"], 1)

            def turn_z(G, c):
                if isinstance(G, int) and G < 2:
                    pe.wait_ge(mix.hi_h, START + G * KC)
                elif c == 0:
                    pe.wait_ge(mix.hi_h, START + G * KC)
                    pe.wait_ge(k.x3_done, START + (G - 2) * 2)
                else:
                    pe.wait_ge(s["obn_done"], START + (G - 2) * 2 + 1)
                norm.tensor(pe, G, c, ring[:, c])

            def turn_o(G, i, nxt):
                if i == 0:
                    pe.wait_ge(s["o_done"], START + (G + 1) * KC)
                    pe.wait_ge(k.x3_done, START + G * 2)
                elif nxt:
                    pe.wait_ge(mix.hi_h, START + (G + 2) * KC + 1)
                for j in (2 * i, 2 * i + 1):
                    for c in range(KC):
                        a = (j % 2) * D + c * P
                        last = nc.tensor.transpose(ring[:, 1 - i, a:a + P], o[:, c, j * P:(j + 1) * P], k.ident[:])
                last.then_inc(s["ot_ready"], 1)

            def output(G, i, nxt):
                if i == 0:
                    pe.wait_ge(s["obn_done"], START + G * 2 + 2)
                    pe.wait_ge(s["lo_o"], START + (G + 1) * KC)
                    pe.wait_ge(s["wo_lo"], START + 1)
                elif nxt:
                    pe.wait_ge(mix.hi_h, START + (G + 3) * KC)
                for j in (2 * i, 2 * i + 1):
                    q = slice(j * P, (j + 1) * P)
                    for c in range(KC):
                        last = three_b(nc.tensor, ring[:, i, (j % 2) * D:(j % 2 + 1) * D], oh[:, c, q], ol[:, c, q],
                                       woh, wol, G // GPB, c)
                last.then_inc(s["out_ready"], 1)

            def body(G, prev, nxt, nxt2):
                piece(G, 0, K_, prev)
                if nxt:
                    turn_z(G + 1, 0)
                piece(G, 0, V_, prev)
                if prev:
                    turn_o(G - 1, 0, nxt)
                    turn_o(G - 1, 1, nxt)
                piece(G, 0, R_, prev)
                if nxt:
                    turn_z(G + 1, 1)
                piece(G, 1, K_, prev)
                if prev:
                    output(G - 1, 0, nxt)
                piece(G, 1, V_, prev)
                if prev:
                    output(G - 1, 1, nxt)
                piece(G, 1, R_, prev)

            through_groups(pe, body)
            for i in range(2):
                turn_o(GROUPS - 1, i, False)
            for i in range(2):
                output(GROUPS - 1, i, False)


def three_b(eng, out, lh, ll, rh, rl, b, c):
    pick = lambda r: r[:, bass.ds(b, 1), c, :].rearrange("p o d -> p (o d)")
    return three(eng, out, lh, ll, pick(rh), pick(rl), c == 0, c == KC - 1)


def channel_mixing(nc, k, d):
    with ExitStack() as ctx:
        sb = lambda n, s, t=F32: ctx.enter_context(nc.sbuf_tensor(n, s, t))
        sem = lambda n: ctx.enter_context(nc.semaphore(n))
        ps = lambda n, s: ctx.enter_context(nc.psum_tensor(n, s, F32))
        K_, R_ = range(2)
        raw = sb("raw4", [P, 3, KC, D])
        mix = Shifted(nc, k, ctx, "4", ("mu_k", "mu_r"))
        wvh, wvl = sb("wvh4", [P, KC, D], F32R), sb("wvl4", [P, KC, D], F32R)
        kr = sb("kr4", [P, KC, GW])
        ka = sb("ka4", [P, KC, GW])
        kah, kal = sb("kah4", [P, KC, GW], F32R), sb("kal4", [P, KC, GW], F32R)
        sr = sb("sr4", [P, KC, GW])
        rv = sb("rv4", [P, KC, GW])
        norm = Norm(nc, k, ctx, "n4", 1, 2)
        kp, rp, vp, ring = (ps(n, [P, KC, 512]) for n in ("kp4", "rp4", "vp4", "ring4"))
        w_in = [sem(f"c_w_in{i}") for i in range(3)]
        names = ("wv_hi wv_lo k_ready r_ready kr_done ka_done hi_k lo_k sr_done v_ready rv_done yt_ready x4_done")
        s = {n: sem("c_" + n) for n in names.split()}
        block = ctx.enter_context(nc.Block())

        @block.sync
        def _(sp):
            for i, w in enumerate((d["w4k"], d["w4r"], d["w4v"])):
                sp.dma_start(raw[:, i], w.rearrange("(c p) n -> p c n", p=P)).then_inc(w_in[i], 16)
            with sp.Fori(0, GROUPS) as G:
                sp.wait_ge(s["x4_done"], START + (G + 1) * 2)
                sp.dma_start(d["out"][bass.ds(G, 1)].rearrange("o (t p) d -> p (o t) d", p=P),
                             k.x[:, bass.ds(G * GT, GT), :]).then_inc(k.stored, 16)
            sp.wait_ge(k.stored, GROUPS * 16)

        @block.gpsimd
        def _(pool):
            begin(pool, mix.om_done, mix.scaled_done, mix.zeroed, s["ka_done"], norm.ve_done, norm.rstd_done)
            norm.gpsimd(pool, 0)
            mix.gpsimd(pool, raw, w_in)
            norm.gpsimd(pool, 1)

            def body(G, prev, nxt, nxt2):
                for c in range(KC):
                    pool.wait_ge(s["kr_done"], START + G * KC + c + 1)
                    pool.wait_ge(s["lo_k"], START + G * KC)
                    nc.gpsimd.tensor_tensor(ka[:, c], kr[:, c], kr[:, c], ALU.mult).then_inc(s["ka_done"], 1)
                if nxt2:
                    norm.gpsimd(pool, G + 2)

            through_groups(pool, body)

        @block.scalar
        def _(act):
            begin(act, s["wv_hi"], mix.w_hi, mix.hi_h, s["kr_done"], s["hi_k"], s["sr_done"])
            mix.scalar_zero(act)
            for c in range(KC):
                mix.scalar_h(act, norm, 0, c, ring[:, c])
            for i in range(2):
                mix.scalar_weights(act, i)
            act.wait_ge(w_in[2], 16)
            nc.scalar.copy(wvh[:], raw[:, 2]).then_inc(s["wv_hi"], 1)

            def relu(G, c):
                act.wait_ge(s["k_ready"], START + G * KC + c + 1)
                act.wait_ge(s["ka_done"], START + G * KC)
                nc.scalar.activation(kr[:, c], kp[:, c], ACT.Relu).then_inc(s["kr_done"], 1)

            def body(G, prev, nxt, nxt2):
                relu(G, 0)
                if nxt:
                    mix.scalar_h(act, norm, G + 1, 0, ring[:, 0])
                relu(G, 1)
                if nxt:
                    mix.scalar_h(act, norm, G + 1, 1, ring[:, 1])
                for c in range(KC):
                    act.wait_ge(s["ka_done"], START + G * KC + c + 1)
                    act.wait_ge(s["v_ready"], START + G * KC)
                    nc.scalar.copy(kah[:, c], ka[:, c]).then_inc(s["hi_k"], 1)
                for c in range(KC):
                    act.wait_ge(s["r_ready"], START + G * KC + c + 1)
                    act.wait_ge(s["rv_done"], START + G * KC)
                    nc.scalar.activation(sr[:, c], rp[:, c], ACT.Sigmoid).then_inc(s["sr_done"], 1)

            through_groups(act, body)

        @block.vector
        def _(v):
            begin(v, s["wv_lo"], mix.w_lo, mix.lo_h, s["lo_k"], s["rv_done"], s["x4_done"], norm.bn_done, norm.stats, norm.z_done)
            norm.vector_stats(v, 0, 0)
            norm.vector_z(v, 0, 0)
            norm.vector_stats(v, 1, GT)
            for c in range(KC):
                mix.vector_h(v, 0, c)
            for i in range(2):
                mix.vector_weights(v, i)
            norm.vector_z(v, 1, GT)
            v.wait_ge(s["wv_hi"], START + 1)
            nc.vector.tensor_tensor(wvl[:], raw[:, 2], wvh[:], ALU.subtract).then_inc(s["wv_lo"], 1)

            def product(G):
                b = G // GPB
                for c in range(KC):
                    v.wait_ge(s["sr_done"], START + G * KC + c + 1)
                    v.wait_ge(s["v_ready"], START + G * KC + c + 1)
                    v.wait_ge(s["yt_ready"], START + G * 2)
                    gate = k.gatecol[:, 1, 1, c, b:b + 1] if isinstance(G, int) else k.gatecol[:, 1, 1, c, bass.ds(b, 1)]
                    nc.vector.scalar_tensor_tensor(out=rv[:, c], in0=sr[:, c], scalar=gate, in1=vp[:, c],
                                                   op0=ALU.mult, op1=ALU.mult).then_inc(s["rv_done"], 1)

            def final(G, i):
                v.wait_ge(s["yt_ready"], START + G * 2 + i + 1)
                apart(k, v)
                xt = k.x[:, bass.ds(G * GT + 2 * i, 2), :].rearrange("p t d -> p (t d)")
                nc.vector.tensor_tensor(xt, xt, ring[:, i], ALU.add).then_inc(s["x4_done"], 1)

            def body(G, prev, nxt, nxt2):
                if prev:
                    product(G - 1)
                if nxt:
                    for c in range(KC):
                        mix.vector_h(v, G + 1, c)
                if nxt2:
                    norm.vector_stats(v, G + 2, (G + 2) * GT)
                for c in range(KC):
                    v.wait_ge(s["hi_k"], START + G * KC + c + 1)
                    nc.vector.tensor_tensor(kal[:, c], ka[:, c], kah[:, c], ALU.subtract).then_inc(s["lo_k"], 1)
                if nxt2:
                    norm.vector_z(v, G + 2, (G + 2) * GT)
                if prev:
                    final(G - 1, 0)
                    final(G - 1, 1)

            through_groups(v, body)
            product(GROUPS - 1)
            final(GROUPS - 1, 0)
            final(GROUPS - 1, 1)

        @block.tensor
        def _(pe):
            begin(pe, s["k_ready"], s["r_ready"], s["v_ready"], s["yt_ready"], norm.zt_done)

            def turn_z(G, c):
                pe.wait_ge(mix.hi_h, START + G * KC)
                if not isinstance(G, int) or G >= 2:
                    pe.wait_ge(s["x4_done"], START + (G - 2) * 2)
                norm.tensor(pe, G, c, ring[:, c])

            def k_of(G, c, prev):
                if c == 0:
                    pe.wait_ge(mix.lo_h, START + (G + 1) * KC)
                if not prev:
                    pe.wait_ge(mix.w_lo, START + 1)
                pe.wait_ge(s["kr_done"], START + G * KC)
                mix.tensor(kp[:, c], K_, slice(c * P, (c + 1) * P), G).then_inc(s["k_ready"], 1)

            def r_of(G, c, prev):
                if not prev:
                    pe.wait_ge(mix.w_lo, START + 2)
                pe.wait_ge(s["sr_done"], START + G * KC)
                mix.tensor(rp[:, c], R_, slice(c * P, (c + 1) * P), G).then_inc(s["r_ready"], 1)

            def v_of(G, c):
                if c == 0:
                    pe.wait_ge(s["wv_lo"], START + 1)
                    pe.wait_ge(s["lo_k"], START + (G + 1) * KC)
                    pe.wait_ge(s["rv_done"], START + G * KC)
                m = slice(c * P, (c + 1) * P)
                for kc in range(KC):
                    last = three(nc.tensor, vp[:, c], wvh[:, kc, m], wvl[:, kc, m], kah[:, kc], kal[:, kc], kc == 0, kc == KC - 1)
                last.then_inc(s["v_ready"], 1)

            def turn_back(G, i, nxt):
                if i == 0:
                    pe.wait_ge(s["rv_done"], START + (G + 1) * KC)
                    pe.wait_ge(s["x4_done"], START + G * 2)
                if nxt:
                    pe.wait_ge(mix.hi_h, START + (G + 2) * KC + i + 1)
                for j in range(2):
                    for c in range(KC):
                        a = j * D + c * P
                        q = slice((2 * i + j) * P, (2 * i + j + 1) * P)
                        last = nc.tensor.transpose(ring[:, i, a:a + P], rv[:, c, q], k.ident[:])
                last.then_inc(s["yt_ready"], 1)

            for c in range(KC):
                if c == 0:
                    pe.wait_ge(norm.z_done, START + 1)
                norm.tensor(pe, 0, c, ring[:, c])

            def body(G, prev, nxt, nxt2):
                k_of(G, 0, prev)
                if nxt:
                    turn_z(G + 1, 0)
                k_of(G, 1, prev)
                if nxt:
                    turn_z(G + 1, 1)
                r_of(G, 0, prev)
                if prev:
                    turn_back(G - 1, 0, nxt)
                r_of(G, 1, prev)
                if prev:
                    turn_back(G - 1, 1, nxt)
                v_of(G, 0)
                v_of(G, 1)

            through_groups(pe, body)
            turn_back(GROUPS - 1, 0, False)
            turn_back(GROUPS - 1, 1, False)


def program(nc, d, stages=4):
    with ExitStack() as ctx:
        sb = lambda n, s, t=F32: ctx.enter_context(nc.sbuf_tensor(n, s, t))
        k = Kept()
        k.stage_sems = []
        k.sem = lambda n: ctx.enter_context(nc.semaphore(n))
        k.x = sb("x", [P, TILES, D])
        k.cols = sb("cols", [P, KC, len(COLS)])
        k.rows = sb("rows", [P, 2 * D + E])
        k.colmod = sb("colmod", [P, 2, 4, KC, B])
        k.gatecol = sb("gatecol", [P, 2, 2, KC, B])
        k.gate = sb("gate", [P, 3 * B, D])
        k.bo_gate = sb("bo_gate", [P, B, D])
        k.ident = sb("ident", [P, P])
        k.causal = sb("causal", [P, P])
        k.mhalf = sb("mhalf", [P, TPB])
        k.consts, k.x1_done, k.x2_done, k.x3_done, k.stored = (k.sem(n) for n in ("consts", "x1_done", "x2_done", "x3_done", "stored"))
        k.passed = {nc.gpsimd.engine: k.sem("passed_gpsimd"), nc.vector.engine: k.sem("passed_vector"),
                    nc.scalar.engine: k.sem("passed_scalar")}
        with ExitStack() as first:
            sb1 = lambda n, s: first.enter_context(nc.sbuf_tensor(n, s, F32))
            k.prob = sb1("prob", [P, 2, T])
            k.raw = k.prob[:, 0].rearrange("p (w n) -> p w n", w=4)
            k.bn, k.mv = sb1("bn1", [P, TPB, 6]), sb1("mv1", [P, TILES, 2])
            setup(nc, k, d)
            attention(nc, k, d)
        nc.clear_and_free_semaphores(k.stage_sems)
        nc.all_engine_barrier()
        if stages >= 2:
            k.stage_sems = []
            experts(nc, k, d)
            nc.clear_and_free_semaphores(k.stage_sems)
            nc.all_engine_barrier()
        if stages >= 3:
            time_mixing(nc, k, d)
        if stages >= 4:
            channel_mixing(nc, k, d)
        else:
            block = ctx.enter_context(nc.Block())

            @block.sync
            def _(sp):
                for G in range(GROUPS):
                    sp.wait_ge(k.x_in[G // GPB], 16 * GPB)
                    sp.dma_start(d["out"][G].rearrange("(t p) d -> p t d", p=P), k.x[:, G * GT:(G + 1) * GT, :]).then_inc(k.stored, 16)
                sp.wait_ge(k.stored, GROUPS * 16)


def layout(inputs):
    a = {n: np.asarray(v) for n, v in inputs.items()}
    vec = {"bq": "L0_attn_bq", "bk": "L0_attn_bk", "mix_k": "L1_attn_time_mix_k", "mix_v": "L1_attn_time_mix_v",
           "mix_r": "L1_attn_time_mix_r", "decay": "L1_attn_time_decay", "first": "L1_attn_time_first",
           "ln_g": "L1_attn_ln_g", "ln_b": "L1_attn_ln_b", "mu_r": "L1_ffn_mu_r", "mu_k": "L1_ffn_mu_k"}
    rows = [a[vec[n]].reshape(D) for n in COLS[:C0]] + [a[f"L{l}_c"][b] for l in range(2) for b in range(B)]
    out = {
        "x": a["L0_attn_y_all"].reshape(B * T, D),
        "cols": np.ascontiguousarray(np.stack(rows).reshape(len(COLS), KC, P).transpose(2, 1, 0)),
        "rows": np.concatenate([a["L0_attn_bv"], a["L0_attn_bo"], a["L0_ffn_expert_bias"]]).reshape(1, 2 * D + E),
        "wmod": np.stack([a["L0_wmod"], a["L1_wmod"]]),
        "wq": a["L0_attn_Wq"], "wk": a["L0_attn_Wk"], "wv": a["L0_attn_Wv"], "wo": a["L0_attn_Wo"],
        "router": a["L0_ffn_W_gate_router"], "wg": a["L0_ffn_Wg"], "wu": a["L0_ffn_Wu"], "wd": a["L0_ffn_Wd"],
        "wg_s": a["L0_ffn_Wg_s"], "wu_s": a["L0_ffn_Wu_s"], "wd_s": a["L0_ffn_Wd_s"],
    }
    for n, w in (("w3k", "L1_attn_Wk"), ("w3v", "L1_attn_Wv"), ("w3r", "L1_attn_Wr"), ("w3o", "L1_attn_Wo"),
                 ("w4k", "L1_ffn_W_k"), ("w4r", "L1_ffn_W_r"), ("w4v", "L1_ffn_W_v")):
        out[n] = a[w].T
    return {n: np.ascontiguousarray(v) for n, v in out.items()}


def kernel(**inputs):
    import concourse.bacc as bacc
    from concourse.bass_utils import run_bass_kernel_spmd

    arrays = layout(inputs)
    nc = bacc.Bacc("TRN2", target_bir_lowering=False, num_devices=1)
    d = {n: nc.dram_tensor("in_" + n, v.shape, mybir.dt.from_np(v.dtype), kind="ExternalInput").ap()
                     for n, v in arrays.items()}
    d["out"] = nc.dram_tensor("out", (GROUPS, GW, D), F32, kind="ExternalOutput").ap()
    program(nc, d)
    result = run_bass_kernel_spmd(nc, [{"in_" + n: v for n, v in arrays.items()}], core_ids=[0])
    return result.results[0]["out"].reshape(B, T, D)
```
